# Optimizing a Trainium2 kernel written in Bass

```python
import numpy as np
import jax
import jax.numpy as jnp

def _softmax(x, axis=-1):
    return jax.nn.softmax(x, axis=axis)

def _gelu(x):
    return jax.nn.gelu(x, approximate=True)

def _silu(x):
    return jax.nn.silu(x)

def _sigmoid(x):
    return jax.nn.sigmoid(x)

def _layernorm(x, axis=-1, eps=1e-05):
    m = jnp.mean(x, axis=axis, keepdims=True)
    v = jnp.var(x, axis=axis, keepdims=True)
    return (x - m) / jnp.sqrt(v + eps)

def _scatter_add(tgt, idx, src, axis=0):
    return tgt.at[idx].add(src)

def _segment_sum(src, seg, n):
    return jax.ops.segment_sum(src, seg, n)
kernel_name = 'mk_gnn_resnorm_d2_gnn_r8_48b6d3'

def setup_inputs(seed: int=0):
    np.random.seed(seed)
    _w = jnp.asarray

    def _rec_inputs():
        import jax
        import jax.numpy as jnp
        _gk = jax.random.key(seed)
        x = -0.000202 + 1 * jax.random.normal(jax.random.fold_in(_gk, 1), (6250, 128), jnp.float32)
        src = jax.random.randint(jax.random.fold_in(_gk, 2), (200000,), 0, 6250, jnp.int32)
        dst = jax.random.randint(jax.random.fold_in(_gk, 3), (200000,), 0, 6250, jnp.int32)
        _o = jnp.argsort(dst, stable=True)
        src = src[_o]
        dst = dst[_o]
        edge_attr3_1x20 = jax.random.uniform(jax.random.fold_in(_gk, 11), (200000, 1, 20), jnp.float32, 0.0, 1)
        edge_weight1 = jax.random.uniform(jax.random.fold_in(_gk, 13), (200000, 1), jnp.float32, 0.0, 0.999999)
        return (x, src, dst, edge_attr3_1x20, edge_weight1)
    x, src, dst, edge_attr3_1x20, edge_weight1 = _rec_inputs()

    def _L0_gnn_setup():
        import jax, jax.numpy as jnp
        import numpy as np
        N = 6250
        E = 200000
        IN_DIM = 128
        HEADS = 4
        OUT_DIM = 32
        NEG_SLOPE = 0.2
        key = jax.random.key(seed)
        k1, k2, k3, k4, k5, k6 = jax.random.split(key, 6)
        x = jax.random.normal(k1, (N, IN_DIM), dtype=jnp.float32)
        src = jax.random.randint(k2, (E,), 0, N)
        dst = jax.random.randint(k3, (E,), 0, N)
        edge_index = jnp.stack([src, dst], axis=0).astype(jnp.int64)
        W = jax.random.normal(k4, (IN_DIM, HEADS * OUT_DIM), dtype=jnp.float32) * 0.08
        att = jax.random.normal(k5, (HEADS, 2 * OUT_DIM), dtype=jnp.float32) * 0.1
        bias = jnp.zeros((HEADS * OUT_DIM,), dtype=jnp.float32)
        return {'x': x, 'edge_index': edge_index, 'W': W, 'att': att, 'bias': bias}
    _L0_gnn_all = _L0_gnn_setup()
    _L0_gnn_in = {k: v for k, v in _L0_gnn_all.items() if k in ('W', 'att', 'bias')}
    del _L0_gnn_all

    def _L1_gnn_setup():
        import jax, jax.numpy as jnp
        import numpy as np
        N_ATOMS = 6250
        N_PAIRS = 75000
        D_FEAT = 128
        D_FILT = 128
        N_RBF = 20

        def ssp(x):
            return jax.nn.softplus(x) - jnp.log(2.0).astype(x.dtype)
        key = jax.random.key(seed)
        ks = jax.random.split(key, 12)
        inp = {'x': jax.random.normal(ks[0], (N_ATOMS, D_FEAT), dtype=jnp.float32), 'pairlist': jax.random.randint(ks[1], (2, N_PAIRS), 0, N_ATOMS, dtype=jnp.int64), 'f_ij': jax.random.uniform(ks[2], (N_PAIRS, 1, N_RBF), dtype=jnp.float32), 'f_ij_cutoff': jax.random.uniform(ks[3], (N_PAIRS, 1), dtype=jnp.float32), 'W_in': jax.random.normal(ks[4], (D_FEAT, D_FILT), dtype=jnp.float32) * 0.05, 'W_f1': jax.random.normal(ks[5], (N_RBF, D_FILT), dtype=jnp.float32) * 0.05, 'b_f1': jnp.zeros((D_FILT,), dtype=jnp.float32), 'W_f2': jax.random.normal(ks[6], (D_FILT, D_FILT), dtype=jnp.float32) * 0.05, 'b_f2': jnp.zeros((D_FILT,), dtype=jnp.float32), 'W_o1': jax.random.normal(ks[7], (D_FILT, D_FEAT), dtype=jnp.float32) * 0.05, 'b_o1': jnp.zeros((D_FEAT,), dtype=jnp.float32), 'W_o2': jax.random.normal(ks[8], (D_FEAT, D_FEAT), dtype=jnp.float32) * 0.05, 'b_o2': jnp.zeros((D_FEAT,), dtype=jnp.float32)}
        return inp
    _L1_gnn_all = _L1_gnn_setup()
    _L1_gnn_in = {k: v for k, v in _L1_gnn_all.items() if k in ('W_in', 'W_f1', 'b_f1', 'W_f2', 'b_f2', 'W_o1', 'b_o1', 'W_o2', 'b_o2')}
    del _L1_gnn_all
    return {'x': x, 'src': src, 'dst': dst, 'edge_attr3_1x20': edge_attr3_1x20, 'edge_weight1': edge_weight1, 'L0_gnn_W': _L0_gnn_in['W'], 'L0_gnn_att': _L0_gnn_in['att'], 'L0_gnn_bias': _L0_gnn_in['bias'], 'L1_gnn_W_in': _L1_gnn_in['W_in'], 'L1_gnn_W_f1': _L1_gnn_in['W_f1'], 'L1_gnn_b_f1': _L1_gnn_in['b_f1'], 'L1_gnn_W_f2': _L1_gnn_in['W_f2'], 'L1_gnn_b_f2': _L1_gnn_in['b_f2'], 'L1_gnn_W_o1': _L1_gnn_in['W_o1'], 'L1_gnn_b_o1': _L1_gnn_in['b_o1'], 'L1_gnn_W_o2': _L1_gnn_in['W_o2'], 'L1_gnn_b_o2': _L1_gnn_in['b_o2']}

def reference(x, src, dst, edge_attr3_1x20, edge_weight1, L0_gnn_W, L0_gnn_att, L0_gnn_bias, L1_gnn_W_in, L1_gnn_W_f1, L1_gnn_b_f1, L1_gnn_W_f2, L1_gnn_b_f2, L1_gnn_W_o1, L1_gnn_b_o1, L1_gnn_W_o2, L1_gnn_b_o2):
    import jax
    import jax.numpy as jnp

    def _L0_gnn_ref(x, edge_index, W, att, bias):
        import jax, jax.numpy as jnp
        import numpy as np
        N = 6250
        E = 200000
        IN_DIM = 128
        HEADS = 4
        OUT_DIM = 32
        NEG_SLOPE = 0.2
        src, dst = (edge_index[0], edge_index[1])
        n = x.shape[0]
        Wh = (x @ W).reshape(n, HEADS, OUT_DIM)
        a_src = jnp.einsum('nhf,hf->nh', Wh, att[:, :OUT_DIM])
        a_dst = jnp.einsum('nhf,hf->nh', Wh, att[:, OUT_DIM:])
        logits = jax.nn.leaky_relu(a_src[src] + a_dst[dst], negative_slope=NEG_SLOPE)
        seg_max = jax.ops.segment_max(logits, dst, num_segments=n)
        exp_s = jnp.exp(logits - seg_max[dst])
        denom = jnp.clip(jax.ops.segment_sum(exp_s, dst, num_segments=n), 1e-09, None)
        alpha = exp_s / denom[dst]
        messages = alpha[:, :, None] * Wh[src]
        out = jax.ops.segment_sum(messages.reshape(-1, HEADS * OUT_DIM), dst, num_segments=n)
        return out + bias

    def _L1_gnn_ref(x, pairlist, f_ij, f_ij_cutoff, W_in, W_f1, b_f1, W_f2, b_f2, W_o1, b_o1, W_o2, b_o2):
        import jax, jax.numpy as jnp
        import numpy as np
        N_ATOMS = 6250
        N_PAIRS = 75000
        D_FEAT = 128
        D_FILT = 128
        N_RBF = 20

        def ssp(x):
            return jax.nn.softplus(x) - jnp.log(2.0).astype(x.dtype)
        n_atoms = x.shape[0]
        h = x @ W_in
        Wij = ssp(f_ij[:, 0, :] @ W_f1 + b_f1) @ W_f2 + b_f2
        idx_i = pairlist[0]
        idx_j = pairlist[1]
        x_ij = h[idx_j] * Wij * f_ij_cutoff
        agg = jax.ops.segment_sum(x_ij, idx_i, num_segments=n_atoms)
        out = ssp(agg @ W_o1 + b_o1) @ W_o2 + b_o2
        return out
    edge_index = jnp.stack([src, dst])
    x = _layernorm(x + _L0_gnn_ref(x, edge_index, L0_gnn_W, L0_gnn_att, L0_gnn_bias), axis=-1)
    x = _layernorm(x + _L1_gnn_ref(x, edge_index, edge_attr3_1x20, edge_weight1, L1_gnn_W_in, L1_gnn_W_f1, L1_gnn_b_f1, L1_gnn_W_f2, L1_gnn_b_f2, L1_gnn_W_o1, L1_gnn_b_o1, L1_gnn_W_o2, L1_gnn_b_o2), axis=-1)
    return x

_drawn_inputs = setup_inputs


def setup_inputs(seed=0):
    import zlib

    import numpy as np

    out = dict(_drawn_inputs(seed))
    spreads = {'L0_gnn_bias': (0.0, 0.1),
     'L1_gnn_b_f1': (0.0, 0.8),
     'L1_gnn_b_f2': (0.0, 0.507),
     'L1_gnn_b_o1': (0.0, 1.804),
     'L1_gnn_b_o2': (0.0, 0.785)}
    factors = {'edge_attr3_1x20': 8.0, 'edge_weight1': 3.291, 'L1_gnn_W_f1': 4.502, 'L1_gnn_W_f2': 3.693}
    for name, (base, spread) in spreads.items():
        noise = np.random.default_rng([zlib.crc32(name.encode()), seed]).standard_normal(out[name].shape)
        drawn = base * np.exp(spread * noise) if base else spread * noise
        out[name] = jnp.asarray(drawn.astype(out[name].dtype))
    for name, factor in factors.items():
        out[name] = (out[name] * factor).astype(out[name].dtype)
    return out
```

```python
import concourse.bass as bass
from concourse import mybir
from contextlib import ExitStack

P = 128
D = 128
HEADS = 4
F = D // HEADS
RBF = 20
N = 6250
E = 200000
T = 8
GE = P * T
NG = -(-E // (2 * GE)) * 2
EP = NG * GE
NB = 50
NT = NB * P
WN = 48
Q = 4
COPIES = T
ROW = D + HEADS
SLOPE = 0.2
EPS = 1e-5
LN2 = 0.6931471805599453
SPREAD_MAX = 60.0
SKIP = 1 << 17
V_CAP = 40.0

ALU = mybir.AluOpType
ACT = mybir.ActivationFunctionType
AX = mybir.AxisListType
F32 = mybir.dt.float32
I32 = mybir.dt.int32
U32 = mybir.dt.uint32
BF16 = mybir.dt.bfloat16
RMAX = bass.bass_isa.ReduceOp.max


def wait_for(eng, sem, count):
    if isinstance(count, int) and count <= 0:
        return
    eng.wait_ge(sem, count)


def wait_apart(eng, sem, count, passed):
    if isinstance(count, int) and count <= 0:
        return
    eng.wait_ge(sem, count)
    eng.sem_inc(passed, 1)


def pairs(eng, total, body):
    for b in range(2):
        body(b, b, 0)
    with eng.Fori(1, total // 2) as i:
        for b in range(2):
            body(i * 2 + b, b, i)


def skewed(eng, first, second):
    first(0, 0, 0)
    first(1, 1, 0)
    second(0, 0, 0)
    first(2, 0, 1)
    second(1, 1, 0)
    with eng.Fori(1, NG // 2 - 1) as i:
        first(i * 2 + 1, 1, i)
        second(i * 2, 0, i)
        first(i * 2 + 2, 0, i + 1)
        second(i * 2 + 1, 1, i)
    first(NG - 1, 1, NG // 2 - 1)
    second(NG - 2, 0, NG // 2 - 1)
    second(NG - 1, 1, NG // 2 - 1)


def gnn_kernel(nc, x, src, dst, f_ij, cut, W, att, bias0, W_in, W_f1, b_f1, W_f2, b_f2,
               W_o1, b_o1, W_o2, b_o2, out):
    with ExitStack() as ctx:
        def sb(name, shape, dt=F32):
            return ctx.enter_context(nc.sbuf_tensor(name, shape, dt))

        def sem(name):
            return ctx.enter_context(nc.semaphore(name))

        wh_d = nc.dram_tensor("wh_d", [NT, ROW], F32)
        dk_d = nc.dram_tensor("dk_d", [NT, 2 * HEADS], F32)
        x1_d = nc.dram_tensor("x1_d", [NT, D], F32)
        h_d = nc.dram_tensor("h_d", [NT, D], F32)
        agg_d = nc.dram_tensor("agg_d", [COPIES * NT, D], F32)

        bank = [ctx.enter_context(nc.psum_tensor(f"bank{i}", [P, 512], F32)) for i in range(8)]

        ident = sb("ident", [P, P])
        ones = sb("ones", [P, P])
        ones_bf = sb("ones_bf", [P, P], BF16)
        iota_w = sb("iota_w", [P, WN])
        iota_p = sb("iota_p", [P, 1])
        copy_row = sb("copy_row", [P, T])
        rank_w = sb("rank_w", [P, 1])
        rank_cap = sb("rank_cap", [P, 1])
        zeros = sb("zeros", [P, D])
        w_sb = sb("w_sb", [P, D])
        wT = sb("wT", [P, D])
        att_blk = sb("att_blk", [P, 2 * HEADS])
        v_sb = sb("v_sb", [P, D + 2 * HEADS])
        win_sb = sb("win_sb", [P, D])
        wf1_sb = sb("wf1_sb", [Q * RBF, Q, D])
        wf2_sb = sb("wf2_sb", [P, D])
        wo1_sb = sb("wo1_sb", [P, D])
        wo2_sb = sb("wo2_sb", [P, D])
        bf1_c = sb("bf1_c", [P, 1])
        bo1_c = sb("bo1_c", [P, 1])
        rows_in = sb("rows_in", [1, 3, D])
        rows_eff = sb("rows_eff", [1, 3, D])
        split_f = sb("split_f", [1, 2, D])
        split_b = sb("split_b", [1, 3, D], BF16)
        bf2_3 = sb("bf2_3", [3, D], BF16)
        bc = sb("bc", [P, 2, D])
        dst_all = sb("dst_all", [P, NG, T], I32)
        rel_all = sb("rel_all", [P, NG, T])
        base_f = sb("base_f", [1, NG])
        base_bc = sb("base_bc", [P, NG])
        node_id = sb("node_id", [P, NG])
        sd_all = sb("sd_all", [P, NB, 2 * HEADS])
        dk_all = sb("dk_all", [P, NB, 2 * HEADS])
        zk = sb("zk", [P, NB, HEADS])
        ext = sb("ext", [P, 2 * HEADS + 2])
        ext_all = sb("ext_all", [P, 2 * HEADS + 2])
        accden = sb("accden", [P, 2, NT])
        idx = sb("idx", [P, 2, T], I32)
        drow = sb("drow", [WN, 2, GE], I32)
        dkwin = sb("dkwin", [WN, 2, 2 * HEADS])
        rows = sb("rows", [P, 2, T, ROW])
        oneT = sb("oneT", [WN, 2, T, P])
        one = sb("one", [P, 2, T, WN])
        z = sb("z", [P, 2, T, HEADS])
        lg = sb("lg", [P, 2, T, HEADS])
        ls = sb("ls", [P, 2, T, HEADS])
        wgt = sb("wgt", [P, 2, T, D])
        msg = sb("msg", [P, 2, T, D])
        xb = sb("xb", [P, 2, D])
        nT = sb("nT", [P, 2, D])
        nS = sb("nS", [P, 2, D + 2 * HEADS])
        den = sb("den", [P, 2, P])
        rec = sb("rec", [P, 2, P])
        gT = sb("gT", [P, 2, P])
        t1 = sb("t1", [P, 2, D])
        t2 = sb("t2", [P, 2, D])
        stats = sb("stats", [P, 2, 6])
        mv = sb("mv", [P, 2, 2])
        rstd = sb("rstd", [P, 2, 1])
        lnvar = sb("lnvar", [P, 2, 1])
        eps_c = sb("eps_c", [P, 1])
        y1 = sb("y1", [P, 2, D])
        agg8 = msg
        ag = sb("ag", [P, 2, D])
        fin = sb("fin", [P, 2, T * RBF])
        srow = sb("srow", [P, 2, GE], I32)
        scol = sb("scol", [P, 2, T], I32)
        crow = sb("crow", [WN, 2, GE])
        hwin = sb("hwin", [WN, 2, D])
        fT = sb("fT", [Q * RBF, 2, 2, P])
        ex = sb("ex", [P, 2, 512])
        exc = sb("exc", [P, 2, 512])
        ln = sb("ln", [P, 2, 512])
        gact = wgt[:, :, :, :].rearrange("p b (q t) f -> p b q (t f)", q=2)
        oneTc = oneT
        eq = sb("eq", [P, 2, T, P])
        hsb = sb("hsb", [P, 2, 512])
        xij = sb("xij", [P, 2, 512])
        dup = sb("dup", [P, 2, T])
        sidx_f = sb("sidx_f", [P, 2, T])
        sidx = sb("sidx", [P, 2, T], I32)
        xo = msg

        pool_consts = sem("pool_consts")
        dve_consts = sem("dve_consts")
        w_cleared = sem("w_cleared")
        weights_in = sem("weights_in")
        index_in = sem("index_in")
        agg_zeroed = sem("agg_zeroed")
        su_pe = sem("su_pe")
        su_dve = sem("su_dve")
        su_act = sem("su_act")
        split_in = sem("split_in")
        ext_ready = sem("ext_ready")
        ext_reduced = sem("ext_reduced")
        dk_ready = sem("dk_ready")
        dk_out = sem("dk_out")
        acc_zeroed = sem("acc_zeroed")
        pool_passed = sem("pool_passed")
        dve_passed = sem("dve_passed")
        a_x_in = [sem(f"a_x_in{b}") for b in range(2)]
        a_turned = sem("a_turned")
        a_xT = sem("a_xT")
        a_v = sem("a_v")
        a_row = sem("a_row")
        a_out = [sem(f"a_out{b}") for b in range(2)]
        idx_in = [sem(f"idx_in{b}") for b in range(2)]
        drow_in = [sem(f"drow_in{b}") for b in range(2)]
        dkwin_in = [sem(f"dkwin_in{b}") for b in range(2)]
        rows_got = [sem(f"rows_got{b}") for b in range(2)]
        oneT_made = sem("oneT_made")
        one_made = sem("one_made")
        expanded = sem("expanded")
        z_made = sem("z_made")
        lg_made = sem("lg_made")
        ls_made = sem("ls_made")
        wgt_made = sem("wgt_made")
        msg_made = sem("msg_made")
        summed = sem("summed")
        acc_added = sem("acc_added")
        b_x_in = [sem(f"b_x_in{b}") for b in range(2)]
        b_c = sem("b_c")
        chain_b = sem("chain_b")
        b_rstd = sem("b_rstd")
        b_gT = sem("b_gT")
        b_g = sem("b_g")
        b_y = sem("b_y")
        b_turned = sem("b_turned")
        b_yT = sem("b_yT")
        b_h = sem("b_h")
        b_hs = sem("b_hs")
        b_y_out = [sem(f"b_y_out{b}") for b in range(2)]
        b_h_out = [sem(f"b_h_out{b}") for b in range(2)]
        fin_in = [sem(f"fin_in{b}") for b in range(2)]
        srow_in = [sem(f"srow_in{b}") for b in range(2)]
        scol_in = [sem(f"scol_in{b}") for b in range(2)]
        drow1_in = [sem(f"drow1_in{b}") for b in range(2)]
        crow_in = [sem(f"crow_in{b}") for b in range(2)]
        hwin_in = [sem(f"hwin_in{b}") for b in range(2)]
        f_turned = sem("f_turned")
        fT_made = sem("fT_made")
        v_made = sem("v_made")
        ex_made = sem("ex_made")
        exc_made = sem("exc_made")
        ln_made = sem("ln_made")
        gact_made = sem("gact_made")
        eq_made = sem("eq_made")
        oneTc_made = sem("oneTc_made")
        hd_made = sem("hd_made")
        hsb_made = sem("hsb_made")
        wij_made = sem("wij_made")
        xij_made = sem("xij_made")
        rank_made = sem("rank_made")
        dup_made = sem("dup_made")
        sidxf_made = sem("sidxf_made")
        sidx_made = sem("sidx_made")
        presummed = sem("presummed")
        xo_made = sem("xo_made")
        earlier_added = sem("earlier_added")
        added = [sem(f"added{t}") for t in range(COPIES)]
        c_agg_in = [sem(f"c_agg_in{b}") for b in range(2)]
        c_x_in = [sem(f"c_x_in{b}") for b in range(2)]
        c_c = sem("c_c")
        c_ag = sem("c_ag")
        c_turned = sem("c_turned")
        c_agT = sem("c_agT")
        c_o = sem("c_o")
        c_ex = sem("c_ex")
        c_exc = sem("c_exc")
        c_ln = sem("c_ln")
        c_g = sem("c_g")
        c_y = sem("c_y")
        c_fin = sem("c_fin")
        c_t2 = sem("c_t2")
        c_rstd = sem("c_rstd")
        c_out = [sem(f"c_out{b}") for b in range(2)]

        src_g = src.rearrange("(g p t) -> g p t", p=P, t=T)
        dst_g = dst.rearrange("(g e) -> g e", e=GE)
        src_e = src.rearrange("(g e) -> g e", e=GE)
        cut_e = cut.rearrange("(g e) -> g e", e=GE)
        f_g = f_ij.rearrange("(g p t) r -> g p (t r)", p=P, t=T)
        agg_c = agg_d[:, :].rearrange("(c n) f -> n c f", c=COPIES)

        block = ctx.enter_context(nc.Block())

        @block.sync
        def _(sp):
            sp.dma_start(dst_all[:, :, :], dst.rearrange("(g p t) -> p g t", p=P, t=T)).then_inc(index_in, 16)
            sp.dma_start(w_sb[:, :], W).then_inc(weights_in, 16)
            sp.dma_start(win_sb[:, :], W_in).then_inc(weights_in, 16)
            sp.dma_start(wf2_sb[:, :], W_f2).then_inc(weights_in, 16)
            sp.dma_start(wo1_sb[:, :], W_o1).then_inc(weights_in, 16)
            sp.dma_start(wo2_sb[:, :], W_o2).then_inc(weights_in, 16)
            sp.dma_start(bf1_c[:, :], b_f1.rearrange("(p a) -> p a", a=1)).then_inc(weights_in, 16)
            sp.dma_start(bo1_c[:, :], b_o1.rearrange("(p a) -> p a", a=1)).then_inc(weights_in, 16)
            sp.dma_start(rows_in[:, 0, :], b_f2.rearrange("(a p) -> a p", a=1)).then_inc(weights_in, 16)
            sp.dma_start(rows_in[:, 1, :], b_o2.rearrange("(a p) -> a p", a=1)).then_inc(weights_in, 16)
            sp.dma_start(rows_in[:, 2, :], bias0.rearrange("(a p) -> a p", a=1)).then_inc(weights_in, 16)
            sp.wait_ge(w_cleared, 2)
            for h in range(HEADS):
                for side in range(2):
                    sp.dma_start(att_blk[F * h:F * h + F, side * HEADS + h:side * HEADS + h + 1],
                                 att[h:h + 1, side * F:side * F + F].rearrange("o f -> f o"),
                                 allow_slow_non_contiguous=True).then_inc(weights_in, 16)
            for t in range(Q):
                sp.dma_start(wf1_sb[RBF * t:RBF * t + RBF, t, :], W_f1).then_inc(weights_in, 16)

            def load_x(nb, b, i):
                wait_for(sp, a_turned, nb - 1)
                sp.dma_start(xb[:, b, :], x[bass.ds(nb * P, P), :]).then_inc(a_x_in[b], 16)

            pairs(sp, NB, load_x)

            sp.wait_ge(su_dve, 8)
            sp.dma_start(bf2_3[:, :], split_b[0:1, :, :]).then_inc(split_in, 16)

            sp.wait_ge(dk_out, 16)
            sp.wait_ge(index_in, 16)

            def load_group0(g, b, i):
                wait_for(sp, lg_made, g - 1)
                sp.dma_start(idx[:, b, :], src_g[bass.ds(g, 1), :, :].rearrange("o p t -> p (o t)")
                             ).then_inc(idx_in[b], 16)
                wait_for(sp, oneT_made, g - 1)
                sp.dma_start(drow[:, b, :], dst_g[bass.ds(g, 1), :].to_broadcast([WN, GE])
                             ).then_inc(drow_in[b], 16)
                wait_for(sp, expanded, g - 1)
                base = sp.value_load(dst_all[0:1, bass.ds(g, 1), 0], min_val=0, max_val=NT - WN)
                sp.dma_start(dkwin[:, b, :], dk_d[bass.ds(base, WN), :]).then_inc(dkwin_in[b], 16)

            pairs(sp, NG, load_group0)

            def load_xb(nb, b, i):
                wait_for(sp, b_y, nb - 1)
                sp.dma_start(xb[:, b, :], x[bass.ds(nb * P, P), :]).then_inc(b_x_in[b], 16)

            sp.wait_ge(a_turned, NB)
            pairs(sp, NB, load_xb)

            sp.wait_ge(oneT_made, NG)
            for b in range(2):
                sp.wait_ge(b_h_out[b], 16 * (NB // 2))

            def load_group1(g, b, i):
                wait_for(sp, f_turned, g - 1)
                sp.dma_start(fin[:, b, :], f_g[bass.ds(g, 1), :, :].rearrange("o p c -> p (o c)")
                             ).then_inc(fin_in[b], 16)
                wait_for(sp, eq_made, g - 1)
                sp.dma_start(srow[:, b, :], src_e[bass.ds(g, 1), :].to_broadcast([P, GE])
                             ).then_inc(srow_in[b], 16)
                wait_for(sp, sidxf_made, g - 1)
                sp.dma_start(scol[:, b, :], src_g[bass.ds(g, 1), :, :].rearrange("o p t -> p (o t)")
                             ).then_inc(scol_in[b], 16)
                wait_for(sp, oneTc_made, g - 1)
                sp.dma_start(drow[:, b, :], dst_g[bass.ds(g, 1), :].to_broadcast([WN, GE])
                             ).then_inc(drow1_in[b], 16)
                sp.dma_start(crow[:, b, :], cut_e[bass.ds(g, 1), :].to_broadcast([WN, GE])
                             ).then_inc(crow_in[b], 16)
                wait_for(sp, hd_made, 2 * (g - 1))
                base = sp.value_load(dst_all[0:1, bass.ds(g, 1), 0], min_val=0, max_val=NT - WN)
                sp.dma_start(hwin[:, b, :], h_d[bass.ds(base, WN), :]).then_inc(hwin_in[b], 16)

            pairs(sp, NG, load_group1)

            for t in range(COPIES):
                sp.wait_ge(added[t], 16 * NG)

            def load_c(nb, b, i):
                wait_for(sp, c_ag, nb - 1)
                sp.dma_start(agg8[:, b, :, :], agg_c[bass.ds(nb * P, P), :, :]).then_inc(c_agg_in[b], 16)
                wait_for(sp, c_fin, nb - 1)
                sp.dma_start(xb[:, b, :], x1_d[bass.ds(nb * P, P), :]).then_inc(c_x_in[b], 16)

            sp.wait_ge(b_y, NB)
            for b in range(2):
                sp.wait_ge(b_y_out[b], 16 * (NB // 2))
            pairs(sp, NB, load_c)
            for b in range(2):
                sp.wait_ge(c_out[b], 16 * (NB // 2))

        @block.gpsimd
        def _(pool):
            pool.memset(ident[:, :], 0.0).then_inc(pool_consts, 1)
            pool.memset(wf1_sb[:, :, :], 0.0).then_inc(w_cleared, 1)
            pool.memset(att_blk[:, :], 0.0).then_inc(w_cleared, 1)
            pool.iota(iota_w[:, :], pattern=[[1, WN]], base=0, channel_multiplier=0,
                      allow_small_or_imprecise_dtypes=True).then_inc(pool_consts, 1)
            pool.iota(iota_p[:, :], pattern=[[0, 1]], base=0, channel_multiplier=1,
                      allow_small_or_imprecise_dtypes=True).then_inc(pool_consts, 1)
            pool.iota(copy_row[:, :], pattern=[[NT, T]], base=0, channel_multiplier=0,
                      allow_small_or_imprecise_dtypes=True).then_inc(pool_consts, 1)
            pool.wait_ge(pool_consts, 4)
            pool.affine_select(out=ident[:, :], in_=ident[:, :], compare_op=ALU.not_equal, fill=1.0,
                               base=0, pattern=[[-1, P]], channel_multiplier=1).then_inc(pool_consts, 1)

            def store_row(nb, b, i):
                wait_apart(pool, a_row, 2 * (nb + 1), pool_passed)
                pool.dma_start(wh_d[bass.ds(nb * P, P), :], nS[:, b, 0:ROW]).then_inc(a_out[b], 16)

            pairs(pool, NB, store_row)

            pool.wait_ge(ext_ready, 4)
            pool.partition_all_reduce(ext_all[:, :], ext[:, :], P, RMAX).then_inc(ext_reduced, 1)

            for b in range(2):
                pool.wait_ge(a_out[b], 16 * (NB // 2))

            def gather(g, b, i):
                wait_apart(pool, idx_in[b], 16 * (i + 1), pool_passed)
                wait_apart(pool, msg_made, g - 1, pool_passed)
                for t in range(T):
                    pool.indirect_dma_start(
                        out=rows[:, b, t, :], out_offset=None, in_=wh_d[:, :],
                        in_offset=bass.IndirectOffsetOnAxis(ap=idx[:, b, t:t + 1].bitcast(U32), axis=0),
                        bounds_check=NT - 1, oob_is_err=False).then_inc(rows_got[b], 16)

            pairs(pool, NG, gather)

            def store_b(nb, b, i):
                wait_apart(pool, b_y, nb + 1, pool_passed)
                pool.dma_start(x1_d[bass.ds(nb * P, P), :], y1[:, b, :]).then_inc(b_y_out[b], 16)
                wait_apart(pool, b_hs, nb + 1, pool_passed)
                pool.dma_start(h_d[bass.ds(nb * P, P), :], nS[:, b, 0:D]).then_inc(b_h_out[b], 16)

            pairs(pool, NB, store_b)

            pool.wait_ge(agg_zeroed, 16 * COPIES)

            def scatter(g, b, i):
                for t in range(T):
                    wait_for(pool, added[t], 16 * g)
                pool.sem_inc(earlier_added, 1)
                wait_apart(pool, sidx_made, g + 1, pool_passed)
                wait_apart(pool, xo_made, 2 * (g + 1), pool_passed)
                for t in range(T):
                    pool.indirect_dma_start(
                        out=agg_d[:, :],
                        out_offset=bass.IndirectOffsetOnAxis(ap=sidx[:, b, t:t + 1].bitcast(U32), axis=0),
                        in_=xo[:, b, t, :], in_offset=None, bounds_check=COPIES * NT - 1,
                        oob_is_err=False, compute_op=ALU.add).then_inc(added[t], 16)

            pairs(pool, NG, scatter)

            def store_c(nb, b, i):
                wait_apart(pool, c_fin, nb + 1, pool_passed)
                pool.dma_start(out[bass.ds(nb * P, P), :], y1[:, b, :]).then_inc(c_out[b], 16)

            pairs(pool, NB, store_c)

        @block.scalar
        def _(act):
            act.wait_ge(dve_consts, 4)
            for t in range(COPIES):
                act.dma_start(agg_d[t * NT:(t + 1) * NT, :].rearrange("(p r) f -> p r f", p=P),
                              zeros[:, :].unsqueeze(1).to_broadcast([P, NB, D])).then_inc(agg_zeroed, 16)
            act.wait_ge(su_pe, 1)
            act.copy(wT[:, :], bank[0][:, 0:D]).then_inc(su_act, 1)
            act.wait_ge(su_dve, 1)
            act.activation(rank_w[:, :], rank_cap[:, :], ACT.Exp).then_inc(su_act, 1)

            def turn_a(nb, b, i):
                act.wait_ge(a_turned, nb + 1)
                wait_for(act, a_v, nb - 1)
                act.copy(nT[:, b, :], bank[b][:, 0:D]).then_inc(a_xT, 1)

            pairs(act, NB, turn_a)
            act.wait_ge(dk_ready, 1)
            act.dma_start(dk_d[:, :].rearrange("(n p) c -> p n c", p=P), dk_all[:, :, :]).then_inc(dk_out, 16)

            def weigh(g, b, i):
                act.wait_ge(ls_made, g + 1)
                wait_for(act, summed, g - 1)
                act.activation(wgt[:, b, :, :].rearrange("p t (h f) -> p t h f", h=HEADS),
                               ls[:, b, :, :].unsqueeze(3).to_broadcast([P, T, HEADS, F]), ACT.Exp
                               ).then_inc(wgt_made, 1)

            pairs(act, NG, weigh)

            act.wait_ge(a_v, NB)

            def inverse_root(nb, b, variance_sem, count, rstd_sem):
                act.wait_ge(variance_sem, count)
                act.activation(lnvar[:, b, :], mv[:, b, 1:2], ACT.Ln, bias=eps_c[:, 0:1]).then_inc(rstd_sem, 1)
                act.wait_ge(rstd_sem, 2 * nb + 1)
                act.activation(rstd[:, b, :], lnvar[:, b, :], ACT.Exp, scale=-0.5).then_inc(rstd_sem, 1)

            def turn_b(nb, b, i):
                inverse_root(nb, b, chain_b, 5 * (nb + 1), b_rstd)
                act.wait_ge(b_turned, nb + 1)
                wait_for(act, b_h, nb - 1)
                act.copy(nT[:, b, :], bank[2 + b][:, 0:D]).then_inc(b_yT, 1)
                act.wait_ge(b_h, nb + 1)
                if not isinstance(i, int) or i > 0:
                    act.wait_ge(b_h_out[b], 16 * i)
                act.copy(nS[:, b, 0:D], bank[4 + b][:, 0:D]).then_inc(b_hs, 1)

            pairs(act, NB, turn_b)

            def filter_part(g, b, i):
                act.wait_ge(f_turned, g + 1)
                wait_for(act, v_made, 2 * (g - 1))
                act.copy(fT[:, b, :, :], bank[0][0:Q * RBF, 0:2 * P].rearrange("r (q p) -> r q p", q=2)
                         ).then_inc(fT_made, 1)
                for q in range(2):
                    act.wait_ge(exc_made, 2 * g + q + 1)
                    wait_for(act, ln_made, 2 * g + q - 1)
                    act.activation(ex[:, q, :], exc[:, q, :], ACT.Exp).then_inc(ex_made, 1)
                for q in range(2):
                    act.wait_ge(ex_made, 2 * g + q + 1)
                    wait_for(act, gact_made, 2 * g + q - 1)
                    act.activation(ln[:, q, :], ex[:, q, :], ACT.Ln, bias=1.0).then_inc(ln_made, 1)

            def message_part(g, b, i):
                for q in range(2):
                    act.wait_ge(hd_made, 2 * g + q + 1)
                    wait_for(act, xij_made, 2 * g + q - 1)
                    act.copy(hsb[:, q, :], bank[3][:, :]).then_inc(hsb_made, 1)
                for q in range(2):
                    act.wait_ge(presummed, 2 * g + q + 1)
                    if q == 0:
                        wait_for(act, earlier_added, g)
                    act.copy(xo[:, b, Q * q:Q * q + Q, :].rearrange("p t f -> p (t f)"),
                             bank[6][:, :]).then_inc(xo_made, 1)

            skewed(act, filter_part, message_part)

            def node_c(nb, b, i):
                act.wait_ge(c_turned, nb + 1)
                wait_for(act, c_o, nb - 1)
                act.copy(nT[:, b, :], bank[b][:, 0:D]).then_inc(c_agT, 1)
                act.wait_ge(c_exc, nb + 1)
                wait_for(act, c_ln, nb - 1)
                act.activation(ex[:, b, 0:P], exc[:, b, 0:P], ACT.Exp).then_inc(c_ex, 1)
                act.wait_ge(c_ex, nb + 1)
                wait_for(act, c_g, nb - 1)
                act.activation(ln[:, b, 0:P], ex[:, b, 0:P], ACT.Ln, bias=1.0).then_inc(c_ln, 1)
                inverse_root(nb, b, c_c, 3 * (nb + 1), c_rstd)

            pairs(act, NB, node_c)

        @block.tensor
        def _(pe):
            pe.wait_ge(pool_consts, 5)
            pe.wait_ge(weights_in, 16 * 22)
            pe.transpose(bank[0][:, 0:D], w_sb[:, :], ident[:, :]).then_inc(su_pe, 1)
            pe.wait_ge(su_act, 1)
            pe.matmul(bank[1][:, 0:2 * HEADS], wT[:, :], att_blk[:, :], start=True, stop=True).then_inc(su_pe, 1)
            pe.wait_ge(dve_consts, 4)
            pe.matmul(bank[2][0:1, 0:D], ones[:, 0:1], wf2_sb[:, :], start=True, stop=True)
            pe.matmul(bank[3][0:1, 0:D], ones[:, 0:1], wo2_sb[:, :], start=True, stop=True).then_inc(su_pe, 1)
            pe.wait_ge(su_dve, 5)
            pe.matmul(bank[4][:, 0:D], ones[0:1, :], rows_eff[0:1, 1, :], start=True, stop=True)
            pe.matmul(bank[5][:, 0:D], ones[0:1, :], rows_eff[0:1, 2, :], start=True, stop=True).then_inc(su_pe, 1)
            pe.wait_ge(su_dve, 6)
            pe.matmul(bank[6][:, 0:NG], ones[0:1, :], base_f[0:1, :], start=True, stop=True).then_inc(su_pe, 1)
            pe.wait_ge(su_dve, 14)

            def project(nb, b, i):
                pe.wait_ge(a_x_in[b], 16 * (i + 1))
                wait_for(pe, a_xT, nb - 1)
                pe.transpose(bank[b][:, 0:D], xb[:, b, :], ident[:, :]).then_inc(a_turned, 1)
                pe.wait_ge(a_xT, nb + 1)
                wait_for(pe, a_row, 2 * (nb - 1))
                pe.matmul(bank[2 + b][:, 0:D + 2 * HEADS], nT[:, b, :], v_sb[:, :], start=True,
                          stop=True).then_inc(a_v, 1)

            pairs(pe, NB, project)
            pe.wait_ge(a_row, 2 * NB)

            def attend(g, b, i):
                pe.wait_ge(oneT_made, g + 1)
                pe.wait_ge(dkwin_in[b], 16 * (i + 1))
                wait_for(pe, ls_made, g)
                for t in range(T):
                    mm = pe.matmul(bank[0][:, t * 8:t * 8 + 8], oneT[:, b, t, :], dkwin[:, b, :],
                                   start=True, stop=True)
                mm.then_inc(expanded, 1)
                pe.wait_ge(one_made, g + 1)
                pe.wait_ge(msg_made, g + 1)
                wait_for(pe, acc_added, g)
                for t in range(T):
                    pe.matmul(bank[1][:, 0:WN], msg[:, b, t, :], one[:, b, t, :],
                              start=(t == 0), stop=(t == T - 1))
                    mm = pe.matmul(bank[2][:, 0:WN], wgt[:, b, t, :], one[:, b, t, :],
                                   start=(t == 0), stop=(t == T - 1))
                mm.then_inc(summed, 1)

            pairs(pe, NG, attend)
            pe.wait_ge(acc_added, NG)

            def node_b(nb, b, i):
                pe.wait_ge(b_gT, nb + 1)
                wait_for(pe, b_g, nb - 1)
                pe.transpose(bank[b][:, 0:D], gT[:, b, :], ident[:, :]).then_inc(b_c, 1)
                pe.wait_ge(b_y, nb + 1)
                wait_for(pe, b_yT, nb - 1)
                pe.transpose(bank[2 + b][:, 0:D], y1[:, b, :], ident[:, :]).then_inc(b_turned, 1)
                pe.wait_ge(b_yT, nb + 1)
                wait_for(pe, b_hs, nb - 1)
                pe.matmul(bank[4 + b][:, 0:D], nT[:, b, :], win_sb[:, :], start=True, stop=True
                          ).then_inc(b_h, 1)

            pairs(pe, NB, node_b)
            pe.wait_ge(b_hs, NB)
            pe.wait_ge(split_in, 16)

            def filter_part(g, b, i):
                pe.wait_ge(fin_in[b], 16 * (i + 1))
                wait_for(pe, fT_made, g)
                for q in range(2):
                    mm = pe.transpose(bank[0][0:Q * RBF, q * P:(q + 1) * P],
                                      fin[:, b, q * Q * RBF:(q + 1) * Q * RBF], ident[:, :])
                mm.then_inc(f_turned, 1)
                pe.wait_ge(fT_made, g + 1)
                for q in range(2):
                    wait_for(pe, gact_made, 2 * g + q - 1)
                    for t in range(Q):
                        mm = pe.matmul(bank[1 + q][:, t * P:(t + 1) * P], wf1_sb[:, t, :],
                                       fT[:, b, q, :], start=True, stop=True)
                    mm.then_inc(v_made, 1)

            def message_part(g, b, i):
                pe.wait_ge(oneTc_made, g + 1)
                pe.wait_ge(hwin_in[b], 16 * (i + 1))
                for q in range(2):
                    wait_for(pe, hsb_made, 2 * g + q)
                    for t in range(Q):
                        mm = pe.matmul(bank[3][:, t * P:(t + 1) * P], oneTc[:, b, q * Q + t, :],
                                       hwin[:, b, :], start=True, stop=True)
                    mm.then_inc(hd_made, 1)
                    pe.wait_ge(gact_made, 2 * g + q + 1)
                    wait_for(pe, xij_made, 2 * g + q - 1)
                    pe.matmul(bank[4 + q][:, :], ones_bf[0:3, :],
                              bf2_3[:, :].unsqueeze(1).to_broadcast([3, Q, D]), start=True, stop=False)
                    for t in range(Q):
                        mm = pe.matmul(bank[4 + q][:, t * P:(t + 1) * P],
                                       gact[:, b, q, t * P:(t + 1) * P], wf2_sb[:, :],
                                       start=False, stop=(t == Q - 1))
                    mm.then_inc(wij_made, 1)
                pe.wait_ge(eq_made, g + 1)
                wait_for(pe, dup_made, g)
                for t in range(T):
                    mm = pe.matmul(bank[7][:, t:t + 1], eq[:, b, t, :], rank_w[:, 0:1],
                                   start=True, stop=True)
                mm.then_inc(rank_made, 1)
                for q in range(2):
                    pe.wait_ge(xij_made, 2 * g + q + 1)
                    wait_for(pe, xo_made, 2 * g + q)
                    for t in range(Q):
                        mm = pe.matmul(bank[6][:, t * P:(t + 1) * P], eq[:, b, q * Q + t, :],
                                       xij[:, q, t * P:(t + 1) * P], start=True, stop=True)
                    mm.then_inc(presummed, 1)

            skewed(pe, filter_part, message_part)
            pe.wait_ge(dup_made, NG)
            pe.wait_ge(xo_made, 2 * NG)

            def node_c(nb, b, i):
                pe.wait_ge(c_ag, nb + 1)
                wait_for(pe, c_agT, nb - 1)
                pe.transpose(bank[b][:, 0:P], ag[:, b, :], ident[:, :]).then_inc(c_turned, 1)
                pe.wait_ge(c_agT, nb + 1)
                wait_for(pe, c_g, nb - 1)
                pe.matmul(bank[2 + b][:, 0:P], wo1_sb[:, :], nT[:, b, :], start=True, stop=True
                          ).then_inc(c_o, 1)
                pe.wait_ge(c_g, nb + 1)
                wait_for(pe, c_fin, nb - 1)
                pe.matmul(bank[4 + b][:, 0:D], gT[:, b, :], wo2_sb[:, :], start=True, stop=True
                          ).then_inc(c_y, 1)

            pairs(pe, NB, node_c)

        @block.vector
        def _(dve):
            dve.memset(zeros[:, :], 0.0).then_inc(dve_consts, 1)
            dve.memset(ones_bf[:, :], 1.0).then_inc(dve_consts, 1)
            dve.memset(eps_c[:, :], EPS).then_inc(dve_consts, 1)
            dve.memset(ones[:, :], 1.0).then_inc(dve_consts, 1)
            dve.memset(accden[:, :, :], 0.0).then_inc(acc_zeroed, 1)
            dve.wait_ge(pool_consts, 5)
            dve.tensor_scalar(rank_cap[:, :], iota_p[:, :], -LN2, 60 * LN2, ALU.mult, ALU.add
                              ).then_inc(su_dve, 1)
            dve.wait_ge(weights_in, 16 * 22)
            dve.tensor_copy(v_sb[:, 0:D], w_sb[:, :]).then_inc(su_dve, 1)
            dve.wait_ge(su_pe, 3)
            dve.scalar_tensor_tensor(out=rows_eff[0:1, 0, :], in0=bank[2][0:1, 0:D], scalar=-LN2,
                                     in1=rows_in[0:1, 0, :], op0=ALU.mult, op1=ALU.add
                                     ).then_inc(su_dve, 1)
            dve.scalar_tensor_tensor(out=rows_eff[0:1, 1, :], in0=bank[3][0:1, 0:D], scalar=-LN2,
                                     in1=rows_in[0:1, 1, :], op0=ALU.mult, op1=ALU.add
                                     ).then_inc(su_dve, 1)
            dve.tensor_copy(rows_eff[0:1, 2, :], rows_in[0:1, 2, :]).then_inc(su_dve, 1)
            dve.wait_ge(index_in, 16)
            dve.tensor_copy(base_f[:, :], dst_all[0:1, :, 0]).then_inc(su_dve, 1)
            chain = [6]

            def link(ins):
                chain[0] += 1
                ins.then_inc(su_dve, 1)
                dve.wait_ge(su_dve, chain[0])

            dve.wait_ge(su_dve, 6)
            parts = [rows_eff[0:1, 0, :], split_f[0:1, 0, :], split_f[0:1, 1, :]]
            dve.tensor_copy(split_b[0:1, 0, :], parts[0]).then_inc(acc_zeroed, 1)
            dve.wait_ge(acc_zeroed, 2)
            dve.tensor_tensor(parts[1], parts[0], split_b[0:1, 0, :], ALU.subtract).then_inc(acc_zeroed, 1)
            dve.wait_ge(acc_zeroed, 3)
            dve.tensor_copy(split_b[0:1, 1, :], parts[1]).then_inc(acc_zeroed, 1)
            dve.wait_ge(acc_zeroed, 4)
            dve.tensor_tensor(parts[2], parts[1], split_b[0:1, 1, :], ALU.subtract).then_inc(acc_zeroed, 1)
            dve.wait_ge(acc_zeroed, 5)
            link(dve.tensor_copy(split_b[0:1, 2, :], parts[2]))
            dve.wait_ge(su_pe, 4)
            link(dve.tensor_copy(v_sb[:, D:D + 2 * HEADS], bank[1][:, 0:2 * HEADS]))
            link(dve.tensor_copy(bc[:, 0, :], bank[4][:, 0:D]))
            link(dve.tensor_copy(bc[:, 1, :], bank[5][:, 0:D]))
            dve.wait_ge(su_act, 2)
            link(dve.tensor_scalar(rank_cap[:, :], rank_w[:, :], 2.5, None, ALU.mult))
            dve.wait_ge(su_pe, 5)
            link(dve.tensor_copy(base_bc[:, :], bank[6][:, 0:NG]))
            link(dve.tensor_scalar(node_id[:, :], base_bc[:, :], iota_p[:, 0:1], None, ALU.add))
            link(dve.tensor_tensor(rel_all[:, :, :], dst_all[:, :, :],
                                   base_bc[:, :].unsqueeze(2).to_broadcast([P, NG, T]),
                                   ALU.subtract))

            def row_a(nb, b, i):
                dve.wait_ge(a_v, nb + 1)
                if not isinstance(i, int) or i > 0:
                    dve.wait_ge(a_out[b], 16 * i)
                dve.tensor_copy(nS[:, b, 0:ROW], bank[2 + b][:, 0:ROW]).then_inc(a_row, 1)
                dve.tensor_copy(sd_all[:, bass.ds(nb, 1), :].rearrange("p o c -> p (o c)"),
                                bank[2 + b][:, D:D + 2 * HEADS]).then_inc(a_row, 1)

            pairs(dve, NB, row_a)

            dve.wait_ge(a_row, 2 * NB)
            s_hn = sd_all[:, :, 0:HEADS].rearrange("p n h -> p h n")
            dve.tensor_reduce(ext[:, 0:HEADS], s_hn, AX.X, ALU.max).then_inc(ext_ready, 1)
            dve.tensor_reduce(ext[:, HEADS:2 * HEADS], s_hn, AX.X, ALU.min, negate=True).then_inc(ext_ready, 1)
            dve.tensor_reduce(ext[:, 8:9], rel_all[:, :, :], AX.XY, ALU.max).then_inc(ext_ready, 1)
            dve.tensor_reduce(ext[:, 9:10], rel_all[:, :, :], AX.XY, ALU.min, negate=True).then_inc(ext_ready, 1)
            dve.wait_ge(ext_reduced, 1)
            link(dve.tensor_copy(dk_all[:, :, 0:HEADS], sd_all[:, :, HEADS:2 * HEADS]))
            link(dve.tensor_tensor(zk[:, :, :], sd_all[:, :, HEADS:2 * HEADS],
                                   ext_all[:, 0:HEADS].unsqueeze(1).to_broadcast([P, NB, HEADS]), ALU.add))
            dve.scalar_tensor_tensor(out=dk_all[:, :, HEADS:2 * HEADS], in0=zk[:, :, :], scalar=SLOPE,
                                     in1=zk[:, :, :], op0=ALU.mult, op1=ALU.max).then_inc(dk_ready, 1)
            dve.wait_ge(dk_ready, 1)

            def attend(g, b, i):
                dve.wait_ge(drow_in[b], 16 * (i + 1))
                wait_for(dve, expanded, g - 1)
                dve.tensor_scalar(oneT[:, b, :, :].rearrange("n t p -> n p t"),
                                  drow[:, b, :].rearrange("n (p t) -> n p t", t=T),
                                  node_id[0:WN, bass.ds(g, 1)], None, ALU.is_equal).then_inc(oneT_made, 1)
                wait_for(dve, summed, g - 1)
                dve.tensor_tensor(one[:, b, :, :], iota_w[:, :].unsqueeze(1).to_broadcast([P, T, WN]),
                                  rel_all[:, bass.ds(g, 1), :].rearrange("p o t -> p (o t)")
                                  .unsqueeze(2).to_broadcast([P, T, WN]), ALU.is_equal).then_inc(one_made, 1)
                dve.wait_ge(rows_got[b], 16 * T * (i + 1))
                dve.wait_ge(expanded, g + 1)
                pd = bank[0][:, 0:T * 8].rearrange("p (t c) -> p t c", c=8)
                dve.tensor_tensor(z[:, b, :, :], rows[:, b, :, D:ROW], pd[:, :, 0:HEADS], ALU.add
                                  ).then_inc(z_made, 1)
                dve.wait_ge(z_made, g + 1)
                dve.scalar_tensor_tensor(out=lg[:, b, :, :], in0=z[:, b, :, :], scalar=SLOPE,
                                         in1=z[:, b, :, :], op0=ALU.mult, op1=ALU.max).then_inc(lg_made, 1)
                dve.wait_ge(lg_made, g + 1)
                wait_for(dve, wgt_made, g - 1)
                dve.tensor_tensor(ls[:, b, :, :], lg[:, b, :, :], pd[:, :, HEADS:2 * HEADS], ALU.subtract
                                  ).then_inc(ls_made, 1)
                dve.wait_ge(wgt_made, g + 1)
                dve.tensor_tensor(msg[:, b, :, :], rows[:, b, :, 0:D], wgt[:, b, :, :], ALU.mult
                                  ).then_inc(msg_made, 1)
                dve.wait_ge(summed, g + 1)
                wait_for(dve, acc_added, g)
                base = dve.value_load(dst_all[0:1, bass.ds(g, 1), 0], min_val=0, max_val=NT - WN)
                for k in range(2):
                    ins = dve.tensor_tensor(accden[:, k, bass.ds(base, WN)], accden[:, k, bass.ds(base, WN)],
                                            bank[1 + k][:, 0:WN], ALU.add)
                    if k:
                        ins.then_inc(acc_added, 1)

            pairs(dve, NG, attend)
            dve.wait_ge(acc_added, NG)

            def norm(nb, b, c_sem, c0, rstd_sem, out_sem):
                dve.bn_stats(stats[:, b, :], t2[:, b, :]).then_inc(c_sem, 1)
                wait_apart(dve, c_sem, c0 + 1, dve_passed)
                dve.bn_aggr(mv[:, b, :], stats[:, b, :]).then_inc(c_sem, 1)
                dve.wait_ge(c_sem, c0 + 2)
                dve.wait_ge(rstd_sem, 2 * (nb + 1))
                dve.tensor_scalar(y1[:, b, :], t2[:, b, :], mv[:, b, 0:1], rstd[:, b, 0:1],
                                  ALU.subtract, ALU.mult).then_inc(out_sem, 1)

            def node_b(nb, b, i):
                c0 = nb * 5
                dve.tensor_scalar(den[:, b, :], accden[:, 1, bass.ds(nb * P, P)], 1e-37, None, ALU.max
                                  ).then_inc(chain_b, 1)
                dve.wait_ge(chain_b, c0 + 1)
                dve.reciprocal(rec[:, b, :], den[:, b, :]).then_inc(chain_b, 1)
                dve.wait_ge(chain_b, c0 + 2)
                wait_for(dve, b_c, nb - 1)
                dve.tensor_tensor(gT[:, b, :], accden[:, 0, bass.ds(nb * P, P)], rec[:, b, :], ALU.mult
                                  ).then_inc(b_gT, 1)
                dve.wait_ge(b_c, nb + 1)
                dve.wait_ge(b_x_in[b], 16 * (i + 1))
                dve.tensor_tensor(t1[:, b, :], bank[b][:, 0:D], xb[:, b, :], ALU.add).then_inc(b_g, 1)
                dve.wait_ge(b_g, nb + 1)
                dve.tensor_tensor(t2[:, b, :], t1[:, b, :], bc[:, 1, :], ALU.add).then_inc(chain_b, 1)
                dve.wait_ge(chain_b, c0 + 3)
                if not isinstance(i, int) or i > 0:
                    dve.wait_ge(b_y_out[b], 16 * i)
                wait_for(dve, b_turned, nb - 1)
                norm(nb, b, chain_b, c0 + 3, b_rstd, b_y)

            pairs(dve, NB, node_b)
            dve.wait_ge(b_y, NB)
            dve.wait_ge(b_c, NB)

            def filter_part(g, b, i):
                dve.wait_ge(srow_in[b], 16 * (i + 1))
                dve.wait_ge(scol_in[b], 16 * (i + 1))
                wait_for(dve, presummed, 2 * (g - 1))
                dve.tensor_tensor(eq[:, b, :, :], srow[:, b, :].rearrange("k (p t) -> k t p", t=T),
                                  scol[:, b, :].unsqueeze(2).to_broadcast([P, T, P]), ALU.is_equal
                                  ).then_inc(eq_made, 1)
                dve.wait_ge(drow1_in[b], 16 * (i + 1))
                dve.wait_ge(crow_in[b], 16 * (i + 1))
                wait_for(dve, hd_made, 2 * (g - 1))
                dve.scalar_tensor_tensor(out=oneTc[:, b, :, :].rearrange("n t p -> n p t"),
                                         in0=drow[:, b, :].rearrange("n (p t) -> n p t", t=T),
                                         scalar=node_id[0:WN, bass.ds(g, 1)],
                                         in1=crow[:, b, :].rearrange("n (p t) -> n p t", t=T),
                                         op0=ALU.is_equal, op1=ALU.mult).then_inc(oneTc_made, 1)
                for q in range(2):
                    dve.wait_ge(v_made, 2 * g + q + 1)
                    wait_for(dve, ex_made, 2 * g + q - 1)
                    dve.tensor_scalar(exc[:, q, :], bank[1 + q][:, :], bf1_c[:, 0:1], V_CAP, ALU.add,
                                      ALU.min).then_inc(exc_made, 1)
                for q in range(2):
                    dve.wait_ge(ln_made, 2 * g + q + 1)
                    if q == 0:
                        wait_for(dve, wij_made, 2 * (g - 1))
                    dve.scalar_tensor_tensor(out=gact[:, b, q, :], in0=bank[1 + q][:, :],
                                             scalar=bf1_c[:, 0:1], in1=ln[:, q, :], op0=ALU.add,
                                             op1=ALU.max).then_inc(gact_made, 1)

            def message_part(g, b, i):
                for q in range(2):
                    dve.wait_ge(hsb_made, 2 * g + q + 1)
                    dve.wait_ge(wij_made, 2 * g + q + 1)
                    wait_for(dve, presummed, 2 * g + q - 1)
                    dve.tensor_tensor(xij[:, q, :], bank[4 + q][:, :], hsb[:, q, :], ALU.mult
                                      ).then_inc(xij_made, 1)
                dve.wait_ge(rank_made, g + 1)
                dve.tensor_scalar(dup[:, b, :], bank[7][:, 0:T], rank_cap[:, 0:1], float(SKIP),
                                  ALU.is_gt, ALU.mult).then_inc(dup_made, 1)
                dve.wait_ge(dup_made, g + 1)
                dve.tensor_tensor(sidx_f[:, b, :], dup[:, b, :], scol[:, b, :], ALU.add).then_inc(sidxf_made, 1)
                dve.wait_ge(sidxf_made, g + 1)
                wait_for(dve, earlier_added, g)
                dve.tensor_tensor(sidx[:, b, :], sidx_f[:, b, :], copy_row[:, :], ALU.add).then_inc(sidx_made, 1)

            skewed(dve, filter_part, message_part)

            def node_c(nb, b, i):
                c0 = nb * 3
                dve.wait_ge(c_agg_in[b], 16 * (i + 1))
                wait_for(dve, c_turned, nb - 1)
                dve.tensor_reduce(ag[:, b, :], agg8[:, b, :, :].rearrange("p c f -> p f c"), AX.X, ALU.add
                                  ).then_inc(c_ag, 1)
                dve.wait_ge(c_o, nb + 1)
                wait_for(dve, c_ex, nb - 1)
                dve.tensor_scalar(exc[:, b, 0:P], bank[2 + b][:, 0:P], bo1_c[:, 0:1], V_CAP, ALU.add,
                                  ALU.min).then_inc(c_exc, 1)
                dve.wait_ge(c_ln, nb + 1)
                wait_for(dve, c_y, nb - 1)
                dve.scalar_tensor_tensor(out=gT[:, b, :], in0=bank[2 + b][:, 0:P], scalar=bo1_c[:, 0:1],
                                         in1=ln[:, b, 0:P], op0=ALU.add, op1=ALU.max).then_inc(c_g, 1)
                dve.wait_ge(c_y, nb + 1)
                dve.tensor_tensor(t1[:, b, :], bank[4 + b][:, 0:D], bc[:, 0, :], ALU.add).then_inc(c_c, 1)
                dve.wait_ge(c_c, c0 + 1)
                dve.wait_ge(c_x_in[b], 16 * (i + 1))
                if not isinstance(i, int) or i > 0:
                    dve.wait_ge(c_out[b], 16 * i)
                dve.tensor_tensor(t2[:, b, :], t1[:, b, :], xb[:, b, :], ALU.add).then_inc(c_t2, 1)
                dve.wait_ge(c_t2, nb + 1)
                norm(nb, b, c_c, c0 + 1, c_rstd, c_fin)

            pairs(dve, NB, node_c)



def kernel(**inputs):
    import numpy as np
    import concourse.bacc as bacc
    from concourse.bass_utils import run_bass_kernel_spmd

    def padded(a, rows, fill=0):
        a = np.asarray(a)
        return np.concatenate([a, np.full((rows - a.shape[0],) + a.shape[1:], fill, a.dtype)])

    arrays = {
        "x": padded(inputs["x"], NT),
        "src": padded(inputs["src"], EP, N),
        "dst": padded(inputs["dst"], EP, N),
        "f_ij": padded(np.asarray(inputs["edge_attr3_1x20"]).reshape(E, RBF), EP),
        "cut": padded(np.asarray(inputs["edge_weight1"]).reshape(E), EP),
        "W": inputs["L0_gnn_W"], "att": inputs["L0_gnn_att"], "bias0": inputs["L0_gnn_bias"],
        "W_in": inputs["L1_gnn_W_in"], "W_f1": inputs["L1_gnn_W_f1"], "b_f1": inputs["L1_gnn_b_f1"],
        "W_f2": inputs["L1_gnn_W_f2"], "b_f2": inputs["L1_gnn_b_f2"],
        "W_o1": inputs["L1_gnn_W_o1"], "b_o1": inputs["L1_gnn_b_o1"],
        "W_o2": inputs["L1_gnn_W_o2"], "b_o2": inputs["L1_gnn_b_o2"],
    }
    arrays = {f"in_{k}": np.ascontiguousarray(v) for k, v in arrays.items()}
    nc = bacc.Bacc("TRN2", target_bir_lowering=False, num_devices=1)
    args = [nc.dram_tensor(k, a.shape, mybir.dt.from_np(a.dtype), kind="ExternalInput").ap()
            for k, a in arrays.items()]
    out = nc.dram_tensor("out", (NT, D), F32, kind="ExternalOutput").ap()
    gnn_kernel(nc, *args, out)
    r = run_bass_kernel_spmd(nc, [arrays], core_ids=[0])
    return r.results[0]["out"][:N]
```

```python
import concourse.bass as bass
from concourse import mybir
from contextlib import ExitStack

P = 128
D = 128
HEADS = 4
F = D // HEADS
RBF = 20
N = 6250
E = 200000
T = 8
GE = P * T
NG = -(-E // (2 * GE)) * 2
EP = NG * GE
GP = NG // 2
K = 4
NS = -(-(N + P + 1) // (K * P))
NB = K * NS
NT = NB * P
SPLIT = 3
WN = P // SPLIT
W3 = SPLIT * WN
Q = 4
COPIES = 4
ROW = D + HEADS
COLS = D + 2 * HEADS
SLOPE = 0.2
EPS = 1e-5
LN2 = 0.6931471805599453
SPREAD_MAX = 60.0
V_CAP = 40.0

ALU = mybir.AluOpType
ACT = mybir.ActivationFunctionType
AX = mybir.AxisListType
F32 = mybir.dt.float32
I32 = mybir.dt.int32
I16 = mybir.dt.int16
U32 = mybir.dt.uint32
BF16 = mybir.dt.bfloat16
RMAX = bass.bass_isa.ReduceOp.max


def wait_for(eng, sem, count):
    if isinstance(count, int) and count <= 0:
        return
    eng.wait_ge(sem, count)


def wait_apart(eng, sem, count, passed):
    if isinstance(count, int) and count <= 0:
        return
    eng.wait_ge(sem, count)
    eng.sem_inc(passed, 1)


def interleaved(eng, total, parts):
    lead = max(ahead for ahead, _ in parts)

    def step(g, b, i):
        for ahead, stage in parts:
            if isinstance(g, int) and not 0 <= g + ahead < total:
                continue
            pair = i + (b + ahead) // 2 if (b + ahead) // 2 else i
            stage(g + ahead if ahead else g, (b + ahead) % 2, pair)

    for g in range(-lead, 2):
        step(g, g % 2, g // 2)
    whole = (total - lead) // 2
    with eng.Fori(1, whole) as i:
        for b in range(2):
            step(i * 2 + b if b else i * 2, b, i)
    for g in range(2 * whole, total):
        step(g, g % 2, g // 2)


def done(total, b):
    return 16 * ((total - b + 1) // 2)


def gnn_kernel(nc, x, src, dst, f_ij, cut, W, att, bias0, W_in, W_f1, b_f1, W_f2, b_f2,
               W_o1, b_o1, W_o2, b_o2, out):
    with ExitStack() as ctx:
        def sb(name, shape, dt=F32):
            return ctx.enter_context(nc.sbuf_tensor(name, shape, dt))

        def sem(name):
            return ctx.enter_context(nc.semaphore(name))

        src16_d = nc.dram_tensor("src16_d", [EP], I16)
        dst16_d = nc.dram_tensor("dst16_d", [EP], I16)
        wh_d = nc.dram_tensor("wh_d", [NT, ROW], F32)
        ad3_d = nc.dram_tensor("ad3_d", [SPLIT * NT, HEADS], BF16)
        h3_d = nc.dram_tensor("h3_d", [SPLIT * NT, D], BF16)
        x1_d = nc.dram_tensor("x1_d", [NT, D], F32)
        agg_d = nc.dram_tensor("agg_d", [COPIES * NT, D], F32)

        bank = [ctx.enter_context(nc.psum_tensor(f"bank{i}", [P, 512], F32)) for i in range(8)]

        ident = sb("ident", [P, P])
        ones = sb("ones", [P, P])
        ones_bf = sb("ones_bf", [P, P], BF16)
        iota_w = sb("iota_w", [P, WN])
        iota_3w = sb("iota_3w", [P, WN])
        below = sb("below", [P, WN])
        third = sb("third", [P, 1])
        iota_p = sb("iota_p", [P, 1])
        copy_row = sb("copy_row", [P, T])
        spare_row = sb("spare_row", [P, T])
        rank_w = sb("rank_w", [P, 1], BF16)
        rank_cap = sb("rank_cap", [P, 1])
        zeros = sb("zeros", [P, D])
        w_sb = sb("w_sb", [P, D])
        wT = sb("wT", [P, D])
        att_blk = sb("att_blk", [P, 2 * HEADS])
        v_sb = sb("v_sb", [P, COLS])
        win_sb = sb("win_sb", [P, D])
        wf1_sb = sb("wf1_sb", [P, Q, D])
        wf2_sb = sb("wf2_sb", [P, D])
        wo1_sb = sb("wo1_sb", [P, D])
        wo2_sb = sb("wo2_sb", [P, D])
        bf1_c = sb("bf1_c", [P, 1])
        bo1_c = sb("bo1_c", [P, 1])
        rows_in = sb("rows_in", [1, 3, D])
        rows_eff = sb("rows_eff", [1, 3, D])
        rest = sb("rest", [1, 2, D])
        split_b = sb("split_b", [1, SPLIT, D], BF16)
        bf2_3 = sb("bf2_3", [SPLIT, D], BF16)
        bc = sb("bc", [P, 2, D])
        first_dst = sb("first_dst", [1, NG], I32)
        first_f = sb("first_f", [1, NG])
        first_row = sb("first_row", [1, NG], I32)
        base_bc = sb("base_bc", [P, NG])
        node_id = sb("node_id", [P, NG])
        edges = sb("edges", [GP, 2, GE], I32)
        edges16 = sb("edges16", [GP, 2, GE], I16)
        group_f = sb("group_f", [GP, 5, 2])
        sd_all = sb("sd_all", [P, NB, 2 * HEADS])
        ad_rest = sb("ad_rest", [P, 2, NB, HEADS])
        ad3 = sb("ad3", [P, NB, SPLIT, HEADS], BF16)
        ext = sb("ext", [P, 2 * HEADS + 2])
        ext_all = sb("ext_all", [P, 2 * HEADS + 2])
        eps_c = sb("eps_c", [P, 1])
        acc = sb("acc", [P, NT])
        den = sb("den", [HEADS, NT])
        idx = sb("idx", [P, 2, T], I32)
        dcol = sb("dcol", [P, 2, T], I32)
        drow = sb("drow", [W3, 2, GE], I16)
        adwin = sb("adwin", [W3, 2, HEADS], BF16)
        rows = sb("rows", [P, 2, T, ROW])
        oneT = sb("oneT", [W3, 2, T, P], BF16)
        rel = sb("rel", [P, 2, T])
        one = sb("one", [P, 2, T, WN])
        z = sb("z", [P, 2, T, 2 * HEADS])
        lg = sb("lg", [P, 2, T, 2 * HEADS])
        ls = sb("ls", [P, 2, T, HEADS])
        msg = sb("msg", [P, 2, T, ROW])
        win = sb("win", [WN, 2, ROW])
        xb = sb("xb", [P, 2, K, D])
        nT = sb("nT", [P, 2, K, P])
        nS = sb("nS", [P, 2, K, COLS])
        accs = sb("accs", [P, 2, K, P])
        dens = sb("dens", [HEADS, 2, K, P])
        clamped = sb("clamped", [P, 2, K * HEADS])
        rec = sb("rec", [P, 2, K * HEADS])
        xbias = sb("xbias", [P, 2, K, D])
        t1 = sb("t1", [P, 2, K, D])
        stats = sb("stats", [P, 2, K, 6])
        mv = sb("mv", [P, 2, K, 2])
        lnvar = sb("lnvar", [P, 2, K])
        rstd = sb("rstd", [P, 2, K])
        y1 = sb("y1", [P, 2, K, D])
        h3 = sb("h3", [P, 2, K, SPLIT, D], BF16)
        hr = accs
        fin = sb("fin", [P, 2, T * RBF])
        srow = sb("srow", [P, 2, GE], I16)
        scol = sb("scol", [P, 2, T], I32)
        ccol = sb("ccol", [P, 2, T])
        hwin = sb("hwin", [W3, 2, D], BF16)
        fT = sb("fT", [P, 2, 2, P])
        exc = sb("exc", [P, 2, 512])
        ex = sb("ex", [P, 2, 512])
        ln = sb("ln", [P, 2, 512])
        gact = sb("gact", [P, 2, 2, 512])
        eq = sb("eq", [P, 2, T, P])
        hsb = sb("hsb", [P, 2, Q, D])
        xij = sb("xij", [P, 2, Q * D])
        away = sb("away", [P, 2, T])
        home = sb("home", [P, 2, T])
        shift = sb("shift", [P, 2, T])
        sidx = sb("sidx", [P, 2, T], I32)
        xo = msg[:, :, :, 0:D]
        agg4 = acc[:, 0:2 * COPIES * K * D].rearrange("p (b c k f) -> p b c k f", b=2, c=COPIES, k=K)
        ag = xbias
        t2 = nS[:, :, :, 0:D]

        made_pool = sem("made_pool")
        made_dve = sem("made_dve")
        padded_cleared = sem("padded_cleared")
        w_in = sem("w_in")
        weights_in = sem("weights_in")
        first_in = sem("first_in")
        edges_in = sem("edges_in")
        edges16_made = sem("edges16_made")
        edges16_out = sem("edges16_out")
        agg_zeroed = sem("agg_zeroed")
        w_turned = sem("w_turned")
        wT_made = sem("wT_made")
        watt_made = sem("watt_made")
        v_ready = sem("v_ready")
        colsums_made = sem("colsums_made")
        rows_ready = sem("rows_ready")
        bc_spread = sem("bc_spread")
        first_ready = sem("first_ready")
        base_spread = sem("base_spread")
        bases_ready = sem("bases_ready")
        split_made = sem("split_made")
        split_in = sem("split_in")
        rank_exp = sem("rank_exp")
        rank_made = sem("rank_made")
        rank_ready = sem("rank_ready")
        third_made = sem("third_made")
        rel_checked = sem("rel_checked")
        group_made = sem("group_made")
        acc_zeroed = sem("acc_zeroed")
        fT_cleared = sem("fT_cleared")
        ext_ready = sem("ext_ready")
        ext_reduced = sem("ext_reduced")
        ad_split = sem("ad_split")
        ad_out = sem("ad_out")
        pool_passed = sem("pool_passed")
        dve_passed = sem("dve_passed")
        pe_passed = sem("pe_passed")
        sp_passed = sem("sp_passed")
        a_x_in = [sem(f"a_x_in{b}") for b in range(2)]
        a_turned = sem("a_turned")
        a_xT = sem("a_xT")
        a_v = sem("a_v")
        a_row = sem("a_row")
        a_out = [sem(f"a_out{b}") for b in range(2)]
        idx_in = [sem(f"idx_in{b}") for b in range(2)]
        dcol_in = [sem(f"dcol_in{b}") for b in range(2)]
        drow_in = [sem(f"drow_in{b}") for b in range(2)]
        adwin_in = [sem(f"adwin_in{b}") for b in range(2)]
        rows_got = [sem(f"rows_got{b}") for b in range(2)]
        oneT_made = sem("oneT_made")
        rel_made = sem("rel_made")
        one_made = sem("one_made")
        expanded = sem("expanded")
        z_made = sem("z_made")
        lg_made = sem("lg_made")
        ls_made = sem("ls_made")
        wgt_made = sem("wgt_made")
        msg_made = sem("msg_made")
        summed = sem("summed")
        win_made = sem("win_made")
        win_turned = sem("win_turned")
        acc_added = sem("acc_added")
        attended = sem("attended")
        b_x_in = [sem(f"b_x_in{b}") for b in range(2)]
        b_accs = sem("b_accs")
        b_turned = sem("b_turned")
        b_clamped = sem("b_clamped")
        b_rec = sem("b_rec")
        b_t1 = sem("b_t1")
        b_xbias = sem("b_xbias")
        b_t2 = sem("b_t2")
        b_stats = sem("b_stats")
        b_mv = sem("b_mv")
        b_lnvar = sem("b_lnvar")
        b_rstd = sem("b_rstd")
        b_y = sem("b_y")
        b_yturned = sem("b_yturned")
        b_yT = sem("b_yT")
        b_h = sem("b_h")
        b_hi = sem("b_hi")
        b_hr = sem("b_hr")
        b_mid = sem("b_mid")
        b_lo = sem("b_lo")
        b_y_out = [sem(f"b_y_out{b}") for b in range(2)]
        b_h_out = [sem(f"b_h_out{b}") for b in range(2)]
        fin_in = [sem(f"fin_in{b}") for b in range(2)]
        srow_in = [sem(f"srow_in{b}") for b in range(2)]
        scol_in = [sem(f"scol_in{b}") for b in range(2)]
        ccol_in = [sem(f"ccol_in{b}") for b in range(2)]
        drow1_in = [sem(f"drow1_in{b}") for b in range(2)]
        hwin_in = [sem(f"hwin_in{b}") for b in range(2)]
        f_turned = sem("f_turned")
        fT_made = sem("fT_made")
        v_made = sem("v_made")
        exc_made = sem("exc_made")
        ex_made = sem("ex_made")
        ln_made = sem("ln_made")
        gact_made = sem("gact_made")
        eq_made = sem("eq_made")
        oneT1_made = sem("oneT1_made")
        hd_made = sem("hd_made")
        hsb_made = sem("hsb_made")
        wij_made = sem("wij_made")
        xij_made = sem("xij_made")
        ranked = sem("ranked")
        away_made = sem("away_made")
        home_made = sem("home_made")
        shift_made = sem("shift_made")
        sidx_made = sem("sidx_made")
        presummed = sem("presummed")
        xo_made = sem("xo_made")
        earlier_added = sem("earlier_added")
        added = [sem(f"added{c}") for c in range(COPIES)]
        c_agg_in = [sem(f"c_agg_in{b}") for b in range(2)]
        c_x_in = [sem(f"c_x_in{b}") for b in range(2)]
        c_ag = sem("c_ag")
        c_turned = sem("c_turned")
        c_agT = sem("c_agT")
        c_o = sem("c_o")
        c_exc = sem("c_exc")
        c_ex = sem("c_ex")
        c_ln = sem("c_ln")
        c_g = sem("c_g")
        c_y = sem("c_y")
        c_t1 = sem("c_t1")
        c_t2 = sem("c_t2")
        c_stats = sem("c_stats")
        c_mv = sem("c_mv")
        c_lnvar = sem("c_lnvar")
        c_rstd = sem("c_rstd")
        c_fin = sem("c_fin")
        c_out = [sem(f"c_out{b}") for b in range(2)]

        src_g = src.rearrange("(g p t) -> g p t", p=P, t=T)
        dst_g = dst.rearrange("(g p t) -> g p t", p=P, t=T)
        cut_g = cut.rearrange("(g p t) -> g p t", p=P, t=T)
        f_g = f_ij.rearrange("(g p t) r -> g p (t r)", p=P, t=T)
        src16_g = src16_d[:].rearrange("(g e) -> g e", e=GE)
        dst16_g = dst16_d[:].rearrange("(g e) -> g e", e=GE)
        x_k = x.rearrange("(p k) f -> p k f", k=NB)
        out_k = out.rearrange("(p k) f -> p k f", k=NB)
        wh_k = wh_d[:, :].rearrange("(p k) f -> p k f", k=NB)
        x1_k = x1_d[:, :].rearrange("(p k) f -> p k f", k=NB)
        h3_k = h3_d[:, :].rearrange("(p k c) f -> p k c f", k=NB, c=SPLIT)
        agg_k = agg_d[:, :].rearrange("(c p k) f -> c p k f", c=COPIES, k=NB)
        acc_k = acc[:, :].rearrange("f (p k) -> f k p", k=NB)
        den_k = den[:, :].rearrange("h (p k) -> h k p", k=NB)

        def four(s):
            return bass.ds(s * K, K)

        block = ctx.enter_context(nc.Block())

        @block.sync
        def _(sp):
            sp.dma_start(w_sb[:, :], W).then_inc(w_in, 16)
            sp.wait_ge(padded_cleared, 2)
            for h in range(HEADS):
                for side in range(2):
                    sp.dma_start(att_blk[F * h:F * h + F, side * HEADS + h:side * HEADS + h + 1],
                                 att[h:h + 1, side * F:side * F + F].rearrange("o f -> f o"),
                                 allow_slow_non_contiguous=True).then_inc(w_in, 16)

            def load_a(s, b, i):
                wait_apart(sp, a_turned, s - 1, sp_passed)
                sp.dma_start(xb[:, b, :, :], x_k[:, four(s), :]).then_inc(a_x_in[b], 16)

            def store_a(s, b, i):
                wait_apart(sp, a_row, 2 * (s + 1), sp_passed)
                sp.dma_start(wh_k[:, four(s), :], nS[:, b, :, 0:ROW]).then_inc(a_out[b], 16)

            interleaved(sp, NS, [(1, load_a), (0, store_a)])
            sp.wait_ge(ad_split, 5)
            sp.dma_start(ad3_d[:, :].rearrange("(p k c) h -> p (k c h)", k=NB, c=SPLIT),
                         ad3[:, :, :, :].rearrange("p k c h -> p (k c h)")).then_inc(ad_out, 16)

            sp.wait_ge(edges16_out, 16)
            sp.wait_ge(first_ready, 2)
            sp.wait_ge(split_made, 5)
            sp.dma_start(bf2_3[:, :], split_b[0:1, :, :]).then_inc(split_in, 16)

            def load_group0(g, b, i):
                wait_apart(sp, z_made, 2 * (g - 1), sp_passed)
                sp.dma_start(idx[:, b, :], src_g[bass.ds(g, 1), :, :].rearrange("o p t -> p (o t)")
                             ).then_inc(idx_in[b], 16)
                wait_apart(sp, rel_made, g - 1, sp_passed)
                sp.dma_start(dcol[:, b, :], dst_g[bass.ds(g, 1), :, :].rearrange("o p t -> p (o t)")
                             ).then_inc(dcol_in[b], 16)
                wait_apart(sp, oneT_made, g - 1, sp_passed)
                sp.dma_start(drow[:, b, :], dst16_g[bass.ds(g, 1), :].to_broadcast([W3, GE])
                             ).then_inc(drow_in[b], 16)
                if isinstance(g, int) and g == 0:
                    sp.wait_ge(ad_out, 16)
                wait_apart(sp, expanded, g - 1, sp_passed)
                row = sp.value_load(first_row[0:1, bass.ds(g, 1)], min_val=0, max_val=SPLIT * (NT - WN))
                sp.dma_start(adwin[:, b, :], ad3_d[bass.ds(row, W3), :]).then_inc(adwin_in[b], 16)

            interleaved(sp, NG, [(0, load_group0)])

            def load_b(s, b, i):
                wait_apart(sp, b_xbias, s - 1, sp_passed)
                sp.dma_start(xb[:, b, :, :], x_k[:, four(s), :]).then_inc(b_x_in[b], 16)

            def store_b(s, b, i):
                wait_apart(sp, b_y, s + 1, sp_passed)
                sp.dma_start(x1_k[:, four(s), :], y1[:, b, :, :]).then_inc(b_y_out[b], 16)
                wait_apart(sp, b_lo, s + 1, sp_passed)
                sp.dma_start(h3_k[:, four(s), :, :], h3[:, b, :, :, :]).then_inc(b_h_out[b], 16)

            sp.wait_ge(a_turned, NS)
            interleaved(sp, NS, [(1, load_b), (0, store_b)])

            sp.wait_ge(oneT_made, NG)
            sp.wait_ge(edges16_out, 32)

            def load_group1(g, b, i):
                wait_apart(sp, f_turned, g - 1, sp_passed)
                sp.dma_start(fin[:, b, :], f_g[bass.ds(g, 1), :, :].rearrange("o p c -> p (o c)")
                             ).then_inc(fin_in[b], 16)
                wait_apart(sp, eq_made, g - 1, sp_passed)
                sp.dma_start(srow[:, b, :], src16_g[bass.ds(g, 1), :].to_broadcast([P, GE])
                             ).then_inc(srow_in[b], 16)
                wait_apart(sp, away_made, g - 1, sp_passed)
                wait_apart(sp, home_made, g - 1, sp_passed)
                sp.dma_start(scol[:, b, :], src_g[bass.ds(g, 1), :, :].rearrange("o p t -> p (o t)")
                             ).then_inc(scol_in[b], 16)
                wait_apart(sp, oneT1_made, g - 1, sp_passed)
                sp.dma_start(drow[:, b, :], dst16_g[bass.ds(g, 1), :].to_broadcast([W3, GE])
                             ).then_inc(drow1_in[b], 16)
                wait_apart(sp, hsb_made, 2 * (g - 1), sp_passed)
                sp.dma_start(ccol[:, b, :], cut_g[bass.ds(g, 1), :, :].rearrange("o p t -> p (o t)")
                             ).then_inc(ccol_in[b], 16)
                if isinstance(g, int) and g == 0:
                    for b_out in range(2):
                        sp.wait_ge(b_h_out[b_out], done(NS, b_out))
                wait_apart(sp, hd_made, 2 * (g - 1), sp_passed)
                row = sp.value_load(first_row[0:1, bass.ds(g, 1)], min_val=0, max_val=SPLIT * (NT - WN))
                sp.dma_start(hwin[:, b, :], h3_d[bass.ds(row, W3), :]).then_inc(hwin_in[b], 16)

            interleaved(sp, NG, [(0, load_group1)])

            for c in range(COPIES):
                sp.wait_ge(added[c], 16 * NG * T // COPIES)

            def load_agg_c(s, b, i):
                wait_apart(sp, c_ag, s - 1, sp_passed)
                for c in range(COPIES):
                    sp.dma_start(agg4[:, b, c, :, :],
                                 agg_k[c:c + 1, :, four(s), :].rearrange("o p k f -> p (o k) f")
                                 ).then_inc(c_agg_in[b], 16)

            def load_x_c(s, b, i):
                wait_apart(sp, c_t2, s - 1, sp_passed)
                sp.dma_start(xb[:, b, :, :], x1_k[:, four(s), :]).then_inc(c_x_in[b], 16)

            def store_c(s, b, i):
                wait_apart(sp, c_fin, s + 1, sp_passed)
                sp.dma_start(out_k[:, four(s), :], y1[:, b, :, :]).then_inc(c_out[b], 16)

            sp.wait_ge(b_xbias, NS)
            for b in range(2):
                sp.wait_ge(b_y_out[b], done(NS, b))
            interleaved(sp, NS, [(2, load_agg_c), (1, load_x_c), (0, store_c)])
            for b in range(2):
                sp.wait_ge(c_out[b], done(NS, b))

        @block.gpsimd
        def _(pool):
            pool.memset(wf1_sb[:, :, :], 0.0).then_inc(padded_cleared, 1)
            pool.memset(att_blk[:, :], 0.0).then_inc(padded_cleared, 1)
            pool.memset(ident[:, :], 0.0).then_inc(made_pool, 1)
            pool.wait_ge(made_pool, 1)
            pool.affine_select(out=ident[:, :], in_=ident[:, :], compare_op=ALU.not_equal, fill=1.0,
                               base=0, pattern=[[-1, P]], channel_multiplier=1).then_inc(made_pool, 1)
            pool.iota(iota_w[:, :], pattern=[[1, WN]], base=0, channel_multiplier=0,
                      allow_small_or_imprecise_dtypes=True).then_inc(made_pool, 1)
            pool.iota(iota_3w[:, :], pattern=[[SPLIT, WN]], base=0, channel_multiplier=0,
                      allow_small_or_imprecise_dtypes=True).then_inc(made_pool, 1)
            pool.iota(iota_p[:, :], pattern=[[0, 1]], base=0, channel_multiplier=1,
                      allow_small_or_imprecise_dtypes=True).then_inc(made_pool, 1)
            pool.iota(copy_row[:, :], pattern=[[0, T // COPIES], [NT, COPIES]], base=0,
                      channel_multiplier=0, allow_small_or_imprecise_dtypes=True).then_inc(made_pool, 1)
            pool.iota(spare_row[:, :], pattern=[[0, T]], base=NT - P, channel_multiplier=1,
                      allow_small_or_imprecise_dtypes=True).then_inc(made_pool, 1)
            pool.memset(acc[:, :], 0.0).then_inc(acc_zeroed, 1)
            pool.memset(den[:, :], 0.0).then_inc(acc_zeroed, 1)
            pool.memset(fT[:, :, :, :], 0.0).then_inc(fT_cleared, 1)

            pool.wait_ge(ext_ready, 2)
            pool.wait_ge(rel_checked, 3)
            pool.partition_all_reduce(ext_all[:, :], ext[:, :], P, RMAX).then_inc(ext_reduced, 1)

            for b in range(2):
                pool.wait_ge(a_out[b], done(NS, b))

            def gather(g, b, i):
                wait_apart(pool, idx_in[b], 16 * (i + 1), pool_passed)
                wait_apart(pool, msg_made, g - 1, pool_passed)
                for t in range(T):
                    pool.indirect_dma_start(
                        out=rows[:, b, t, :], out_offset=None, in_=wh_d[:, :],
                        in_offset=bass.IndirectOffsetOnAxis(ap=idx[:, b, t:t + 1].bitcast(U32), axis=0),
                        bounds_check=NT - 1, oob_is_err=False).then_inc(rows_got[b], 16)

            interleaved(pool, NG, [(0, gather)])

            def bias_b(s, b, i):
                wait_for(pool, b_x_in[b], 16 * (i + 1))
                wait_for(pool, b_t2, s - 1)
                pool.tensor_tensor(xbias[:, b, :, :], xb[:, b, :, :],
                                   bc[:, 1, :].unsqueeze(1).to_broadcast([P, K, D]), ALU.add
                                   ).then_inc(b_xbias, 1)

            def last_part_b(s, b, i):
                wait_for(pool, b_mid, s + 1)
                pool.tensor_tensor(h3[:, b, :, 2, :], hr[:, b, :, :], h3[:, b, :, 1, :], ALU.subtract
                                   ).then_inc(b_lo, 1)

            interleaved(pool, NS, [(1, bias_b), (0, last_part_b)])

            pool.wait_ge(agg_zeroed, 16 * COPIES)

            def scatter(g, b, i):
                wait_apart(pool, sidx_made, g + 1, pool_passed)
                wait_apart(pool, xo_made, 2 * (g + 1), pool_passed)
                for t in range(T):
                    wait_for(pool, added[t % COPIES], 16 * (g * (T // COPIES) + t // COPIES))
                    pool.sem_inc(earlier_added if t == COPIES - 1 else pool_passed, 1)
                    pool.indirect_dma_start(
                        out=agg_d[:, :],
                        out_offset=bass.IndirectOffsetOnAxis(ap=sidx[:, b, t:t + 1].bitcast(U32), axis=0),
                        in_=xo[:, b, t, :], in_offset=None, bounds_check=COPIES * NT - 1,
                        oob_is_err=False, compute_op=ALU.add).then_inc(added[t % COPIES], 16)

            interleaved(pool, NG, [(0, scatter)])

        @block.scalar
        def _(act):
            act.dma_start(edges[:, :, :], dst.rearrange("(p g e) -> p g e", g=2, e=GE)).then_inc(edges_in, 16)
            act.dma_start(first_dst[:, :], dst.rearrange("(g e) -> g e", e=GE)[:, 0:1].rearrange("g o -> o g"),
                          allow_slow_non_contiguous=True).then_inc(first_in, 16)
            act.dma_start(wf2_sb[:, :], W_f2).then_inc(weights_in, 16)
            act.dma_start(wo2_sb[:, :], W_o2).then_inc(weights_in, 16)
            act.dma_start(rows_in[:, 0, :], b_f2.rearrange("(a p) -> a p", a=1)).then_inc(weights_in, 16)
            act.dma_start(rows_in[:, 1, :], b_o2.rearrange("(a p) -> a p", a=1)).then_inc(weights_in, 16)
            act.dma_start(rows_in[:, 2, :], bias0.rearrange("(a p) -> a p", a=1)).then_inc(weights_in, 16)
            act.dma_start(win_sb[:, :], W_in).then_inc(weights_in, 16)
            act.dma_start(wo1_sb[:, :], W_o1).then_inc(weights_in, 16)
            act.dma_start(bf1_c[:, :], b_f1.rearrange("(p a) -> p a", a=1)).then_inc(weights_in, 16)
            act.dma_start(bo1_c[:, :], b_o1.rearrange("(p a) -> p a", a=1)).then_inc(weights_in, 16)
            act.wait_ge(padded_cleared, 2)
            for t in range(Q):
                act.dma_start(wf1_sb[RBF * t:RBF * t + RBF, t, :], W_f1).then_inc(weights_in, 16)
            act.wait_ge(w_turned, 1)
            act.copy(wT[:, :], bank[0][:, 0:D]).then_inc(wT_made, 1)
            act.wait_ge(rank_exp, 1)
            act.activation(rank_w[:, :], rank_cap[:, :], ACT.Exp).then_inc(rank_made, 1)
            act.wait_ge(edges16_made, 1)
            act.dma_start(dst16_d[:].rearrange("(p g e) -> p g e", g=2, e=GE), edges16[:, :, :]
                          ).then_inc(edges16_out, 16)
            act.wait_ge(rel_checked, 3)
            act.dma_start(edges[:, :, :], src.rearrange("(p g e) -> p g e", g=2, e=GE)).then_inc(edges_in, 16)

            def turn_a(s, b, i):
                wait_for(act, a_turned, s + 1)
                wait_for(act, a_v, 2 * (s - 1))
                act.copy(nT[:, b, :, :].rearrange("p k n -> p (k n)"), bank[b][:, :]).then_inc(a_xT, 1)

            interleaved(act, NS, [(0, turn_a)])
            act.wait_ge(edges16_made, 2)
            act.dma_start(src16_d[:].rearrange("(p g e) -> p g e", g=2, e=GE), edges16[:, :, :]
                          ).then_inc(edges16_out, 16)
            act.wait_ge(made_dve, 4)
            for c in range(COPIES):
                act.dma_start(agg_d[c * NT:(c + 1) * NT, :].rearrange("(p r) f -> p r f", p=P),
                              zeros[:, :].unsqueeze(1).to_broadcast([P, NB, D])).then_inc(agg_zeroed, 16)

            def weigh(g, b, i):
                wait_for(act, ls_made, g + 1)
                wait_for(act, summed, g - 1)
                act.activation(msg[:, b, :, D:ROW], ls[:, b, :, :], ACT.Exp).then_inc(wgt_made, 1)

            def window_out(g, b, i):
                wait_for(act, summed, g + 1)
                wait_for(act, win_turned, g - 1)
                act.copy(win[:, b, :], bank[2 + b][0:WN, 0:ROW]).then_inc(win_made, 1)

            interleaved(act, NG, [(1, weigh), (0, window_out)])

            def inverse_root(s, b, mv_sem, lnvar_sem, rstd_sem):
                wait_for(act, mv_sem, s + 1)
                act.activation(lnvar[:, b, :], mv[:, b, :, 1], ACT.Ln, bias=eps_c[:, 0:1]).then_inc(lnvar_sem, 1)
                wait_for(act, lnvar_sem, s + 1)
                act.activation(rstd[:, b, :], lnvar[:, b, :], ACT.Exp, scale=-0.5).then_inc(rstd_sem, 1)

            def sums_b(s, b, i):
                wait_for(act, b_turned, s - 1)
                wait_for(act, b_lo, s - 1)
                act.copy(accs[:, b, :, :], acc_k[:, four(s), :]).then_inc(b_accs, 1)
                act.copy(dens[:, b, :, :], den_k[:, four(s), :]).then_inc(b_accs, 1)

            def finish_b(s, b, i):
                inverse_root(s, b, b_mv, b_lnvar, b_rstd)
                wait_for(act, b_yturned, s + 1)
                wait_for(act, b_h, s - 1)
                act.copy(nT[:, b, :, :].rearrange("p k n -> p (k n)"), bank[4][:, :]).then_inc(b_yT, 1)
                wait_for(act, b_h, s + 1)
                wait_for(act, b_h_out[b], 16 * i)
                act.copy(h3[:, b, :, 0, :], bank[5][:, :].rearrange("p (k f) -> p k f", k=K)
                         ).then_inc(b_hi, 1)
                wait_for(act, b_hr, s + 1)
                act.copy(h3[:, b, :, 1, :], hr[:, b, :, :]).then_inc(b_mid, 1)

            act.wait_ge(attended, 1)
            interleaved(act, NS, [(1, sums_b), (0, finish_b)])

            def turn_1(g, b, i):
                wait_for(act, f_turned, g + 1)
                wait_for(act, v_made, 2 * (g - 1))
                act.copy(fT[0:Q * RBF, b, :, :], bank[0][0:Q * RBF, 0:2 * P]
                         .rearrange("r (q p) -> r q p", q=2)).then_inc(fT_made, 1)

            def expanded_h(g, b, i):
                wait_for(act, ccol_in[b], 16 * (i + 1))
                for q in range(2):
                    wait_for(act, hd_made, 2 * g + q + 1)
                    wait_for(act, xij_made, 2 * g + q - 1)
                    for t in range(Q):
                        ins = act.activation(hsb[:, q, t, :], bank[3 + 4 * q][:, t * D:(t + 1) * D],
                                             ACT.Copy, scale=ccol[:, b, q * Q + t:q * Q + t + 1])
                    ins.then_inc(hsb_made, 1)

            def softplus_1(g, b, i):
                for q in range(2):
                    wait_for(act, exc_made, 2 * g + q + 1)
                    wait_for(act, ln_made, 2 * g + q - 1)
                    act.activation(ex[:, q, :], exc[:, q, :], ACT.Exp).then_inc(ex_made, 1)
                for q in range(2):
                    wait_for(act, ex_made, 2 * g + q + 1)
                    wait_for(act, gact_made, 2 * g + q - 1)
                    act.activation(ln[:, q, :], ex[:, q, :], ACT.Ln, bias=1.0).then_inc(ln_made, 1)

            def messages_out(g, b, i):
                for q in range(2):
                    wait_for(act, presummed, 2 * g + q + 1)
                    if q == 0:
                        wait_for(act, earlier_added, g)
                    act.copy(xo[:, b, Q * q:Q * q + Q, :],
                             bank[6][:, :].rearrange("p (t f) -> p t f", t=Q)).then_inc(xo_made, 1)

            act.wait_ge(fT_cleared, 1)
            interleaved(act, NG, [(1, turn_1), (0, expanded_h), (1, softplus_1), (0, messages_out)])

            def inner_c(s, b, i):
                wait_for(act, c_turned, s + 1)
                wait_for(act, c_o, s - 1)
                act.copy(nT[:, b, :, :].rearrange("p k n -> p (k n)"), bank[b][:, :]).then_inc(c_agT, 1)
                wait_for(act, c_exc, s + 1)
                wait_for(act, c_ln, s - 1)
                act.activation(ex[:, b, :], exc[:, b, :], ACT.Exp).then_inc(c_ex, 1)
                wait_for(act, c_ex, s + 1)
                wait_for(act, c_g, s - 1)
                act.activation(ln[:, b, :], ex[:, b, :], ACT.Ln, bias=1.0).then_inc(c_ln, 1)

            def finish_c(s, b, i):
                inverse_root(s, b, c_mv, c_lnvar, c_rstd)

            interleaved(act, NS, [(1, inner_c), (0, finish_c)])

        @block.tensor
        def _(pe):
            pe.wait_ge(made_pool, 7)
            pe.wait_ge(w_in, 16 * 9)
            pe.transpose(bank[0][:, 0:D], w_sb[:, :], ident[:, :]).then_inc(w_turned, 1)
            pe.wait_ge(wT_made, 1)
            pe.matmul(bank[1][:, 0:2 * HEADS], wT[:, :], att_blk[:, :], start=True, stop=True
                      ).then_inc(watt_made, 1)
            pe.wait_ge(v_ready, 2)

            def project_a(s, b, i):
                wait_for(pe, a_x_in[b], 16 * (i + 1))
                wait_for(pe, a_xT, s - 1)
                for k in range(K):
                    mm = pe.transpose(bank[b][:, k * P:(k + 1) * P], xb[:, b, k, :], ident[:, :])
                mm.then_inc(a_turned, 1)
                wait_for(pe, a_xT, s + 1)
                wait_for(pe, a_row, 2 * (s - 1))
                for half in range(2):
                    for k in range(2):
                        mm = pe.matmul(bank[2 + 2 * b + half][:, k * COLS:(k + 1) * COLS],
                                       nT[:, b, 2 * half + k, :], v_sb[:, :], start=True, stop=True)
                    mm.then_inc(a_v, 1)

            interleaved(pe, NS, [(0, project_a)])

            pe.wait_ge(made_dve, 4)
            pe.wait_ge(weights_in, 16 * 13)
            pe.wait_ge(a_row, 2 * NS)
            pe.matmul(bank[2][0:1, 0:D], ones[:, 0:1], wf2_sb[:, :], start=True, stop=True)
            pe.matmul(bank[2][0:1, D:2 * D], ones[:, 0:1], wo2_sb[:, :], start=True, stop=True
                      ).then_inc(colsums_made, 1)
            pe.wait_ge(first_ready, 1)
            pe.matmul(bank[3][:, 0:NG], ones[0:1, :], first_f[0:1, :], start=True, stop=True
                      ).then_inc(base_spread, 1)
            pe.wait_ge(rows_ready, 3)
            pe.matmul(bank[4][:, 0:2 * D], ones[0:1, :], rows_eff[0:1, 1:3, :], start=True, stop=True
                      ).then_inc(bc_spread, 1)
            pe.wait_ge(split_made, 6)

            def expand_0(g, b, i):
                wait_for(pe, oneT_made, g + 1)
                wait_for(pe, adwin_in[b], 16 * (i + 1))
                wait_for(pe, z_made, 2 * (g - 1))
                for t in range(T):
                    mm = pe.matmul(bank[b][:, t * HEADS:(t + 1) * HEADS], oneT[:, b, t, :],
                                   adwin[:, b, :], start=True, stop=True)
                mm.then_inc(expanded, 1)

            def sum_0(g, b, i):
                wait_for(pe, one_made, g + 1)
                wait_for(pe, msg_made, g + 1)
                wait_for(pe, win_made, g - 1)
                for t in range(T):
                    mm = pe.matmul(bank[2 + b][0:WN, 0:ROW], one[:, b, t, :], msg[:, b, t, :],
                                   start=(t == 0), stop=(t == T - 1))
                mm.then_inc(summed, 1)
                wait_for(pe, win_made, g + 1)
                wait_apart(pe, acc_added, g - 1, pe_passed)
                pe.transpose(bank[4 + b][:, 0:WN], win[:, b, 0:D], ident[0:WN, 0:WN])
                pe.transpose(bank[4 + b][0:HEADS, P:P + WN], win[:, b, D:ROW], ident[0:WN, 0:WN]
                             ).then_inc(win_turned, 1)

            interleaved(pe, NG, [(1, expand_0), (0, sum_0)])

            def turn_b(s, b, i):
                wait_for(pe, b_accs, 2 * (s + 1))
                wait_for(pe, b_t1, s - 1)
                for k in range(K):
                    pe.transpose(bank[b][:, k * D:(k + 1) * D], accs[:, b, k, :], ident[:, :])
                for k in range(K):
                    mm = pe.transpose(bank[2 + b][:, k * HEADS:(k + 1) * HEADS], dens[:, b, k, :],
                                      ident[0:HEADS, 0:HEADS])
                mm.then_inc(b_turned, 1)

            def h_b(s, b, i):
                wait_for(pe, b_y, s + 1)
                wait_for(pe, b_yT, s)
                for k in range(K):
                    mm = pe.transpose(bank[4][:, k * P:(k + 1) * P], y1[:, b, k, :], ident[:, :])
                mm.then_inc(b_yturned, 1)
                wait_for(pe, b_yT, s + 1)
                wait_for(pe, b_hr, s)
                for k in range(K):
                    mm = pe.matmul(bank[5][:, k * D:(k + 1) * D], nT[:, b, k, :], win_sb[:, :],
                                   start=True, stop=True)
                mm.then_inc(b_h, 1)

            pe.wait_ge(attended, 1)
            interleaved(pe, NS, [(1, turn_b), (0, h_b)])
            pe.wait_ge(b_hr, NS)
            pe.wait_ge(split_in, 16)
            pe.wait_ge(rank_ready, 1)

            def turn_1(g, b, i):
                wait_for(pe, fin_in[b], 16 * (i + 1))
                wait_for(pe, fT_made, g)
                wait_for(pe, shift_made, g - 1)
                for q in range(2):
                    mm = pe.transpose(bank[0][0:Q * RBF, q * P:(q + 1) * P],
                                      fin[:, b, q * Q * RBF:(q + 1) * Q * RBF], ident[:, :])
                mm.then_inc(f_turned, 1)

            def expand_1(g, b, i):
                wait_for(pe, oneT1_made, g + 1)
                wait_for(pe, hwin_in[b], 16 * (i + 1))
                for q in range(2):
                    wait_for(pe, hsb_made, 2 * g + q - 1)
                    for t in range(Q):
                        mm = pe.matmul(bank[3 + 4 * q][:, t * D:(t + 1) * D], oneT[:, b, q * Q + t, :],
                                       hwin[:, b, :], start=True, stop=True)
                    mm.then_inc(hd_made, 1)

            def inner_1(g, b, i):
                wait_for(pe, fT_made, g + 1)
                for q in range(2):
                    wait_for(pe, gact_made, 2 * g + q - 1)
                    for t in range(Q):
                        mm = pe.matmul(bank[1 + q][:, t * P:(t + 1) * P], wf1_sb[:, t, :],
                                       fT[:, b, q, :], start=True, stop=True)
                    mm.then_inc(v_made, 1)

            def outer_1(g, b, i):
                for q in range(2):
                    wait_for(pe, gact_made, 2 * g + q + 1)
                    wait_for(pe, xij_made, 2 * g + q - 1)
                    pe.matmul(bank[4 + q][:, :], ones_bf[0:SPLIT, :],
                              bf2_3[:, :].unsqueeze(1).to_broadcast([SPLIT, Q, D]), start=True, stop=False)
                    for t in range(Q):
                        mm = pe.matmul(bank[4 + q][:, t * D:(t + 1) * D],
                                       gact[:, b, q, t * P:(t + 1) * P], wf2_sb[:, :],
                                       start=False, stop=(t == Q - 1))
                    mm.then_inc(wij_made, 1)

            def presum_1(g, b, i):
                wait_for(pe, eq_made, g + 1)
                wait_for(pe, shift_made, g)
                for t in range(T):
                    mm = pe.matmul(bank[0][:, 2 * P + t:2 * P + t + 1],
                                   eq[:, b, t, :].bitcast(BF16)[:, 1::2], rank_w[:, 0:1],
                                   start=True, stop=True)
                mm.then_inc(ranked, 1)
                for q in range(2):
                    wait_for(pe, xij_made, 2 * g + q + 1)
                    wait_for(pe, xo_made, 2 * g + q)
                    for t in range(Q):
                        mm = pe.matmul(bank[6][:, t * D:(t + 1) * D], eq[:, b, q * Q + t, :],
                                       xij[:, q, t * D:(t + 1) * D], start=True, stop=True)
                    mm.then_inc(presummed, 1)

            interleaved(pe, NG, [(1, turn_1), (0, expand_1), (1, inner_1), (0, outer_1), (0, presum_1)])
            pe.wait_ge(shift_made, NG)
            pe.wait_ge(xo_made, 2 * NG)

            def inner_c(s, b, i):
                wait_for(pe, c_ag, s + 1)
                wait_for(pe, c_agT, s - 1)
                for k in range(K):
                    mm = pe.transpose(bank[b][:, k * P:(k + 1) * P], ag[:, b, k, :], ident[:, :])
                mm.then_inc(c_turned, 1)
                wait_for(pe, c_agT, s + 1)
                wait_for(pe, c_g, s - 1)
                pe.matmul(bank[2 + b][:, :], wo1_sb[:, :], nT[:, b, :, :], start=True, stop=True
                          ).then_inc(c_o, 1)

            def outer_c(s, b, i):
                wait_for(pe, c_g, s + 1)
                wait_for(pe, c_t1, s - 1)
                for k in range(K):
                    mm = pe.matmul(bank[4 + b][:, k * D:(k + 1) * D], gact[:, b, 0, k * P:(k + 1) * P],
                                   wo2_sb[:, :], start=True, stop=True)
                mm.then_inc(c_y, 1)

            interleaved(pe, NS, [(1, inner_c), (0, outer_c)])

        @block.vector
        def _(dve):
            dve.memset(zeros[:, :], 0.0).then_inc(made_dve, 1)
            dve.memset(ones_bf[:, :], 1.0).then_inc(made_dve, 1)
            dve.memset(eps_c[:, :], EPS).then_inc(made_dve, 1)
            dve.memset(ones[:, :], 1.0).then_inc(made_dve, 1)
            dve.memset(ext[:, :], 0.0).then_inc(rel_checked, 1)
            dve.wait_ge(made_pool, 7)
            dve.tensor_scalar(rank_cap[:, :], iota_p[:, :], -LN2, 60 * LN2, ALU.mult, ALU.add
                              ).then_inc(rank_exp, 1)
            dve.wait_ge(w_in, 16 * 9)
            dve.tensor_copy(v_sb[:, 0:D], w_sb[:, :]).then_inc(v_ready, 1)
            dve.wait_ge(watt_made, 1)
            dve.tensor_copy(v_sb[:, D:COLS], bank[1][:, 0:2 * HEADS]).then_inc(v_ready, 1)
            dve.wait_ge(edges_in, 16)
            dve.tensor_copy(edges16[:, :, :], edges[:, :, :]).then_inc(edges16_made, 1)
            dve.tensor_copy(group_f[:, 0, :], edges[:, :, 0]).then_inc(group_made, 1)
            dve.tensor_reduce(group_f[:, 1, :], edges[:, :, :], AX.X, ALU.max).then_inc(group_made, 1)
            dve.tensor_reduce(group_f[:, 2, :], edges[:, :, :], AX.X, ALU.min).then_inc(group_made, 1)
            dve.wait_ge(group_made, 3)
            dve.tensor_tensor(group_f[:, 3, :], group_f[:, 1, :], group_f[:, 0, :], ALU.subtract
                              ).then_inc(group_made, 1)
            dve.tensor_tensor(group_f[:, 4, :], group_f[:, 0, :], group_f[:, 2, :], ALU.subtract
                              ).then_inc(group_made, 1)
            dve.wait_ge(group_made, 5)
            dve.wait_ge(rel_checked, 1)
            dve.tensor_reduce(ext[0:GP, 8:9], group_f[:, 3, :], AX.X, ALU.max).then_inc(rel_checked, 1)
            dve.tensor_reduce(ext[0:GP, 9:10], group_f[:, 4, :], AX.X, ALU.max).then_inc(rel_checked, 1)

            def row_a(s, b, i):
                wait_for(dve, a_out[b], 16 * i)
                for half in range(2):
                    wait_for(dve, a_v, 2 * s + half + 1)
                    both = bank[2 + 2 * b + half][:, 0:2 * COLS].rearrange("p (k c) -> p k c", k=2)
                    dve.tensor_copy(nS[:, b, 2 * half:2 * half + 2, 0:ROW], both[:, :, 0:ROW])
                    dve.tensor_copy(sd_all[:, bass.ds(s * K + 2 * half, 2), :], both[:, :, D:COLS]
                                    ).then_inc(a_row, 1)

            interleaved(dve, NS, [(0, row_a)])

            dve.wait_ge(a_row, 2 * NS)
            ad = sd_all[:, :, HEADS:2 * HEADS]
            dve.tensor_copy(ad3[:, :, 0, :], ad).then_inc(ad_split, 1)
            dve.wait_ge(ad_split, 1)
            dve.tensor_tensor(ad_rest[:, 0, :, :], ad, ad3[:, :, 0, :], ALU.subtract).then_inc(ad_split, 1)
            dve.wait_ge(ad_split, 2)
            dve.tensor_copy(ad3[:, :, 1, :], ad_rest[:, 0, :, :]).then_inc(ad_split, 1)
            dve.wait_ge(ad_split, 3)
            dve.tensor_tensor(ad_rest[:, 1, :, :], ad_rest[:, 0, :, :], ad3[:, :, 1, :], ALU.subtract
                              ).then_inc(ad_split, 1)
            dve.wait_ge(ad_split, 4)
            dve.tensor_copy(ad3[:, :, 2, :], ad_rest[:, 1, :, :]).then_inc(ad_split, 1)
            s_hn = sd_all[:, :, 0:HEADS].rearrange("p n h -> p h n")
            dve.wait_ge(rel_checked, 3)
            dve.tensor_reduce(ext[:, 0:HEADS], s_hn, AX.X, ALU.max).then_inc(ext_ready, 1)
            dve.tensor_reduce(ext[:, HEADS:2 * HEADS], s_hn, AX.X, ALU.min, negate=True).then_inc(ext_ready, 1)
            dve.tensor_scalar(below[:, :], iota_3w[:, :], iota_p[:, 0:1], None, ALU.is_le).then_inc(third_made, 1)
            dve.wait_ge(third_made, 1)
            dve.tensor_reduce(third[:, :], below[:, :], AX.X, ALU.add).then_inc(third_made, 1)
            dve.wait_ge(first_in, 16)
            dve.tensor_copy(first_f[:, :], first_dst[:, :]).then_inc(first_ready, 1)
            dve.tensor_scalar(first_row[:, :], first_dst[:, :], float(SPLIT), None, ALU.mult
                              ).then_inc(first_ready, 1)
            dve.wait_ge(third_made, 2)
            dve.wait_ge(base_spread, 1)
            dve.tensor_copy(base_bc[:, :], bank[3][:, 0:NG]).then_inc(bases_ready, 1)
            dve.tensor_scalar(node_id[:, :], bank[3][:, 0:NG], third[:, 0:1], -1.0, ALU.add, ALU.add
                              ).then_inc(bases_ready, 1)
            dve.wait_ge(bases_ready, 2)
            dve.wait_ge(colsums_made, 1)
            dve.scalar_tensor_tensor(out=rows_eff[0:1, 0, :], in0=bank[2][0:1, 0:D], scalar=-LN2,
                                     in1=rows_in[0:1, 0, :], op0=ALU.mult, op1=ALU.add).then_inc(rows_ready, 1)
            dve.scalar_tensor_tensor(out=rows_eff[0:1, 1, :], in0=bank[2][0:1, D:2 * D], scalar=-LN2,
                                     in1=rows_in[0:1, 1, :], op0=ALU.mult, op1=ALU.add).then_inc(rows_ready, 1)
            dve.tensor_copy(rows_eff[0:1, 2, :], rows_in[0:1, 2, :]).then_inc(rows_ready, 1)
            dve.wait_ge(rows_ready, 3)
            dve.tensor_copy(split_b[0:1, 0, :], rows_eff[0:1, 0, :]).then_inc(split_made, 1)
            dve.wait_ge(split_made, 1)
            dve.tensor_tensor(rest[0:1, 0, :], rows_eff[0:1, 0, :], split_b[0:1, 0, :], ALU.subtract
                              ).then_inc(split_made, 1)
            dve.wait_ge(split_made, 2)
            dve.tensor_copy(split_b[0:1, 1, :], rest[0:1, 0, :]).then_inc(split_made, 1)
            dve.wait_ge(split_made, 3)
            dve.tensor_tensor(rest[0:1, 1, :], rest[0:1, 0, :], split_b[0:1, 1, :], ALU.subtract
                              ).then_inc(split_made, 1)
            dve.wait_ge(split_made, 4)
            dve.tensor_copy(split_b[0:1, 2, :], rest[0:1, 1, :]).then_inc(split_made, 1)
            dve.wait_ge(bc_spread, 1)
            dve.tensor_copy(bc[:, :, :], bank[4][:, 0:2 * D].rearrange("p (r f) -> p r f", r=2)
                            ).then_inc(split_made, 1)
            dve.wait_ge(rank_made, 1)
            dve.tensor_scalar(rank_cap[:, :], rank_w[:, :], 2.5, None, ALU.mult).then_inc(rank_ready, 1)
            dve.wait_ge(edges_in, 32)
            dve.wait_ge(edges16_out, 16)
            dve.tensor_copy(edges16[:, :, :], edges[:, :, :]).then_inc(edges16_made, 1)
            dve.wait_ge(ext_reduced, 1)
            dve.wait_ge(acc_zeroed, 2)

            def weights_0(g, b, i):
                wait_for(dve, drow_in[b], 16 * (i + 1))
                wait_for(dve, expanded, g - 1)
                dve.tensor_scalar(oneT[:, b, :, :].rearrange("n t p -> n p t"),
                                  drow[:, b, :].rearrange("n (p t) -> n p t", t=T),
                                  node_id[0:W3, bass.ds(g, 1)], None, ALU.is_equal).then_inc(oneT_made, 1)
                wait_for(dve, dcol_in[b], 16 * (i + 1))
                dve.tensor_scalar(rel[:, b, :], dcol[:, b, :], base_bc[:, bass.ds(g, 1)], None, ALU.subtract
                                  ).then_inc(rel_made, 1)
                wait_for(dve, rel_made, g + 1)
                wait_for(dve, summed, g - 1)
                dve.tensor_tensor(one[:, b, :, :], iota_w[:, :].unsqueeze(1).to_broadcast([P, T, WN]),
                                  rel[:, b, :].unsqueeze(2).to_broadcast([P, T, WN]), ALU.is_equal
                                  ).then_inc(one_made, 1)
                wait_for(dve, rows_got[b], 16 * T * (i + 1))
                wait_for(dve, expanded, g + 1)
                ad_e = bank[b][:, 0:T * HEADS].rearrange("p (t h) -> p t h", h=HEADS)
                dve.tensor_tensor(z[:, b, :, 0:HEADS], rows[:, b, :, D:ROW], ad_e, ALU.add).then_inc(z_made, 1)
                dve.tensor_tensor(z[:, b, :, HEADS:2 * HEADS], ad_e,
                                  ext_all[:, 0:HEADS].unsqueeze(1).to_broadcast([P, T, HEADS]), ALU.add
                                  ).then_inc(z_made, 1)
                wait_for(dve, z_made, 2 * (g + 1))
                dve.scalar_tensor_tensor(out=lg[:, b, :, :], in0=z[:, b, :, :], scalar=SLOPE,
                                         in1=z[:, b, :, :], op0=ALU.mult, op1=ALU.max).then_inc(lg_made, 1)
                wait_for(dve, lg_made, g + 1)
                wait_for(dve, wgt_made, g - 1)
                dve.tensor_tensor(ls[:, b, :, :], lg[:, b, :, 0:HEADS], lg[:, b, :, HEADS:2 * HEADS],
                                  ALU.subtract).then_inc(ls_made, 1)
                wait_for(dve, wgt_made, g + 1)
                dve.tensor_tensor(msg[:, b, :, 0:D].rearrange("p t (h f) -> p t h f", h=HEADS),
                                  rows[:, b, :, 0:D].rearrange("p t (h f) -> p t h f", h=HEADS),
                                  msg[:, b, :, D:ROW].unsqueeze(3).to_broadcast([P, T, HEADS, F]), ALU.mult
                                  ).then_inc(msg_made, 1)

            def add_0(g, b, i):
                wait_for(dve, win_turned, g + 1)
                wait_for(dve, acc_added, g)
                base = dve.value_load(first_dst[0:1, bass.ds(g, 1)], min_val=0, max_val=NT - WN)
                dve.tensor_tensor(acc[:, bass.ds(base, WN)], acc[:, bass.ds(base, WN)],
                                  bank[4 + b][:, 0:WN], ALU.add)
                dve.tensor_tensor(den[:, bass.ds(base, WN)], den[:, bass.ds(base, WN)],
                                  bank[4 + b][0:HEADS, P:P + WN], ALU.add).then_inc(acc_added, 1)

            interleaved(dve, NG, [(1, weights_0), (0, add_0)])
            dve.wait_ge(acc_added, NG)
            dve.sem_inc(attended, 1)

            def moments(s, b, data, data_sem, count, stats_sem, mv_sem):
                wait_for(dve, data_sem, count)
                for k in range(K):
                    ins = dve.bn_stats(stats[:, b, k, :], data[:, b, k, :])
                ins.then_inc(stats_sem, 1)
                wait_apart(dve, stats_sem, s + 1, dve_passed)
                for k in range(K):
                    ins = dve.bn_aggr(mv[:, b, k, :], stats[:, b, k, :])
                ins.then_inc(mv_sem, 1)

            def normalize(s, b, data, rstd_sem, out_sem):
                wait_for(dve, rstd_sem, s + 1)
                for k in range(K):
                    ins = dve.tensor_scalar(y1[:, b, k, :], data[:, b, k, :], mv[:, b, k, 0:1],
                                            rstd[:, b, k:k + 1], ALU.subtract, ALU.mult)
                ins.then_inc(out_sem, 1)

            def mean_b(s, b, i):
                wait_for(dve, b_turned, s + 1)
                dve.tensor_scalar(clamped[:, b, :], bank[2 + b][:, 0:K * HEADS], 1e-37, None, ALU.max
                                  ).then_inc(b_clamped, 1)
                wait_for(dve, b_clamped, s + 1)
                dve.reciprocal(rec[:, b, :], clamped[:, b, :]).then_inc(b_rec, 1)
                wait_for(dve, b_rec, s + 1)
                dve.tensor_tensor(t1[:, b, :, :].rearrange("p k (h f) -> p (k h) f", h=HEADS),
                                  bank[b][:, :].rearrange("p (k h f) -> p (k h) f", k=K, h=HEADS),
                                  rec[:, b, :].unsqueeze(2).to_broadcast([P, K * HEADS, F]), ALU.mult
                                  ).then_inc(b_t1, 1)
                wait_for(dve, b_t1, s + 1)
                wait_for(dve, b_xbias, s + 1)
                dve.tensor_tensor(t2[:, b, :, :], t1[:, b, :, :], xbias[:, b, :, :], ALU.add).then_inc(b_t2, 1)
                moments(s, b, t2, b_t2, s + 1, b_stats, b_mv)

            def finish_b(s, b, i):
                wait_for(dve, b_y_out[b], 16 * i)
                wait_for(dve, b_yturned, s - 1)
                normalize(s, b, t2, b_rstd, b_y)

            def rest_b(s, b, i):
                wait_for(dve, b_hi, s + 1)
                dve.tensor_tensor(hr[:, b, :, :], bank[5][:, :].rearrange("p (k f) -> p k f", k=K),
                                  h3[:, b, :, 0, :], ALU.subtract).then_inc(b_hr, 1)

            dve.wait_ge(a_out[0], done(NS, 0))
            dve.wait_ge(a_out[1], done(NS, 1))
            interleaved(dve, NS, [(0, finish_b), (1, mean_b), (0, rest_b)])

            def equals_1(g, b, i):
                wait_for(dve, srow_in[b], 16 * (i + 1))
                wait_for(dve, scol_in[b], 16 * (i + 1))
                wait_for(dve, presummed, 2 * (g - 1))
                dve.tensor_tensor(eq[:, b, :, :], srow[:, b, :].rearrange("k (p t) -> k t p", t=T),
                                  scol[:, b, :].unsqueeze(2).to_broadcast([P, T, P]), ALU.is_equal
                                  ).then_inc(eq_made, 1)
                wait_for(dve, drow1_in[b], 16 * (i + 1))
                wait_for(dve, hd_made, 2 * (g - 1))
                dve.tensor_scalar(oneT[:, b, :, :].rearrange("n t p -> n p t"),
                                  drow[:, b, :].rearrange("n (p t) -> n p t", t=T),
                                  node_id[0:W3, bass.ds(g, 1)], None, ALU.is_equal).then_inc(oneT1_made, 1)
                wait_for(dve, sidx_made, g - 1)
                dve.tensor_tensor(home[:, b, :], scol[:, b, :], copy_row[:, :], ALU.add).then_inc(home_made, 1)
                dve.tensor_tensor(away[:, b, :], spare_row[:, :], scol[:, b, :], ALU.subtract
                                  ).then_inc(away_made, 1)

            def clamp_1(g, b, i):
                for q in range(2):
                    wait_for(dve, v_made, 2 * g + q + 1)
                    wait_for(dve, ex_made, 2 * g + q - 1)
                    dve.tensor_scalar(exc[:, q, :], bank[1 + q][:, :], bf1_c[:, 0:1], V_CAP, ALU.add,
                                      ALU.min).then_inc(exc_made, 1)

            def softplus_1(g, b, i):
                for q in range(2):
                    wait_for(dve, ln_made, 2 * g + q + 1)
                    if q == 0:
                        wait_for(dve, wij_made, 2 * (g - 1))
                    dve.scalar_tensor_tensor(out=gact[:, b, q, :], in0=bank[1 + q][:, :],
                                             scalar=bf1_c[:, 0:1], in1=ln[:, q, :], op0=ALU.add,
                                             op1=ALU.max).then_inc(gact_made, 1)

            def messages_1(g, b, i):
                for q in range(2):
                    wait_for(dve, hsb_made, 2 * g + q + 1)
                    wait_for(dve, wij_made, 2 * g + q + 1)
                    wait_for(dve, presummed, 2 * g + q - 1)
                    dve.tensor_tensor(xij[:, q, :], bank[4 + q][:, :],
                                      hsb[:, q, :, :].rearrange("p t f -> p (t f)"), ALU.mult
                                      ).then_inc(xij_made, 1)

            def targets_1(g, b, i):
                wait_for(dve, ranked, g + 1)
                wait_for(dve, away_made, g + 1)
                dve.scalar_tensor_tensor(out=shift[:, b, :], in0=bank[0][:, 2 * P:2 * P + T],
                                         scalar=rank_cap[:, 0:1], in1=away[:, b, :], op0=ALU.is_gt,
                                         op1=ALU.mult).then_inc(shift_made, 1)
                wait_for(dve, shift_made, g + 1)
                wait_for(dve, earlier_added, g)
                dve.tensor_tensor(sidx[:, b, :], shift[:, b, :], home[:, b, :], ALU.add).then_inc(sidx_made, 1)

            interleaved(dve, NG, [(1, clamp_1), (0, messages_1), (1, softplus_1), (0, targets_1),
                                  (2, equals_1)])

            def total_c(s, b, i):
                wait_for(dve, c_agg_in[b], 16 * COPIES * (i + 1))
                wait_for(dve, c_turned, s - 1)
                dve.tensor_reduce(ag[:, b, :, :], agg4[:, b, :, :, :].rearrange("p c k f -> p k f c"),
                                  AX.X, ALU.add).then_inc(c_ag, 1)

            def softplus_c(s, b, i):
                wait_for(dve, c_o, s + 1)
                wait_for(dve, c_ex, s - 1)
                dve.tensor_scalar(exc[:, b, :], bank[2 + b][:, :], bo1_c[:, 0:1], V_CAP, ALU.add,
                                  ALU.min).then_inc(c_exc, 1)
                wait_for(dve, c_ln, s + 1)
                wait_for(dve, c_y, s - 1)
                dve.scalar_tensor_tensor(out=gact[:, b, 0, :], in0=bank[2 + b][:, :],
                                         scalar=bo1_c[:, 0:1], in1=ln[:, b, :], op0=ALU.add,
                                         op1=ALU.max).then_inc(c_g, 1)

            def residual_c(s, b, i):
                wait_for(dve, c_y, s + 1)
                dve.tensor_tensor(t1[:, b, :, :], bank[4 + b][:, :].rearrange("p (k f) -> p k f", k=K),
                                  bc[:, 0, :].unsqueeze(1).to_broadcast([P, K, D]), ALU.add).then_inc(c_t1, 1)
                wait_for(dve, c_t1, s + 1)
                wait_for(dve, c_x_in[b], 16 * (i + 1))
                dve.tensor_tensor(t2[:, b, :, :], t1[:, b, :, :], xb[:, b, :, :], ALU.add).then_inc(c_t2, 1)
                moments(s, b, t2, c_t2, s + 1, c_stats, c_mv)
                wait_for(dve, c_out[b], 16 * i)
                normalize(s, b, t2, c_rstd, c_fin)

            interleaved(dve, NS, [(2, total_c), (1, softplus_c), (0, residual_c)])


def kernel(**inputs):
    import numpy as np
    import concourse.bacc as bacc
    from concourse.bass_utils import run_bass_kernel_spmd

    def padded(a, rows, fill=0):
        a = np.asarray(a)
        return np.concatenate([a, np.full((rows - a.shape[0],) + a.shape[1:], fill, a.dtype)])

    arrays = {
        "x": padded(inputs["x"], NT),
        "src": padded(inputs["src"], EP, N),
        "dst": padded(inputs["dst"], EP, N),
        "f_ij": padded(np.asarray(inputs["edge_attr3_1x20"]).reshape(E, RBF), EP),
        "cut": padded(np.asarray(inputs["edge_weight1"]).reshape(E), EP),
        "W": inputs["L0_gnn_W"], "att": inputs["L0_gnn_att"], "bias0": inputs["L0_gnn_bias"],
        "W_in": inputs["L1_gnn_W_in"], "W_f1": inputs["L1_gnn_W_f1"], "b_f1": inputs["L1_gnn_b_f1"],
        "W_f2": inputs["L1_gnn_W_f2"], "b_f2": inputs["L1_gnn_b_f2"],
        "W_o1": inputs["L1_gnn_W_o1"], "b_o1": inputs["L1_gnn_b_o1"],
        "W_o2": inputs["L1_gnn_W_o2"], "b_o2": inputs["L1_gnn_b_o2"],
    }
    arrays = {f"in_{k}": np.ascontiguousarray(v) for k, v in arrays.items()}
    nc = bacc.Bacc("TRN2", target_bir_lowering=False, num_devices=1)
    args = [nc.dram_tensor(k, a.shape, mybir.dt.from_np(a.dtype), kind="ExternalInput").ap()
            for k, a in arrays.items()]
    out = nc.dram_tensor("out", (NT, D), F32, kind="ExternalOutput").ap()
    gnn_kernel(nc, *args, out)
    r = run_bass_kernel_spmd(nc, [arrays], core_ids=[0])
    return r.results[0]["out"][:N]
```

```python
import concourse.bass as bass
from concourse import mybir
from contextlib import ExitStack

P = 128
D = 128
HEADS = 4
F = D // HEADS
RBF = 20
N = 6250
E = 200000
STEPS0 = (16, 10)
STEPS1 = 11
T = 8
GE = P * T
NG = -(-E // (2 * GE)) * 2
TILES = NG * T
EP = NG * GE
GP = NG // 2
K = 4
NS = -(-(N + P + 1) // (K * P))
NB = K * NS
NT = NB * P
SPLIT = 3
WN = P // SPLIT
W3 = SPLIT * WN
Q = 4
COPIES = 4
ZR = -(-COPIES * NT // NG)
ROW = D + HEADS
COLS = D + 2 * HEADS
SLOPE = 0.2
EPS = 1e-5
LN2 = 0.6931471805599453
SPREAD_MAX = 60.0
LOWEST = -3.0e38
V_CAP = 40.0

ALU = mybir.AluOpType
ACT = mybir.ActivationFunctionType
AX = mybir.AxisListType
F32 = mybir.dt.float32
I32 = mybir.dt.int32
I16 = mybir.dt.int16
U32 = mybir.dt.uint32
BF16 = mybir.dt.bfloat16
RMAX = bass.bass_isa.ReduceOp.max


def wait_for(eng, sem, count):
    if isinstance(count, int) and count <= 0:
        return
    eng.wait_ge(sem, count)


def wait_apart(eng, sem, count, passed):
    if isinstance(count, int) and count <= 0:
        return
    eng.wait_ge(sem, count)
    eng.sem_inc(passed, 1)


def interleaved(eng, total, parts):
    lead = max(ahead for ahead, _ in parts)

    def step(g, b, i):
        for ahead, stage in parts:
            if isinstance(g, int) and not 0 <= g + ahead < total:
                continue
            pair = i + (b + ahead) // 2 if (b + ahead) // 2 else i
            stage(g + ahead if ahead else g, (b + ahead) % 2, pair)

    for g in range(-lead, 2):
        step(g, g % 2, g // 2)
    whole = (total - lead) // 2
    with eng.Fori(1, whole) as i:
        for b in range(2):
            step(i * 2 + b if b else i * 2, b, i)
    for g in range(2 * whole, total):
        step(g, g % 2, g // 2)


def each(eng, total, body):
    body(0)
    with eng.Fori(1, total) as j:
        body(j)


def done(total, b):
    return 16 * ((total - b + 1) // 2)


def gnn_kernel(nc, x, src, dst, f_ij, cut, W, att, bias0, W_in, W_f1, b_f1, W_f2, b_f2,
               W_o1, b_o1, W_o2, b_o2, out):
    with ExitStack() as ctx:
        def sb(name, shape, dt=F32):
            return ctx.enter_context(nc.sbuf_tensor(name, shape, dt))

        def sem(name):
            return ctx.enter_context(nc.semaphore(name))

        src16_d = nc.dram_tensor("src16_d", [EP], I16)
        dst16_d = nc.dram_tensor("dst16_d", [EP], I16)
        wh_d = nc.dram_tensor("wh_d", [NT, ROW], F32)
        ad3_d = nc.dram_tensor("ad3_d", [SPLIT * NT, HEADS], BF16)
        h3_d = nc.dram_tensor("h3_d", [SPLIT * NT, D], BF16)
        x1_d = nc.dram_tensor("x1_d", [NT, D], F32)
        agg_d = nc.dram_tensor("agg_d", [NG * ZR, D], F32)

        ad_d = nc.dram_tensor("ad_d", [NT, HEADS], F32)
        max_d = nc.dram_tensor("max_d", [NT, HEADS], F32)
        sum_d = nc.dram_tensor("sum_d", [NT, ROW], F32)

        bank = [ctx.enter_context(nc.psum_tensor(f"bank{i}", [P, 512], F32)) for i in range(8)]

        ident = sb("ident", [P, P])
        ones = sb("ones", [P, P])
        ones_bf = sb("ones_bf", [P, P], BF16)
        iota_w = sb("iota_w", [P, WN])
        iota_3w = sb("iota_3w", [P, WN])
        below = sb("below", [P, WN])
        third = sb("third", [P, 1])
        iota_p = sb("iota_p", [P, 1])
        copy_row = sb("copy_row", [P, T])
        spare_row = sb("spare_row", [P, T])
        rank_w = sb("rank_w", [P, 1], BF16)
        rank_cap = sb("rank_cap", [P, 1])
        zeros = sb("zeros", [P, max(D, ZR * D // P)])
        w_sb = sb("w_sb", [P, D])
        wT = sb("wT", [P, D])
        att_blk = sb("att_blk", [P, 2 * HEADS])
        v_sb = sb("v_sb", [P, COLS])
        win_sb = sb("win_sb", [P, D])
        wf1_sb = sb("wf1_sb", [P, Q, D])
        wf2_sb = sb("wf2_sb", [P, D])
        wo1_sb = sb("wo1_sb", [P, D])
        wo2_sb = sb("wo2_sb", [P, D])
        bf1_c = sb("bf1_c", [P, 1])
        bo1_c = sb("bo1_c", [P, 1])
        rows_in = sb("rows_in", [1, 3, D])
        rows_eff = sb("rows_eff", [1, 3, D])
        rest = sb("rest", [1, 2, D])
        split_b = sb("split_b", [1, SPLIT, D], BF16)
        bf2_3 = sb("bf2_3", [SPLIT, D], BF16)
        bc = sb("bc", [P, 2, D])
        first_dst = sb("first_dst", [1, NG], I32)
        first_f = sb("first_f", [1, NG])
        first_row = sb("first_row", [1, NG], I32)
        base_bc = sb("base_bc", [P, NG])
        node_id = sb("node_id", [P, NG])
        edges = sb("edges", [GP, 2, GE], I32)
        edges16 = sb("edges16", [GP, 2, GE], I16)
        group_f = sb("group_f", [GP, 5, 2])
        sd_all = sb("sd_all", [P, NB, 2 * HEADS])
        ad_rest = sb("ad_rest", [P, 2, NB, HEADS])
        ad3 = sb("ad3", [P, NB, SPLIT, HEADS], BF16)
        ext = sb("ext", [P, 2 * HEADS + 2])
        ext_all = sb("ext_all", [P, 2 * HEADS + 2])
        eps_c = sb("eps_c", [P, 1])
        acc = sb("acc", [P, NT])
        den = sb("den", [HEADS, NT])
        idx = sb("idx", [P, 2, T], I32)
        dcol = sb("dcol", [P, 2, T], I32)
        drow = sb("drow", [W3, 2, GE], I16)
        adwin = sb("adwin", [W3, 2, HEADS], BF16)
        rows = sb("rows", [P, 2, T, ROW])
        oneT = sb("oneT", [W3, 2, T, P], BF16)
        rel = sb("rel", [P, 2, T])
        one = sb("one", [P, 2, T, WN])
        z = sb("z", [P, 2, T, 2 * HEADS])
        lg = sb("lg", [P, 2, T, 2 * HEADS])
        ls = sb("ls", [P, 2, T, HEADS])
        msg = sb("msg", [P, 2, T, ROW])
        win = sb("win", [WN, 2, ROW])
        gact = sb("gact", [P, 2, 2, 512])
        ex_x1 = sb("ex_x1", [P, 2, 512])
        xb = sb("xb", [P, 2, K, D])
        nT = sb("nT", [P, 2, K, P])
        nS = sb("nS", [P, 2, K, COLS])
        accs = sb("accs", [P, 2, K, P])
        dens = sb("dens", [HEADS, 2, K, P])
        clamped = sb("clamped", [P, 2, K * HEADS])
        rec = sb("rec", [P, 2, K * HEADS])
        xbias = sb("xbias", [P, 2, K, D])
        t1 = sb("t1", [P, 2, K, D])
        stats = sb("stats", [P, 2, K, 6])
        mv = sb("mv", [P, 2, K, 2])
        lnvar = sb("lnvar", [P, 2, K])
        rstd = sb("rstd", [P, 2, K])
        newton = sb("newton", [P, 2, 3, K])
        y1 = sb("y1", [P, 2, K, D])
        x1b = ex_x1[:, :, :].rearrange("p b (k f) -> p b k f", k=K)
        h3 = sb("h3", [P, 2, K, SPLIT, D], BF16)
        hr = gact[:, :, 0, :].rearrange("p b (k f) -> p b k f", k=K)
        fin = sb("fin", [P, 2, T * RBF])
        srow = sb("srow", [P, 2, GE], I16)
        scol = sb("scol", [P, 2, T], I32)
        ccol = sb("ccol", [P, 2, T])
        hwin = sb("hwin", [W3, 2, D], BF16)
        fT = sb("fT", [P, 2, 2, P])
        exc = sb("exc", [P, 2, 512])
        ex = ex_x1
        ln = sb("ln", [P, 2, 512])
        eq = sb("eq", [P, 2, T, P])
        hsb = sb("hsb", [P, 2, Q, D])
        xij = sb("xij", [P, 2, Q * D])
        away = sb("away", [P, 2, T])
        home = sb("home", [P, 2, T])
        shift = sb("shift", [P, 2, T])
        sidx = sb("sidx", [P, 2, T], I32)
        xo = msg[:, :, :, 0:D]
        agg4 = acc[:, 0:2 * COPIES * K * D].rearrange("p (b c k f) -> p b c k f", b=2, c=COPIES, k=K)
        ag = xbias
        pair = eq[:, :, :, :].rearrange("p b (q k) f -> p b q k f", q=2)
        t2 = nS[:, :, :, 0:D]

        spread = sb("spread", [1, HEADS])
        tests = sb("tests", [1, 4])
        mode = sb("mode", [1, 2], I32)
        lowest = ad_rest[:, 0, :, :]
        ad_e = sb("ad_e", [P, HEADS])
        max_e = sb("max_e", [P, HEADS])
        tile_max = sb("tile_max", [P, HEADS])
        new_max = sb("new_max", [P, HEADS])
        penalty = sb("penalty", [P, P])
        h_e = sb("h_e", [P, SPLIT * D], BF16)
        h_sum = sb("h_sum", [P, 2, D])
        scaled = sb("scaled", [P, D])

        mode_steps = sem("mode_steps")
        mode_ready = sem("mode_ready")
        u_lowest = sem("u_lowest")
        u_tables = sem("u_tables")
        u_cols_in = [sem(f"u_cols_in{turn}") for turn in range(2)]
        u_row_in = sem("u_row_in")
        u_rows_got = sem("u_rows_got")
        u_nodes_got = [sem(f"u_nodes_got{turn}") for turn in range(2)]
        u_dve = sem("u_dve")
        u_pe = sem("u_pe")
        u_act = sem("u_act")
        u_added = sem("u_added")
        u_sums_in = sem("u_sums_in")
        u_sums_turned = sem("u_sums_turned")
        u_sums_kept = sem("u_sums_kept")
        w_cols_in = sem("w_cols_in")
        w_edge_in = sem("w_edge_in")
        w_row_in = sem("w_row_in")
        w_gathered = sem("w_gathered")
        w_dve = sem("w_dve")
        w_pe = sem("w_pe")
        w_act = sem("w_act")
        w_added = sem("w_added")
        made_pool = sem("made_pool")
        made_dve = sem("made_dve")
        padded_cleared = sem("padded_cleared")
        w_in = sem("w_in")
        weights_in = sem("weights_in")
        first_in = sem("first_in")
        edges_in = sem("edges_in")
        edges16_made = sem("edges16_made")
        edges16_out = sem("edges16_out")
        agg_zeroed = sem("agg_zeroed")
        w_turned = sem("w_turned")
        wT_made = sem("wT_made")
        v_ready = sem("v_ready")
        colsums_made = sem("colsums_made")
        rows_ready = sem("rows_ready")
        bc_spread = sem("bc_spread")
        first_ready = sem("first_ready")
        base_spread = sem("base_spread")
        bases_ready = sem("bases_ready")
        split_made = sem("split_made")
        rank_exp = sem("rank_exp")
        rank_made = sem("rank_made")
        rank_ready = sem("rank_ready")
        rel_checked = sem("rel_checked")
        group_made = sem("group_made")
        buffers_cleared = sem("buffers_cleared")
        ext_ready = sem("ext_ready")
        ext_reduced = sem("ext_reduced")
        ad_split = sem("ad_split")
        ad_out = sem("ad_out")
        passed = sem("passed")
        a_x_in = [sem(f"a_x_in{b}") for b in range(2)]
        a_turned = sem("a_turned")
        a_xT = sem("a_xT")
        a_v = sem("a_v")
        a_row = sem("a_row")
        a_out = [sem(f"a_out{b}") for b in range(2)]
        group0_in = [sem(f"group0_in{b}") for b in range(2)]
        rows_got = [sem(f"rows_got{b}") for b in range(2)]
        oneT_made = sem("oneT_made")
        rel_made = sem("rel_made")
        one_made = sem("one_made")
        expanded = sem("expanded")
        z_made = sem("z_made")
        lg_made = sem("lg_made")
        ls_made = sem("ls_made")
        wgt_made = sem("wgt_made")
        msg_made = sem("msg_made")
        summed = sem("summed")
        win_made = sem("win_made")
        win_turned = sem("win_turned")
        acc_added = sem("acc_added")
        attended = sem("attended")
        b_x_in = [sem(f"b_x_in{b}") for b in range(2)]
        b_accs = sem("b_accs")
        b_turned = sem("b_turned")
        b_clamped = sem("b_clamped")
        b_rec = sem("b_rec")
        b_t1 = sem("b_t1")
        b_xbias = sem("b_xbias")
        b_t2 = sem("b_t2")
        n_stats = sem("n_stats")
        n_mv = sem("n_mv")
        n_rstd = sem("n_rstd")
        n_newton = sem("n_newton")
        b_y = sem("b_y")
        b_yturned = sem("b_yturned")
        b_yT = sem("b_yT")
        b_h = sem("b_h")
        b_hi = sem("b_hi")
        b_hr = sem("b_hr")
        b_mid = sem("b_mid")
        b_lo = sem("b_lo")
        b_x1b = sem("b_x1b")
        b_y_out = [sem(f"b_y_out{b}") for b in range(2)]
        b_h_out = [sem(f"b_h_out{b}") for b in range(2)]
        fin_in = [sem(f"fin_in{b}") for b in range(2)]
        group1_in = [sem(f"group1_in{b}") for b in range(2)]
        hwin_in = [sem(f"hwin_in{b}") for b in range(2)]
        f_turned = sem("f_turned")
        fT_made = sem("fT_made")
        v_made = sem("v_made")
        exc_made = sem("exc_made")
        ex_made = sem("ex_made")
        ln_made = sem("ln_made")
        gact_made = sem("gact_made")
        eq_made = sem("eq_made")
        oneT1_made = sem("oneT1_made")
        hd_made = sem("hd_made")
        hsb_made = sem("hsb_made")
        wij_made = sem("wij_made")
        xij_made = sem("xij_made")
        ranked = sem("ranked")
        away_made = sem("away_made")
        home_made = sem("home_made")
        shift_made = sem("shift_made")
        sidx_made = sem("sidx_made")
        presummed = sem("presummed")
        xo_made = sem("xo_made")
        earlier_added = sem("earlier_added")
        added = [sem(f"added{c}") for c in range(COPIES)]
        c_agg_in = [sem(f"c_agg_in{b}") for b in range(2)]
        c_x_in = [sem(f"c_x_in{b}") for b in range(2)]
        c_pairs = sem("c_pairs")
        c_ag = sem("c_ag")
        c_turned = sem("c_turned")
        c_agT = sem("c_agT")
        c_o = sem("c_o")
        c_exc = sem("c_exc")
        c_ex = sem("c_ex")
        c_ln = sem("c_ln")
        c_g = sem("c_g")
        c_y = sem("c_y")
        c_t2 = sem("c_t2")
        c_fin = sem("c_fin")
        c_out = [sem(f"c_out{b}") for b in range(2)]

        src_g = src.rearrange("(g p t) -> g p t", p=P, t=T)
        dst_g = dst.rearrange("(g p t) -> g p t", p=P, t=T)
        cut_g = cut.rearrange("(g p t) -> g p t", p=P, t=T)
        f_g = f_ij.rearrange("(g p t) r -> g p (t r)", p=P, t=T)
        src16_g = src16_d[:].rearrange("(g e) -> g e", e=GE)
        dst16_g = dst16_d[:].rearrange("(g e) -> g e", e=GE)
        x_k = x.rearrange("(p k) f -> p k f", k=NB)
        out_k = out.rearrange("(p k) f -> p k f", k=NB)
        wh_k = wh_d[:, :].rearrange("(p k) f -> p k f", k=NB)
        x1_k = x1_d[:, :].rearrange("(p k) f -> p k f", k=NB)
        h3_k = h3_d[:, :].rearrange("(p k c) f -> p k c f", k=NB, c=SPLIT)
        agg_k = agg_d[0:COPIES * NT, :].rearrange("(c p k) f -> c p k f", c=COPIES, k=NB)
        agg_z = agg_d[:, :].rearrange("(g r) f -> g (r f)", g=NG).rearrange("g (p e) -> g p e", p=P)
        acc_k = acc[:, :].rearrange("f (p k) -> f k p", k=NB)
        den_k = den[:, :].rearrange("h (p k) -> h k p", k=NB)

        src_t = src.rearrange("(j p o) -> j p o", p=P, o=1)
        dst_t = dst.rearrange("(j p o) -> j p o", p=P, o=1)
        cut_t = cut.rearrange("(j p o) -> j p o", p=P, o=1)
        f_t = f_ij.rearrange("(j p) r -> j p r", p=P)
        src16_t = src16_d[:].rearrange("(j e) -> j e", e=P)
        dst16_t = dst16_d[:].rearrange("(j e) -> j e", e=P)
        h_rows = h3_d[:, :].rearrange("(n c) f -> n (c f)", c=SPLIT)
        sum_k = sum_d[:, :].rearrange("(p k) c -> p k c", k=NB)

        def four(s):
            return bass.ds(s * K, K)

        block = ctx.enter_context(nc.Block())

        @block.sync
        def _(sp):
            def load_a(s, b, i):
                wait_apart(sp, a_turned, s - 1, passed)
                sp.dma_start(xb[:, b, :, :], x_k[:, four(s), :]).then_inc(a_x_in[b], 16)

            def store_a(s, b, i):
                wait_apart(sp, a_row, 2 * (s + 1), passed)
                sp.dma_start(wh_k[:, four(s), :], nS[:, b, :, 0:ROW]).then_inc(a_out[b], 16)

            interleaved(sp, NS, [(3, load_a), (0, store_a)])
            sp.wait_ge(ad_split, 5)
            sp.dma_start(ad3_d[:, :].rearrange("(p k c) h -> p (k c h)", k=NB, c=SPLIT),
                         ad3[:, :, :, :].rearrange("p k c h -> p (k c h)")).then_inc(ad_out, 16)

            sp.wait_ge(edges16_out, 16)
            sp.wait_ge(first_ready, 2)

            def clear_agg(g):
                sp.dma_start(agg_z[bass.ds(g, 1), :, :].rearrange("o p e -> p (o e)"), zeros[:, 0:ZR * D // P]
                             ).then_inc(agg_zeroed, 16)

            sp.wait_ge(mode_ready, 1)
            fast = sp.value_load(mode[0:1, 0:1], min_val=0, max_val=1)
            with sp.If(fast > 0):
                def load_group0(g, b, i):
                    wait_apart(sp, z_made, 2 * (g - 1), passed)
                    sp.dma_start(idx[:, b, :], src_g[bass.ds(g, 1), :, :].rearrange("o p t -> p (o t)")
                                 ).then_inc(group0_in[b], 16)
                    wait_apart(sp, rel_made, g - 1, passed)
                    sp.dma_start(dcol[:, b, :], dst_g[bass.ds(g, 1), :, :].rearrange("o p t -> p (o t)")
                                 ).then_inc(group0_in[b], 16)
                    wait_apart(sp, oneT_made, g - 1, passed)
                    sp.dma_start(drow[:, b, :], dst16_g[bass.ds(g, 1), :].to_broadcast([W3, GE])
                                 ).then_inc(group0_in[b], 16)
                    if isinstance(g, int) and g == 0:
                        sp.wait_ge(ad_out, 16)
                    wait_apart(sp, expanded, g - 1, passed)
                    row = sp.value_load(first_row[0:1, bass.ds(g, 1)], min_val=0, max_val=SPLIT * (NT - WN))
                    sp.dma_start(adwin[:, b, :], ad3_d[bass.ds(row, W3), :]).then_inc(group0_in[b], 16)
                    clear_agg(g)

                interleaved(sp, NG, [(0, load_group0)])
                sp.wait_ge(oneT_made, NG)
            with sp.Else():
                sp.dma_start(ad_d[:, :].rearrange("(p k) h -> p k h", k=NB), sd_all[:, :, HEADS:2 * HEADS]
                             ).then_inc(u_tables, 16)
                each(sp, NG, clear_agg)
                sp.dma_start(sum_k[:, :, 0:D], zeros[:, 0:D].unsqueeze(1).to_broadcast([P, NB, D])
                             ).then_inc(u_tables, 16)
                sp.dma_start(sum_k[:, :, D:ROW], zeros[:, 0:HEADS].unsqueeze(1).to_broadcast([P, NB, HEADS])
                             ).then_inc(u_tables, 16)
                sp.wait_ge(u_lowest, 1)
                sp.dma_start(max_d[:, :].rearrange("(p k) h -> p k h", k=NB), lowest).then_inc(u_tables, 16)
                for turn in range(2):
                    def load_tile0(j):
                        wait_apart(sp, u_added, 16 * (turn * TILES + j), passed)
                        sp.dma_start(idx[:, 0, 0:1], src_t[bass.ds(j, 1), :, :].rearrange("a p o -> p (a o)")
                                     ).then_inc(u_cols_in[turn], 16)
                        sp.dma_start(dcol[:, 0, 0:1], dst_t[bass.ds(j, 1), :, :].rearrange("a p o -> p (a o)")
                                     ).then_inc(u_cols_in[turn], 16)
                        sp.dma_start(srow[:, 0, 0:P], dst16_t[bass.ds(j, 1), :].to_broadcast([P, P])
                                     ).then_inc(u_row_in, 16)

                    each(sp, TILES, load_tile0)
                sp.wait_ge(u_added, 16 * 2 * TILES)

                def load_sums(k):
                    wait_apart(sp, u_sums_turned, k, passed)
                    sp.dma_start(msg[:, 0, 0, :], sum_k[:, bass.ds(k, 1), :].rearrange("p o c -> p (o c)")
                                 ).then_inc(u_sums_in, 16)

                each(sp, NB, load_sums)

            sp.wait_ge(split_made, 5)
            sp.dma_start(bf2_3[:, :], split_b[0:1, :, :]).then_inc(weights_in, 16)

            def load_b(s, b, i):
                wait_apart(sp, b_xbias, s - 1, passed)
                sp.dma_start(xb[:, b, :, :], x_k[:, four(s), :]).then_inc(b_x_in[b], 16)

            def store_b(s, b, i):
                wait_apart(sp, b_x1b, s + 1, passed)
                sp.dma_start(x1_k[:, four(s), :], x1b[:, b, :, :]).then_inc(b_y_out[b], 16)
                wait_apart(sp, b_lo, s + 1, passed)
                sp.dma_start(h3_k[:, four(s), :, :], h3[:, b, :, :, :]).then_inc(b_h_out[b], 16)

            sp.wait_ge(a_turned, NS)
            interleaved(sp, NS, [(3, load_b), (0, store_b)])

            sp.wait_ge(edges16_out, 32)

            fast = sp.value_load(mode[0:1, 1:2], min_val=0, max_val=1)
            with sp.If(fast > 0):
                def load_group1(g, b, i):
                    wait_apart(sp, f_turned, g - 1, passed)
                    sp.dma_start(fin[:, b, :], f_g[bass.ds(g, 1), :, :].rearrange("o p c -> p (o c)")
                                 ).then_inc(fin_in[b], 16)
                    wait_apart(sp, eq_made, g - 1, passed)
                    sp.dma_start(srow[:, b, :], src16_g[bass.ds(g, 1), :].to_broadcast([P, GE])
                                 ).then_inc(group1_in[b], 16)
                    wait_apart(sp, away_made, g - 1, passed)
                    wait_apart(sp, home_made, g - 1, passed)
                    sp.dma_start(scol[:, b, :], src_g[bass.ds(g, 1), :, :].rearrange("o p t -> p (o t)")
                                 ).then_inc(group1_in[b], 16)
                    wait_apart(sp, oneT1_made, g - 1, passed)
                    sp.dma_start(drow[:, b, :], dst16_g[bass.ds(g, 1), :].to_broadcast([W3, GE])
                                 ).then_inc(group1_in[b], 16)
                    wait_apart(sp, hsb_made, 2 * (g - 1), passed)
                    sp.dma_start(ccol[:, b, :], cut_g[bass.ds(g, 1), :, :].rearrange("o p t -> p (o t)")
                                 ).then_inc(group1_in[b], 16)
                    if isinstance(g, int) and g == 0:
                        for b_out in range(2):
                            sp.wait_ge(b_h_out[b_out], done(NS, b_out))
                    wait_apart(sp, hd_made, 2 * (g - 1), passed)
                    row = sp.value_load(first_row[0:1, bass.ds(g, 1)], min_val=0, max_val=SPLIT * (NT - WN))
                    sp.dma_start(hwin[:, b, :], h3_d[bass.ds(row, W3), :]).then_inc(hwin_in[b], 16)

                interleaved(sp, NG, [(0, load_group1)])
                for c in range(COPIES):
                    sp.wait_ge(added[c], 16 * NG * T // COPIES)
            with sp.Else():
                for b in range(2):
                    sp.wait_ge(b_h_out[b], done(NS, b))

                def load_tile1(j):
                    wait_apart(sp, w_added, 16 * j, passed)
                    sp.dma_start(scol[:, 0, 0:1], src_t[bass.ds(j, 1), :, :].rearrange("a p o -> p (a o)")
                                 ).then_inc(w_cols_in, 16)
                    sp.dma_start(dcol[:, 0, 0:1], dst_t[bass.ds(j, 1), :, :].rearrange("a p o -> p (a o)")
                                 ).then_inc(w_cols_in, 16)
                    sp.dma_start(ccol[:, 0, 0:1], cut_t[bass.ds(j, 1), :, :].rearrange("a p o -> p (a o)")
                                 ).then_inc(w_edge_in, 16)
                    sp.dma_start(fin[:, 0, 0:RBF], f_t[bass.ds(j, 1), :, :].rearrange("a p r -> p (a r)")
                                 ).then_inc(w_edge_in, 16)
                    sp.dma_start(srow[:, 0, 0:P], src16_t[bass.ds(j, 1), :].to_broadcast([P, P])
                                 ).then_inc(w_row_in, 16)

                each(sp, TILES, load_tile1)
                sp.wait_ge(w_added, 16 * TILES)

            def load_agg_c(s, b, i):
                wait_apart(sp, c_pairs, s - 1, passed)
                for c in range(COPIES):
                    sp.dma_start(agg4[:, b, c, :, :],
                                 agg_k[c:c + 1, :, four(s), :].rearrange("o p k f -> p (o k) f")
                                 ).then_inc(c_agg_in[b], 16)

            def load_x_c(s, b, i):
                wait_apart(sp, c_t2, s - 1, passed)
                sp.dma_start(xb[:, b, :, :], x1_k[:, four(s), :]).then_inc(c_x_in[b], 16)

            sp.wait_ge(b_xbias, NS)
            for b in range(2):
                sp.wait_ge(b_y_out[b], done(NS, b))
            interleaved(sp, NS, [(1, load_agg_c), (0, load_x_c)])
            for b in range(2):
                sp.wait_ge(c_out[b], done(NS, b))

        @block.gpsimd
        def _(pool):
            pool.memset(wf1_sb[:, :, :], 0.0).then_inc(padded_cleared, 1)
            pool.memset(att_blk[:, :], 0.0).then_inc(padded_cleared, 1)
            pool.memset(ident[:, :], 0.0).then_inc(made_pool, 1)
            pool.wait_ge(made_pool, 1)
            pool.affine_select(out=ident[:, :], in_=ident[:, :], compare_op=ALU.not_equal, fill=1.0,
                               base=0, pattern=[[-1, P]], channel_multiplier=1).then_inc(made_pool, 1)
            pool.iota(iota_w[:, :], pattern=[[1, WN]], base=0, channel_multiplier=0,
                      allow_small_or_imprecise_dtypes=True).then_inc(made_pool, 1)
            pool.iota(iota_3w[:, :], pattern=[[SPLIT, WN]], base=0, channel_multiplier=0,
                      allow_small_or_imprecise_dtypes=True).then_inc(made_pool, 1)
            pool.iota(iota_p[:, :], pattern=[[0, 1]], base=0, channel_multiplier=1,
                      allow_small_or_imprecise_dtypes=True).then_inc(made_pool, 1)
            pool.iota(copy_row[:, :], pattern=[[0, T // COPIES], [NT, COPIES]], base=0,
                      channel_multiplier=0, allow_small_or_imprecise_dtypes=True).then_inc(made_pool, 1)
            pool.iota(spare_row[:, :], pattern=[[0, T]], base=NT - P, channel_multiplier=1,
                      allow_small_or_imprecise_dtypes=True).then_inc(made_pool, 1)
            pool.memset(acc[:, :], 0.0).then_inc(buffers_cleared, 1)
            pool.memset(den[:, :], 0.0).then_inc(buffers_cleared, 1)
            pool.memset(fT[:, :, :, :], 0.0).then_inc(buffers_cleared, 1)

            pool.wait_ge(ext_ready, 2)
            pool.wait_ge(rel_checked, 3)
            pool.partition_all_reduce(ext_all[:, :], ext[:, :], P, RMAX).then_inc(ext_reduced, 1)

            for b in range(2):
                pool.wait_ge(a_out[b], done(NS, b))

            pool.wait_ge(mode_ready, 1)
            fast = pool.value_load(mode[0:1, 0:1], min_val=0, max_val=1)
            with pool.If(fast > 0):
                def gather(g, b, i):
                    wait_apart(pool, group0_in[b], 64 * (i + 1), passed)
                    wait_apart(pool, msg_made, g - 1, passed)
                    for t in range(T):
                        pool.indirect_dma_start(
                            out=rows[:, b, t, :], out_offset=None, in_=wh_d[:, :],
                            in_offset=bass.IndirectOffsetOnAxis(ap=idx[:, b, t:t + 1].bitcast(U32), axis=0),
                            bounds_check=NT - 1, oob_is_err=False).then_inc(rows_got[b], 16)

                interleaved(pool, NG, [(0, gather)])
            with pool.Else():
                pool.wait_ge(u_tables, 16 * 4)
                for turn in range(2):
                    def tile0(j):
                        wait_apart(pool, u_cols_in[turn], 32 * (j + 1), passed)
                        for out_e, table, at, got in ((rows[:, 0, 0, :], wh_d, idx, u_rows_got),
                                                      (ad_e[:, :], ad_d, dcol, u_nodes_got[turn]),
                                                      (max_e[:, :], max_d, dcol, u_nodes_got[turn])):
                            pool.indirect_dma_start(
                                out=out_e, out_offset=None, in_=table[:, :],
                                in_offset=bass.IndirectOffsetOnAxis(ap=at[:, 0, 0:1].bitcast(U32), axis=0),
                                bounds_check=NT - 1, oob_is_err=False).then_inc(got, 16)
                        wait_apart(pool, u_dve, (STEPS0[0] * TILES if turn else 0) + STEPS0[turn] * (j + 1),
                                   passed)
                        at = bass.IndirectOffsetOnAxis(ap=sidx[:, 0, 0:1].bitcast(U32), axis=0)
                        if turn == 0:
                            pool.indirect_dma_start(
                                out=max_d[:, :], out_offset=at, in_=new_max[:, :], in_offset=None,
                                bounds_check=NT - 1, oob_is_err=False).then_inc(u_added, 16)
                        else:
                            pool.indirect_dma_start(
                                out=sum_d[:, :], out_offset=at, in_=msg[:, 0, 1, :], in_offset=None,
                                bounds_check=NT - 1, oob_is_err=True, compute_op=ALU.add
                                ).then_inc(u_added, 16)

                    each(pool, TILES, tile0)

            def bias_b(s, b, i):
                wait_for(pool, b_x_in[b], 16 * (i + 1))
                wait_for(pool, b_t2, s - 1)
                pool.tensor_tensor(xbias[:, b, :, :], xb[:, b, :, :],
                                   bc[:, 1, :].unsqueeze(1).to_broadcast([P, K, D]), ALU.add
                                   ).then_inc(b_xbias, 1)

            def last_part_b(s, b, i):
                wait_for(pool, b_mid, s + 1)
                pool.tensor_tensor(h3[:, b, :, 2, :], hr[:, b, :, :], h3[:, b, :, 1, :], ALU.subtract
                                   ).then_inc(b_lo, 1)

            def bias_x1_b(s, b, i):
                wait_for(pool, b_y, s + 1)
                wait_for(pool, b_y_out[b], 16 * i)
                pool.tensor_tensor(x1b[:, b, :, :], y1[:, b, :, :],
                                   bc[:, 0, :].unsqueeze(1).to_broadcast([P, K, D]), ALU.add
                                   ).then_inc(b_x1b, 1)

            interleaved(pool, NS, [(2, bias_b), (1, bias_x1_b), (0, last_part_b)])

            pool.wait_ge(agg_zeroed, 16 * NG)

            fast = pool.value_load(mode[0:1, 1:2], min_val=0, max_val=1)
            with pool.If(fast > 0):
                def scatter(g, b, i):
                    wait_apart(pool, sidx_made, g + 1, passed)
                    wait_apart(pool, xo_made, 2 * (g + 1), passed)
                    for t in range(T):
                        wait_for(pool, added[t % COPIES], 16 * (g * (T // COPIES) + t // COPIES))
                        pool.sem_inc(earlier_added if t == COPIES - 1 else passed, 1)
                        pool.indirect_dma_start(
                            out=agg_d[:, :],
                            out_offset=bass.IndirectOffsetOnAxis(ap=sidx[:, b, t:t + 1].bitcast(U32), axis=0),
                            in_=xo[:, b, t, :], in_offset=None, bounds_check=COPIES * NT - 1,
                            oob_is_err=True, compute_op=ALU.add).then_inc(added[t % COPIES], 16)

                interleaved(pool, NG, [(0, scatter)])
            with pool.Else():
                def tile1(j):
                    wait_apart(pool, w_cols_in, 32 * (j + 1), passed)
                    pool.indirect_dma_start(
                        out=h_e[:, :], out_offset=None, in_=h_rows,
                        in_offset=bass.IndirectOffsetOnAxis(ap=dcol[:, 0, 0:1].bitcast(U32), axis=0),
                        bounds_check=NT - 1, oob_is_err=False).then_inc(w_gathered, 16)
                    wait_apart(pool, w_dve, STEPS1 * (j + 1), passed)
                    pool.indirect_dma_start(
                        out=agg_d[:, :],
                        out_offset=bass.IndirectOffsetOnAxis(ap=sidx[:, 0, 0:1].bitcast(U32), axis=0),
                        in_=xo[:, 0, 0, :], in_offset=None, bounds_check=COPIES * NT - 1,
                        oob_is_err=True, compute_op=ALU.add).then_inc(w_added, 16)

                each(pool, TILES, tile1)
            pool.sem_inc(passed, 1)

            def pairs_c(s, b, i):
                wait_for(pool, c_agg_in[b], 16 * COPIES * (i + 1))
                wait_for(pool, c_ag, s - 1)
                pool.tensor_tensor(pair[:, b, :, :, :], agg4[:, b, 0:2, :, :], agg4[:, b, 2:4, :, :], ALU.add
                                   ).then_inc(c_pairs, 1)

            def store_c(s, b, i):
                wait_apart(pool, c_fin, s + 1, passed)
                pool.dma_start(out_k[:, four(s), :], y1[:, b, :, :]).then_inc(c_out[b], 16)

            interleaved(pool, NS, [(4, pairs_c), (0, store_c)])

        @block.scalar
        def _(act):
            act.preload_act_table_set("natural_log_exp_and_others")
            act.dma_start(w_sb[:, :], W).then_inc(w_in, 16)
            act.wait_ge(padded_cleared, 2)
            for h in range(HEADS):
                for side in range(2):
                    act.dma_start(att_blk[F * h:F * h + F, side * HEADS + h:side * HEADS + h + 1],
                                 att[h:h + 1, side * F:side * F + F].rearrange("o f -> f o"),
                                 allow_slow_non_contiguous=True).then_inc(w_in, 16)
            act.dma_start(first_dst[:, :], dst.rearrange("(g e) -> g e", e=GE)[:, 0:1].rearrange("g o -> o g"),
                          allow_slow_non_contiguous=True).then_inc(first_in, 16)
            act.dma_start(edges[:, :, :], dst.rearrange("(p g e) -> p g e", g=2, e=GE)).then_inc(edges_in, 16)
            act.wait_ge(w_turned, 1)
            act.copy(wT[:, :], bank[0][:, 0:D]).then_inc(wT_made, 1)
            act.wait_ge(rank_exp, 1)
            act.activation(rank_w[:, :], rank_cap[:, :], ACT.Exp).then_inc(rank_made, 1)
            act.wait_ge(edges16_made, 1)
            act.dma_start(dst16_d[:].rearrange("(p g e) -> p g e", g=2, e=GE), edges16[:, :, :]
                          ).then_inc(edges16_out, 16)
            act.wait_ge(rel_checked, 3)
            act.dma_start(edges[:, :, :], src.rearrange("(p g e) -> p g e", g=2, e=GE)).then_inc(edges_in, 16)

            def turn_a(s, b, i):
                wait_for(act, a_turned, s + 1)
                wait_for(act, a_v, 2 * (s - 1))
                act.copy(nT[:, b, :, :].rearrange("p k n -> p (k n)"), bank[b][:, :]).then_inc(a_xT, 1)
                if isinstance(s, int) and s == 1:
                    act.dma_start(wf2_sb[:, :], W_f2).then_inc(weights_in, 16)
                    act.dma_start(wo2_sb[:, :], W_o2).then_inc(weights_in, 16)
                    act.dma_start(rows_in[:, 0, :], b_f2.rearrange("(a p) -> a p", a=1)).then_inc(weights_in, 16)
                    act.dma_start(rows_in[:, 1, :], b_o2.rearrange("(a p) -> a p", a=1)).then_inc(weights_in, 16)
                    act.dma_start(rows_in[:, 2, :], bias0.rearrange("(a p) -> a p", a=1)).then_inc(weights_in, 16)
                    act.dma_start(win_sb[:, :], W_in).then_inc(weights_in, 16)
                    act.dma_start(wo1_sb[:, :], W_o1).then_inc(weights_in, 16)
                    act.dma_start(bf1_c[:, :], b_f1.rearrange("(p a) -> p a", a=1)).then_inc(weights_in, 16)
                    act.dma_start(bo1_c[:, :], b_o1.rearrange("(p a) -> p a", a=1)).then_inc(weights_in, 16)
                    for t in range(Q):
                        act.dma_start(wf1_sb[RBF * t:RBF * t + RBF, t, :], W_f1).then_inc(weights_in, 16)

            interleaved(act, NS, [(0, turn_a)])
            act.wait_ge(edges16_made, 2)
            act.dma_start(src16_d[:].rearrange("(p g e) -> p g e", g=2, e=GE), edges16[:, :, :]
                          ).then_inc(edges16_out, 16)

            act.wait_ge(mode_ready, 1)
            fast = act.value_load(mode[0:1, 0:1], min_val=0, max_val=1)
            with act.If(fast > 0):
                def weigh(g, b, i):
                    wait_for(act, ls_made, g + 1)
                    wait_for(act, summed, g - 1)
                    act.activation(msg[:, b, :, D:ROW], ls[:, b, :, :], ACT.Exp).then_inc(wgt_made, 1)

                def window_out(g, b, i):
                    wait_for(act, summed, g + 1)
                    wait_for(act, win_turned, g - 1)
                    act.copy(win[:, b, :], bank[2 + b][0:WN, 0:ROW]).then_inc(win_made, 1)

                interleaved(act, NG, [(1, weigh), (0, window_out)])
            with act.Else():
                def weigh_tile(j):
                    wait_for(act, u_dve, STEPS0[0] * TILES + STEPS0[1] * j + 8)
                    act.activation(msg[:, 0, 0, D:ROW], ls[:, 0, 0, :], ACT.Exp).then_inc(u_act, 1)

                each(act, TILES, weigh_tile)

            def inverse_root(s, b, before):
                wait_for(act, n_mv, s + before + 1)
                act.activation(lnvar[:, b, :], mv[:, b, :, 1], ACT.Ln, bias=eps_c[:, 0:1]).then_inc(n_rstd, 1)
                wait_for(act, n_rstd, 2 * (s + before) + 1)
                act.activation(rstd[:, b, :], lnvar[:, b, :], ACT.Exp, scale=-0.5).then_inc(n_rstd, 1)

            def sums_b(s, b, i):
                wait_for(act, b_turned, s - 1)
                act.copy(accs[:, b, :, :], acc_k[:, four(s), :]).then_inc(b_accs, 1)
                act.copy(dens[:, b, :, :], den_k[:, four(s), :]).then_inc(b_accs, 1)

            def root_b(s, b, i):
                inverse_root(s, b, 0)

            def x1T_b(s, b, i):
                wait_for(act, b_yturned, s + 1)
                wait_for(act, b_h, s - 1)
                act.copy(nT[:, b, :, :].rearrange("p k n -> p (k n)"), bank[4][:, :]).then_inc(b_yT, 1)

            def parts_b(s, b, i):
                wait_for(act, b_h, s + 1)
                wait_for(act, b_h_out[b], 16 * i)
                act.copy(h3[:, b, :, 0, :], bank[5][:, :].rearrange("p (k f) -> p k f", k=K)
                         ).then_inc(b_hi, 1)
                wait_for(act, b_hr, s + 1)
                act.copy(h3[:, b, :, 1, :], hr[:, b, :, :]).then_inc(b_mid, 1)

            act.wait_ge(attended, 1)
            interleaved(act, NS, [(0, x1T_b), (1, root_b), (2, sums_b), (0, parts_b)])

            def turn_1(g, b, i):
                wait_for(act, f_turned, g + 1)
                wait_for(act, v_made, 2 * (g - 1))
                act.copy(fT[0:Q * RBF, b, :, :], bank[0][0:Q * RBF, 0:2 * P]
                         .rearrange("r (q p) -> r q p", q=2)).then_inc(fT_made, 1)

            def expanded_h(g, b, i):
                wait_for(act, group1_in[b], 64 * (i + 1))
                for q in range(2):
                    wait_for(act, hd_made, 2 * g + q + 1)
                    wait_for(act, xij_made, 2 * g + q - 1)
                    for t in range(Q):
                        ins = act.activation(hsb[:, q, t, :], bank[3 + 4 * q][:, t * D:(t + 1) * D],
                                             ACT.Copy, scale=ccol[:, b, q * Q + t:q * Q + t + 1])
                    ins.then_inc(hsb_made, 1)

            def softplus_1(g, b, i):
                for q in range(2):
                    wait_for(act, exc_made, 2 * g + q + 1)
                    wait_for(act, ln_made, 2 * g + q - 1)
                    act.activation(ex[:, q, :], exc[:, q, :], ACT.Exp).then_inc(ex_made, 1)
                for q in range(2):
                    wait_for(act, ex_made, 2 * g + q + 1)
                    wait_for(act, gact_made, 2 * g + q - 1)
                    act.activation(ln[:, q, :], ex[:, q, :], ACT.Ln, bias=1.0).then_inc(ln_made, 1)

            def messages_out(g, b, i):
                for q in range(2):
                    wait_for(act, presummed, 2 * g + q + 1)
                    if q == 0:
                        wait_for(act, earlier_added, g)
                    act.copy(xo[:, b, Q * q:Q * q + Q, :],
                             bank[6][:, :].rearrange("p (t f) -> p t f", t=Q)).then_inc(xo_made, 1)

            fast = act.value_load(mode[0:1, 1:2], min_val=0, max_val=1)
            with act.If(fast > 0):
                act.wait_ge(buffers_cleared, 3)
                interleaved(act, NG, [(1, turn_1), (0, expanded_h), (1, softplus_1), (0, messages_out)])
            with act.Else():
                def softplus_tile(j):
                    wait_for(act, w_pe, 4 * j + 1)
                    act.copy(fT[0:RBF, 0, 0, :], bank[0][0:RBF, 0:P]).then_inc(w_act, 1)
                    wait_for(act, w_dve, STEPS1 * j + 7)
                    act.activation(ex[:, 0, 0:P], exc[:, 0, 0:P], ACT.Exp).then_inc(w_act, 1)
                    wait_for(act, w_act, 3 * j + 2)
                    act.activation(ln[:, 0, 0:P], ex[:, 0, 0:P], ACT.Ln, bias=1.0).then_inc(w_act, 1)

                each(act, TILES, softplus_tile)

            def inner_c(s, b, i):
                wait_for(act, c_turned, s + 1)
                wait_for(act, c_o, s - 1)
                act.copy(nT[:, b, :, :].rearrange("p k n -> p (k n)"), bank[b][:, :]).then_inc(c_agT, 1)
                wait_for(act, c_exc, s + 1)
                wait_for(act, c_ln, s - 1)
                act.activation(ex[:, b, :], exc[:, b, :], ACT.Exp).then_inc(c_ex, 1)
                wait_for(act, c_ex, s + 1)
                wait_for(act, c_g, s - 1)
                act.activation(ln[:, b, :], ex[:, b, :], ACT.Ln, bias=1.0).then_inc(c_ln, 1)

            def root_c(s, b, i):
                inverse_root(s, b, NS)

            interleaved(act, NS, [(2, inner_c), (1, root_c)])

        @block.tensor
        def _(pe):
            pe.wait_ge(made_pool, 7)
            pe.wait_ge(w_in, 16 * 9)
            pe.transpose(bank[0][:, 0:D], w_sb[:, :], ident[:, :]).then_inc(w_turned, 1)
            pe.wait_ge(wT_made, 1)
            pe.matmul(bank[1][:, 0:2 * HEADS], wT[:, :], att_blk[:, :], start=True, stop=True
                      ).then_inc(w_turned, 1)
            pe.wait_ge(v_ready, 2)

            pe.wait_ge(made_dve, 4)
            pe.wait_ge(first_ready, 1)
            pe.matmul(bank[6][:, 0:NG], ones[0:1, :], first_f[0:1, :], start=True, stop=True
                      ).then_inc(base_spread, 1)

            def turn_a(s, b, i):
                wait_for(pe, a_x_in[b], 16 * (i + 1))
                wait_for(pe, a_xT, s - 1)
                for k in range(K):
                    mm = pe.transpose(bank[b][:, k * P:(k + 1) * P], xb[:, b, k, :], ident[:, :])
                mm.then_inc(a_turned, 1)

            def project_a(s, b, i):
                wait_for(pe, a_xT, s + 1)
                wait_for(pe, a_row, 2 * (s - 1))
                for half in range(2):
                    for k in range(2):
                        mm = pe.matmul(bank[2 + 2 * b + half][:, k * COLS:(k + 1) * COLS],
                                       nT[:, b, 2 * half + k, :], v_sb[:, :], start=True, stop=True)
                    mm.then_inc(a_v, 1)

            interleaved(pe, NS, [(1, turn_a), (0, project_a)])

            pe.wait_ge(weights_in, 16 * 13)
            pe.wait_ge(a_row, 2 * NS)
            pe.matmul(bank[2][0:1, 0:D], ones[:, 0:1], wf2_sb[:, :], start=True, stop=True)
            pe.matmul(bank[2][0:1, D:2 * D], ones[:, 0:1], wo2_sb[:, :], start=True, stop=True
                      ).then_inc(colsums_made, 1)
            pe.wait_ge(rows_ready, 3)
            pe.matmul(bank[4][:, 0:2 * D], ones[0:1, :], rows_eff[0:1, 1:3, :], start=True, stop=True
                      ).then_inc(bc_spread, 1)
            pe.wait_ge(split_made, 6)

            pe.wait_ge(mode_ready, 1)
            fast = pe.value_load(mode[0:1, 0:1], min_val=0, max_val=1)
            with pe.If(fast > 0):
                def expand_0(g, b, i):
                    wait_for(pe, oneT_made, g + 1)
                    wait_for(pe, group0_in[b], 64 * (i + 1))
                    wait_for(pe, z_made, 2 * (g - 1))
                    for t in range(T):
                        mm = pe.matmul(bank[b][:, t * HEADS:(t + 1) * HEADS], oneT[:, b, t, :],
                                       adwin[:, b, :], start=True, stop=True)
                    mm.then_inc(expanded, 1)

                def sum_0(g, b, i):
                    wait_for(pe, one_made, g + 1)
                    wait_for(pe, msg_made, g + 1)
                    wait_for(pe, win_made, g - 1)
                    for t in range(T):
                        mm = pe.matmul(bank[2 + b][0:WN, 0:ROW], one[:, b, t, :], msg[:, b, t, :],
                                       start=(t == 0), stop=(t == T - 1))
                    mm.then_inc(summed, 1)
                    wait_for(pe, win_made, g + 1)
                    wait_apart(pe, acc_added, g - 1, passed)
                    pe.transpose(bank[4 + b][:, 0:WN], win[:, b, 0:D], ident[0:WN, 0:WN])
                    pe.transpose(bank[4 + b][0:HEADS, P:P + WN], win[:, b, D:ROW], ident[0:WN, 0:WN]
                                 ).then_inc(win_turned, 1)

                interleaved(pe, NG, [(1, expand_0), (0, sum_0)])
            with pe.Else():
                for turn in range(2):
                    def tile0(j):
                        before = (STEPS0[0] * TILES if turn else 0) + STEPS0[turn] * j
                        wait_for(pe, u_dve, before + 3)
                        pe.matmul(bank[3][:, 0:1], eq[:, 0, 0, :].bitcast(BF16)[:, 1::2], rank_w[:, 0:1],
                                  start=True, stop=True).then_inc(u_pe, 1)
                        if turn == 0:
                            wait_for(pe, u_dve, before + 12)
                            pe.matmul(bank[1][:, :], ones[:, :], exc[:, 0, :], start=True, stop=True
                                      ).then_inc(u_pe, 1)
                        else:
                            wait_for(pe, u_dve, before + 9)
                            wait_for(pe, u_act, j + 1)
                            pe.matmul(bank[2][:, 0:ROW], eq[:, 0, 0, :], msg[:, 0, 0, :], start=True,
                                      stop=True).then_inc(u_pe, 1)

                    each(pe, TILES, tile0)

                def turn_sums(k):
                    wait_for(pe, u_sums_in, 16 * (k + 1))
                    wait_for(pe, u_sums_kept, k)
                    pe.transpose(bank[0][:, 0:P], msg[:, 0, 0, 0:D], ident[:, :])
                    pe.transpose(bank[0][0:HEADS, P:2 * P], msg[:, 0, 0, D:ROW], ident[:, :]
                                 ).then_inc(u_sums_turned, 1)

                each(pe, NB, turn_sums)

            def turn_b(s, b, i):
                wait_for(pe, b_accs, 2 * (s + 1))
                wait_for(pe, b_t1, s - 1)
                for k in range(K):
                    pe.transpose(bank[b][:, k * D:(k + 1) * D], accs[:, b, k, :], ident[:, :])
                for k in range(K):
                    mm = pe.transpose(bank[2 + b][:, k * HEADS:(k + 1) * HEADS], dens[:, b, k, :],
                                      ident[0:HEADS, 0:HEADS])
                mm.then_inc(b_turned, 1)

            def turn_x1_b(s, b, i):
                wait_for(pe, b_y, s + 1)
                wait_for(pe, b_yT, s)
                for k in range(K):
                    mm = pe.transpose(bank[4][:, k * P:(k + 1) * P], y1[:, b, k, :], ident[:, :])
                mm.then_inc(b_yturned, 1)

            def h_b(s, b, i):
                wait_for(pe, b_yT, s + 1)
                wait_for(pe, b_hr, s)
                for k in range(K):
                    mm = pe.matmul(bank[5][:, k * D:(k + 1) * D], nT[:, b, k, :], win_sb[:, :],
                                   start=True, stop=True)
                mm.then_inc(b_h, 1)

            pe.wait_ge(attended, 1)
            interleaved(pe, NS, [(0, h_b), (2, turn_b), (1, turn_x1_b)])
            pe.wait_ge(b_hr, NS)
            pe.wait_ge(weights_in, 16 * 14)
            pe.wait_ge(rank_ready, 1)

            fast = pe.value_load(mode[0:1, 1:2], min_val=0, max_val=1)
            with pe.If(fast > 0):
                def turn_1(g, b, i):
                    wait_for(pe, fin_in[b], 16 * (i + 1))
                    wait_for(pe, fT_made, g)
                    wait_for(pe, shift_made, g - 1)
                    for q in range(2):
                        mm = pe.transpose(bank[0][0:Q * RBF, q * P:(q + 1) * P],
                                          fin[:, b, q * Q * RBF:(q + 1) * Q * RBF], ident[:, :])
                    mm.then_inc(f_turned, 1)

                def expand_1(g, b, i):
                    wait_for(pe, oneT1_made, g + 1)
                    wait_for(pe, hwin_in[b], 16 * (i + 1))
                    for q in range(2):
                        wait_for(pe, hsb_made, 2 * g + q - 1)
                        for t in range(Q):
                            mm = pe.matmul(bank[3 + 4 * q][:, t * D:(t + 1) * D], oneT[:, b, q * Q + t, :],
                                           hwin[:, b, :], start=True, stop=True)
                        mm.then_inc(hd_made, 1)

                def inner_1(g, b, i):
                    wait_for(pe, fT_made, g + 1)
                    for q in range(2):
                        wait_for(pe, gact_made, 2 * g + q - 1)
                        for t in range(Q):
                            mm = pe.matmul(bank[1 + q][:, t * P:(t + 1) * P], wf1_sb[:, t, :],
                                           fT[:, b, q, :], start=True, stop=True)
                        mm.then_inc(v_made, 1)

                def outer_1(g, b, i):
                    for q in range(2):
                        wait_for(pe, gact_made, 2 * g + q + 1)
                        wait_for(pe, xij_made, 2 * g + q - 1)
                        pe.matmul(bank[4 + q][:, :], ones_bf[0:SPLIT, :],
                                  bf2_3[:, :].unsqueeze(1).to_broadcast([SPLIT, Q, D]), start=True, stop=False)
                        for t in range(Q):
                            mm = pe.matmul(bank[4 + q][:, t * D:(t + 1) * D],
                                           gact[:, b, q, t * P:(t + 1) * P], wf2_sb[:, :],
                                           start=False, stop=(t == Q - 1))
                        mm.then_inc(wij_made, 1)

                def presum_1(g, b, i):
                    wait_for(pe, eq_made, g + 1)
                    wait_for(pe, shift_made, g)
                    for t in range(T):
                        mm = pe.matmul(bank[0][:, 2 * P + t:2 * P + t + 1],
                                       eq[:, b, t, :].bitcast(BF16)[:, 1::2], rank_w[:, 0:1],
                                       start=True, stop=True)
                    mm.then_inc(ranked, 1)
                    for q in range(2):
                        wait_for(pe, xij_made, 2 * g + q + 1)
                        wait_for(pe, xo_made, 2 * g + q)
                        for t in range(Q):
                            mm = pe.matmul(bank[6][:, t * D:(t + 1) * D], eq[:, b, q * Q + t, :],
                                           xij[:, q, t * D:(t + 1) * D], start=True, stop=True)
                        mm.then_inc(presummed, 1)

                interleaved(pe, NG, [(1, turn_1), (0, expand_1), (1, inner_1), (0, outer_1), (0, presum_1)])
                pe.wait_ge(shift_made, NG)
                pe.wait_ge(xo_made, 2 * NG)
            with pe.Else():
                def tile1(j):
                    wait_for(pe, w_edge_in, 32 * (j + 1))
                    pe.transpose(bank[0][0:RBF, 0:P], fin[:, 0, 0:RBF], ident[:, :]).then_inc(w_pe, 1)
                    wait_for(pe, w_act, 3 * j + 1)
                    pe.matmul(bank[1][:, 0:P], wf1_sb[:, 0, :], fT[:, 0, 0, :], start=True, stop=True)
                    wait_for(pe, w_dve, STEPS1 * j + 3)
                    pe.matmul(bank[3][:, 0:1], eq[:, 0, 0, :].bitcast(BF16)[:, 1::2], rank_w[:, 0:1],
                              start=True, stop=True).then_inc(w_pe, 1)
                    wait_for(pe, w_dve, STEPS1 * j + 8)
                    pe.matmul(bank[2][:, 0:D], ones_bf[0:SPLIT, :], bf2_3[:, :], start=True, stop=False)
                    pe.matmul(bank[2][:, 0:D], gact[:, 0, 0, 0:P], wf2_sb[:, :], start=False, stop=True
                              ).then_inc(w_pe, 1)
                    wait_for(pe, w_dve, STEPS1 * j + 10)
                    pe.matmul(bank[4][:, 0:D], eq[:, 0, 0, :], xij[:, 0, 0:D], start=True, stop=True
                              ).then_inc(w_pe, 1)

                each(pe, TILES, tile1)

            def turn_c(s, b, i):
                wait_for(pe, c_ag, s + 1)
                wait_for(pe, c_agT, s - 1)
                for k in range(K):
                    mm = pe.transpose(bank[b][:, k * P:(k + 1) * P], ag[:, b, k, :], ident[:, :])
                mm.then_inc(c_turned, 1)

            def inner_c(s, b, i):
                wait_for(pe, c_agT, s + 1)
                wait_for(pe, c_g, s - 1)
                pe.matmul(bank[2 + b][:, :], wo1_sb[:, :], nT[:, b, :, :], start=True, stop=True
                          ).then_inc(c_o, 1)

            def outer_c(s, b, i):
                wait_for(pe, c_g, s + 1)
                wait_for(pe, c_t2, s - 1)
                for k in range(K):
                    mm = pe.matmul(bank[4 + b][:, k * D:(k + 1) * D], gact[:, b, 0, k * P:(k + 1) * P],
                                   wo2_sb[:, :], start=True, stop=True)
                mm.then_inc(c_y, 1)

            interleaved(pe, NS, [(2, turn_c), (2, inner_c), (1, outer_c)])

        @block.vector
        def _(dve):
            dve.memset(zeros[:, :], 0.0).then_inc(made_dve, 1)
            dve.memset(ones_bf[:, :], 1.0).then_inc(made_dve, 1)
            dve.memset(eps_c[:, :], EPS).then_inc(made_dve, 1)
            dve.memset(ones[:, :], 1.0).then_inc(made_dve, 1)
            dve.memset(ext[:, :], 0.0).then_inc(rel_checked, 1)
            dve.wait_ge(made_pool, 7)
            dve.tensor_scalar(rank_cap[:, :], iota_p[:, :], -LN2, 60 * LN2, ALU.mult, ALU.add
                              ).then_inc(rank_exp, 1)
            dve.wait_ge(w_in, 16 * 9)
            dve.tensor_copy(v_sb[:, 0:D], w_sb[:, :]).then_inc(v_ready, 1)
            dve.wait_ge(w_turned, 2)
            dve.tensor_copy(v_sb[:, D:COLS], bank[1][:, 0:2 * HEADS]).then_inc(v_ready, 1)
            dve.tensor_scalar(below[:, :], iota_3w[:, :], iota_p[:, 0:1], None, ALU.is_le).then_inc(bases_ready, 1)
            dve.wait_ge(bases_ready, 1)
            dve.tensor_reduce(third[:, :], below[:, :], AX.X, ALU.add).then_inc(bases_ready, 1)
            dve.wait_ge(first_in, 16)
            dve.tensor_copy(first_f[:, :], first_dst[:, :]).then_inc(first_ready, 1)
            dve.tensor_scalar(first_row[:, :], first_dst[:, :], float(SPLIT), None, ALU.mult
                              ).then_inc(first_ready, 1)
            dve.wait_ge(bases_ready, 2)
            dve.wait_ge(base_spread, 1)
            dve.tensor_copy(base_bc[:, :], bank[6][:, 0:NG]).then_inc(bases_ready, 1)
            dve.tensor_scalar(node_id[:, :], bank[6][:, 0:NG], third[:, 0:1], -1.0, ALU.add, ALU.add
                              ).then_inc(bases_ready, 1)
            dve.wait_ge(bases_ready, 4)
            dve.wait_ge(edges_in, 16)
            dve.tensor_copy(edges16[:, :, :], edges[:, :, :]).then_inc(edges16_made, 1)
            dve.tensor_copy(group_f[:, 0, :], edges[:, :, 0]).then_inc(group_made, 1)
            dve.tensor_reduce(group_f[:, 1, :], edges[:, :, :], AX.X, ALU.max).then_inc(group_made, 1)
            dve.tensor_reduce(group_f[:, 2, :], edges[:, :, :], AX.X, ALU.min).then_inc(group_made, 1)
            dve.wait_ge(group_made, 3)
            dve.tensor_tensor(group_f[:, 3, :], group_f[:, 1, :], group_f[:, 0, :], ALU.subtract
                              ).then_inc(group_made, 1)
            dve.tensor_tensor(group_f[:, 4, :], group_f[:, 0, :], group_f[:, 2, :], ALU.subtract
                              ).then_inc(group_made, 1)
            dve.wait_ge(group_made, 5)
            dve.wait_ge(rel_checked, 1)
            dve.tensor_reduce(ext[0:GP, 8:9], group_f[:, 3, :], AX.X, ALU.max).then_inc(rel_checked, 1)
            dve.tensor_reduce(ext[0:GP, 9:10], group_f[:, 4, :], AX.X, ALU.max).then_inc(rel_checked, 1)

            def row_a(s, b, i):
                wait_for(dve, a_out[b], 16 * i)
                for half in range(2):
                    wait_for(dve, a_v, 2 * s + half + 1)
                    both = bank[2 + 2 * b + half][:, 0:2 * COLS].rearrange("p (k c) -> p k c", k=2)
                    dve.tensor_copy(nS[:, b, 2 * half:2 * half + 2, 0:ROW], both[:, :, 0:ROW])
                    dve.tensor_copy(sd_all[:, bass.ds(s * K + 2 * half, 2), :], both[:, :, D:COLS]
                                    ).then_inc(a_row, 1)

            interleaved(dve, NS, [(0, row_a)])

            s_hn = sd_all[:, :, 0:HEADS].rearrange("p n h -> p h n")
            dve.wait_ge(rel_checked, 3)
            dve.wait_ge(a_row, 2 * NS)
            dve.tensor_reduce(ext[:, 0:HEADS], s_hn, AX.X, ALU.max).then_inc(ext_ready, 1)
            dve.tensor_reduce(ext[:, HEADS:2 * HEADS], s_hn, AX.X, ALU.min, negate=True).then_inc(ext_ready, 1)
            ad = sd_all[:, :, HEADS:2 * HEADS]
            dve.tensor_copy(ad3[:, :, 0, :], ad).then_inc(ad_split, 1)
            dve.wait_ge(ad_split, 1)
            dve.tensor_tensor(ad_rest[:, 0, :, :], ad, ad3[:, :, 0, :], ALU.subtract).then_inc(ad_split, 1)
            dve.wait_ge(ad_split, 2)
            dve.tensor_copy(ad3[:, :, 1, :], ad_rest[:, 0, :, :]).then_inc(ad_split, 1)
            dve.wait_ge(ad_split, 3)
            dve.tensor_tensor(ad_rest[:, 1, :, :], ad_rest[:, 0, :, :], ad3[:, :, 1, :], ALU.subtract
                              ).then_inc(ad_split, 1)
            dve.wait_ge(ad_split, 4)
            dve.tensor_copy(ad3[:, :, 2, :], ad_rest[:, 1, :, :]).then_inc(ad_split, 1)
            dve.wait_ge(ext_reduced, 1)
            dve.tensor_tensor(spread[:, :], ext_all[0:1, 0:HEADS], ext_all[0:1, HEADS:2 * HEADS], ALU.add
                              ).then_inc(mode_steps, 1)
            dve.tensor_scalar(tests[:, 2:3], ext_all[0:1, 8:9], WN - 1.0, None, ALU.is_le).then_inc(mode_steps, 1)
            dve.tensor_scalar(tests[:, 3:4], ext_all[0:1, 9:10], 0.0, None, ALU.is_le).then_inc(mode_steps, 1)
            dve.wait_ge(mode_steps, 3)
            dve.tensor_reduce(tests[:, 0:1], spread[:, :], AX.X, ALU.max).then_inc(mode_steps, 1)
            dve.tensor_tensor(tests[:, 1:2], tests[:, 2:3], tests[:, 3:4], ALU.mult).then_inc(mode_steps, 1)
            dve.wait_ge(mode_steps, 5)
            dve.scalar_tensor_tensor(out=mode[:, 0:1], in0=tests[:, 0:1], scalar=SPREAD_MAX,
                                     in1=tests[:, 1:2], op0=ALU.is_le, op1=ALU.mult).then_inc(mode_steps, 1)
            dve.tensor_copy(mode[:, 1:2], tests[:, 1:2]).then_inc(mode_steps, 1)
            dve.wait_ge(mode_steps, 7)
            dve.sem_inc(mode_ready, 1)
            dve.wait_ge(colsums_made, 1)
            dve.scalar_tensor_tensor(out=rows_eff[0:1, 0, :], in0=bank[2][0:1, 0:D], scalar=-LN2,
                                     in1=rows_in[0:1, 0, :], op0=ALU.mult, op1=ALU.add).then_inc(rows_ready, 1)
            dve.scalar_tensor_tensor(out=rows_eff[0:1, 1, :], in0=bank[2][0:1, D:2 * D], scalar=-LN2,
                                     in1=rows_in[0:1, 1, :], op0=ALU.mult, op1=ALU.add).then_inc(rows_ready, 1)
            dve.tensor_copy(rows_eff[0:1, 2, :], rows_in[0:1, 2, :]).then_inc(rows_ready, 1)
            dve.wait_ge(rows_ready, 3)
            dve.tensor_copy(split_b[0:1, 0, :], rows_eff[0:1, 0, :]).then_inc(split_made, 1)
            dve.wait_ge(split_made, 1)
            dve.tensor_tensor(rest[0:1, 0, :], rows_eff[0:1, 0, :], split_b[0:1, 0, :], ALU.subtract
                              ).then_inc(split_made, 1)
            dve.wait_ge(split_made, 2)
            dve.tensor_copy(split_b[0:1, 1, :], rest[0:1, 0, :]).then_inc(split_made, 1)
            dve.wait_ge(split_made, 3)
            dve.tensor_tensor(rest[0:1, 1, :], rest[0:1, 0, :], split_b[0:1, 1, :], ALU.subtract
                              ).then_inc(split_made, 1)
            dve.wait_ge(split_made, 4)
            dve.tensor_copy(split_b[0:1, 2, :], rest[0:1, 1, :]).then_inc(split_made, 1)
            dve.wait_ge(bc_spread, 1)
            dve.tensor_copy(bc[:, :, :], bank[4][:, 0:2 * D].rearrange("p (r f) -> p r f", r=2)
                            ).then_inc(split_made, 1)
            dve.wait_ge(rank_made, 1)
            dve.tensor_scalar(rank_cap[:, :], rank_w[:, :], 2.5, None, ALU.mult).then_inc(rank_ready, 1)
            dve.wait_ge(edges_in, 32)
            dve.wait_ge(edges16_out, 16)
            dve.tensor_copy(edges16[:, :, :], edges[:, :, :]).then_inc(edges16_made, 1)
            dve.wait_ge(buffers_cleared, 3)

            fast = dve.value_load(mode[0:1, 0:1], min_val=0, max_val=1)
            with dve.If(fast > 0):
                def weights_0(g, b, i):
                    wait_for(dve, group0_in[b], 64 * (i + 1))
                    wait_for(dve, expanded, g - 1)
                    dve.tensor_scalar(oneT[:, b, :, :].rearrange("n t p -> n p t"),
                                      drow[:, b, :].rearrange("n (p t) -> n p t", t=T),
                                      node_id[0:W3, bass.ds(g, 1)], None, ALU.is_equal).then_inc(oneT_made, 1)
                    wait_for(dve, group0_in[b], 64 * (i + 1))
                    dve.tensor_scalar(rel[:, b, :], dcol[:, b, :], base_bc[:, bass.ds(g, 1)], None, ALU.subtract
                                      ).then_inc(rel_made, 1)
                    wait_for(dve, rel_made, g + 1)
                    wait_for(dve, summed, g - 1)
                    dve.tensor_tensor(one[:, b, :, :], iota_w[:, :].unsqueeze(1).to_broadcast([P, T, WN]),
                                      rel[:, b, :].unsqueeze(2).to_broadcast([P, T, WN]), ALU.is_equal
                                      ).then_inc(one_made, 1)
                    wait_for(dve, rows_got[b], 16 * T * (i + 1))
                    wait_for(dve, expanded, g + 1)
                    ad_e = bank[b][:, 0:T * HEADS].rearrange("p (t h) -> p t h", h=HEADS)
                    dve.tensor_tensor(z[:, b, :, 0:HEADS], rows[:, b, :, D:ROW], ad_e, ALU.add).then_inc(z_made, 1)
                    dve.tensor_tensor(z[:, b, :, HEADS:2 * HEADS], ad_e,
                                      ext_all[:, 0:HEADS].unsqueeze(1).to_broadcast([P, T, HEADS]), ALU.add
                                      ).then_inc(z_made, 1)
                    wait_for(dve, z_made, 2 * (g + 1))
                    dve.scalar_tensor_tensor(out=lg[:, b, :, :], in0=z[:, b, :, :], scalar=SLOPE,
                                             in1=z[:, b, :, :], op0=ALU.mult, op1=ALU.max).then_inc(lg_made, 1)
                    wait_for(dve, lg_made, g + 1)
                    wait_for(dve, wgt_made, g - 1)
                    dve.tensor_tensor(ls[:, b, :, :], lg[:, b, :, 0:HEADS], lg[:, b, :, HEADS:2 * HEADS],
                                      ALU.subtract).then_inc(ls_made, 1)
                    wait_for(dve, wgt_made, g + 1)
                    dve.tensor_tensor(msg[:, b, :, 0:D].rearrange("p t (h f) -> p t h f", h=HEADS),
                                      rows[:, b, :, 0:D].rearrange("p t (h f) -> p t h f", h=HEADS),
                                      msg[:, b, :, D:ROW].unsqueeze(3).to_broadcast([P, T, HEADS, F]), ALU.mult
                                      ).then_inc(msg_made, 1)

                def add_0(g, b, i):
                    wait_for(dve, win_turned, g + 1)
                    wait_for(dve, acc_added, g)
                    base = dve.value_load(first_dst[0:1, bass.ds(g, 1)], min_val=0, max_val=NT - WN)
                    dve.tensor_tensor(acc[:, bass.ds(base, WN)], acc[:, bass.ds(base, WN)],
                                      bank[4 + b][:, 0:WN], ALU.add)
                    dve.tensor_tensor(den[:, bass.ds(base, WN)], den[:, bass.ds(base, WN)],
                                      bank[4 + b][0:HEADS, P:P + WN], ALU.add).then_inc(acc_added, 1)

                interleaved(dve, NG, [(1, weights_0), (0, add_0)])
                dve.wait_ge(acc_added, NG)
            with dve.Else():
                dve.memset(lowest, LOWEST).then_inc(u_lowest, 1)

                def targets(u_step, col, ranks, ranks_sem, count):
                    u_step(dve.tensor_tensor(away[:, 0, 0:1], spare_row[:, 0:1], col[:, 0, 0:1], ALU.subtract))
                    u_step(dve.tensor_copy(home[:, 0, 0:1], col[:, 0, 0:1]))
                    wait_for(dve, ranks_sem, count)
                    u_step(dve.scalar_tensor_tensor(out=shift[:, 0, 0:1], in0=ranks, scalar=rank_cap[:, 0:1],
                                                    in1=away[:, 0, 0:1], op0=ALU.is_gt, op1=ALU.mult))
                    u_step(dve.tensor_tensor(sidx[:, 0, 0:1], shift[:, 0, 0:1], home[:, 0, 0:1], ALU.add))

                for turn in range(2):
                    def tile0(j):
                        n = turn * TILES + j
                        before = (STEPS0[0] * TILES if turn else 0) + STEPS0[turn] * j
                        taken = [0]

                        def u_step(ins):
                            taken[0] += 1
                            ins.then_inc(u_dve, 1)
                            wait_for(dve, u_dve, before + taken[0])

                        wait_for(dve, u_rows_got, 16 * (n + 1))
                        wait_for(dve, u_nodes_got[turn], 32 * (j + 1))
                        wait_for(dve, u_row_in, 16 * (n + 1))
                        u_step(dve.tensor_tensor(z[:, 0, 0, 0:HEADS], rows[:, 0, 0, D:ROW], ad_e[:, :], ALU.add))
                        u_step(dve.scalar_tensor_tensor(out=lg[:, 0, 0, 0:HEADS], in0=z[:, 0, 0, 0:HEADS],
                                                        scalar=SLOPE, in1=z[:, 0, 0, 0:HEADS],
                                                        op0=ALU.mult, op1=ALU.max))
                        u_step(dve.tensor_tensor(eq[:, 0, 0, :], srow[:, 0, 0:P],
                                                 dcol[:, 0, 0:1].to_broadcast([P, P]), ALU.is_equal))
                        targets(u_step, dcol, bank[3][:, 0:1], u_pe, 2 * n + 1)
                        if turn == 0:
                            u_step(dve.tensor_scalar(penalty[:, :], eq[:, 0, 0, :], -1.0, -LOWEST,
                                                     ALU.add, ALU.mult))
                            for h in range(HEADS):
                                u_step(dve.tensor_scalar(exc[:, 0, h * P:(h + 1) * P], ident[:, :],
                                                         lg[:, 0, 0, h:h + 1], None, ALU.mult))
                            wait_for(dve, u_pe, 2 * (n + 1))
                            u_step(dve.tensor_tensor(
                                ex[:, 0, :].rearrange("p (h e) -> p h e", h=HEADS),
                                bank[1][:, :].rearrange("p (h e) -> p h e", h=HEADS),
                                eq[:, 0, 0, :].unsqueeze(1).to_broadcast([P, HEADS, P]), ALU.mult))
                            u_step(dve.tensor_tensor(
                                ln[:, 0, :].rearrange("p (h e) -> p h e", h=HEADS),
                                ex[:, 0, :].rearrange("p (h e) -> p h e", h=HEADS),
                                penalty[:, :].unsqueeze(1).to_broadcast([P, HEADS, P]), ALU.add))
                            u_step(dve.tensor_reduce(tile_max[:, :],
                                                     ln[:, 0, :].rearrange("p (h e) -> p h e", h=HEADS),
                                                     AX.X, ALU.max))
                            u_step(dve.tensor_tensor(new_max[:, :], tile_max[:, :], max_e[:, :], ALU.max))
                        else:
                            u_step(dve.tensor_tensor(ls[:, 0, 0, :], lg[:, 0, 0, 0:HEADS], max_e[:, :],
                                                     ALU.subtract))
                            wait_for(dve, u_act, j + 1)
                            u_step(dve.tensor_tensor(
                                msg[:, 0, 0, 0:D].rearrange("p (h f) -> p h f", h=HEADS),
                                rows[:, 0, 0, 0:D].rearrange("p (h f) -> p h f", h=HEADS),
                                msg[:, 0, 0, D:ROW].unsqueeze(2).to_broadcast([P, HEADS, F]), ALU.mult))
                            wait_for(dve, u_pe, 2 * (n + 1))
                            u_step(dve.tensor_copy(msg[:, 0, 1, :], bank[2][:, 0:ROW]))

                    each(dve, TILES, tile0)

                def keep_sums(k):
                    wait_for(dve, u_sums_turned, k + 1)
                    dve.tensor_copy(acc_k[:, bass.ds(k, 1), :].rearrange("f o p -> f (o p)"), bank[0][:, 0:P])
                    dve.tensor_copy(den_k[:, bass.ds(k, 1), :].rearrange("h o p -> h (o p)"),
                                    bank[0][0:HEADS, P:2 * P]).then_inc(u_sums_kept, 1)

                each(dve, NB, keep_sums)
                dve.wait_ge(u_sums_kept, NB)

            dve.sem_inc(attended, 1)

            def moments(s, b, before, data, data_sem):
                wait_for(dve, data_sem, s + 1)
                for k in range(K):
                    ins = dve.bn_stats(stats[:, b, k, :], data[:, b, k, :])
                ins.then_inc(n_stats, 1)
                wait_apart(dve, n_stats, s + before + 1, passed)
                for k in range(K):
                    ins = dve.bn_aggr(mv[:, b, k, :], stats[:, b, k, :])
                ins.then_inc(n_mv, 1)

            def normalize(s, b, before, data, out_sem):
                wait_for(dve, n_rstd, 2 * (s + before + 1))
                n0 = 3 * (s + before)
                dve.scalar_tensor_tensor(out=newton[:, b, 0, :], in0=mv[:, b, :, 1], scalar=eps_c[:, 0:1],
                                         in1=rstd[:, b, :], op0=ALU.add, op1=ALU.mult).then_inc(n_newton, 1)
                wait_for(dve, n_newton, n0 + 1)
                dve.scalar_tensor_tensor(out=newton[:, b, 1, :], in0=newton[:, b, 0, :], scalar=-0.5,
                                         in1=rstd[:, b, :], op0=ALU.mult, op1=ALU.mult).then_inc(n_newton, 1)
                wait_for(dve, n_newton, n0 + 2)
                dve.scalar_tensor_tensor(out=newton[:, b, 2, :], in0=newton[:, b, 1, :], scalar=1.5,
                                         in1=rstd[:, b, :], op0=ALU.add, op1=ALU.mult).then_inc(n_newton, 1)
                wait_for(dve, n_newton, n0 + 3)
                for k in range(K):
                    ins = dve.tensor_scalar(y1[:, b, k, :], data[:, b, k, :], mv[:, b, k, 0:1],
                                            newton[:, b, 2, k:k + 1], ALU.subtract, ALU.mult)
                ins.then_inc(out_sem, 1)

            def mean_b(s, b, i):
                wait_for(dve, b_turned, s + 1)
                dve.tensor_scalar(clamped[:, b, :], bank[2 + b][:, 0:K * HEADS], 1e-37, None, ALU.max
                                  ).then_inc(b_clamped, 1)
                wait_for(dve, b_clamped, s + 1)
                dve.reciprocal(rec[:, b, :], clamped[:, b, :]).then_inc(b_rec, 1)
                wait_for(dve, b_rec, s + 1)
                dve.tensor_tensor(t1[:, b, :, :].rearrange("p k (h f) -> p (k h) f", h=HEADS),
                                  bank[b][:, :].rearrange("p (k h f) -> p (k h) f", k=K, h=HEADS),
                                  rec[:, b, :].unsqueeze(2).to_broadcast([P, K * HEADS, F]), ALU.mult
                                  ).then_inc(b_t1, 1)
                wait_for(dve, b_t1, s + 1)
                wait_for(dve, b_xbias, s + 1)
                dve.tensor_tensor(t2[:, b, :, :], t1[:, b, :, :], xbias[:, b, :, :], ALU.add).then_inc(b_t2, 1)
                moments(s, b, 0, t2, b_t2)

            def finish_b(s, b, i):
                wait_for(dve, b_x1b, s - 1)
                wait_for(dve, b_yturned, s - 1)
                normalize(s, b, 0, t2, b_y)

            def rest_b(s, b, i):
                wait_for(dve, b_hi, s + 1)
                wait_for(dve, b_lo, s - 1)
                dve.tensor_tensor(hr[:, b, :, :], bank[5][:, :].rearrange("p (k f) -> p k f", k=K),
                                  h3[:, b, :, 0, :], ALU.subtract).then_inc(b_hr, 1)

            dve.wait_ge(a_out[0], done(NS, 0))
            dve.wait_ge(a_out[1], done(NS, 1))
            interleaved(dve, NS, [(1, finish_b), (0, rest_b), (2, mean_b)])

            fast = dve.value_load(mode[0:1, 1:2], min_val=0, max_val=1)
            with dve.If(fast > 0):
                def equals_1(g, b, i):
                    wait_for(dve, group1_in[b], 64 * (i + 1))
                    wait_for(dve, presummed, 2 * (g - 1))
                    dve.tensor_tensor(eq[:, b, :, :], srow[:, b, :].rearrange("k (p t) -> k t p", t=T),
                                      scol[:, b, :].unsqueeze(2).to_broadcast([P, T, P]), ALU.is_equal
                                      ).then_inc(eq_made, 1)
                    wait_for(dve, group1_in[b], 64 * (i + 1))
                    wait_for(dve, hd_made, 2 * (g - 1))
                    dve.tensor_scalar(oneT[:, b, :, :].rearrange("n t p -> n p t"),
                                      drow[:, b, :].rearrange("n (p t) -> n p t", t=T),
                                      node_id[0:W3, bass.ds(g, 1)], None, ALU.is_equal).then_inc(oneT1_made, 1)
                    wait_for(dve, sidx_made, g - 1)
                    dve.tensor_tensor(home[:, b, :], scol[:, b, :], copy_row[:, :], ALU.add).then_inc(home_made, 1)
                    dve.tensor_tensor(away[:, b, :], spare_row[:, :], scol[:, b, :], ALU.subtract
                                      ).then_inc(away_made, 1)

                def clamp_1(g, b, i):
                    for q in range(2):
                        wait_for(dve, v_made, 2 * g + q + 1)
                        wait_for(dve, ex_made, 2 * g + q - 1)
                        dve.tensor_scalar(exc[:, q, :], bank[1 + q][:, :], bf1_c[:, 0:1], V_CAP, ALU.add,
                                          ALU.min).then_inc(exc_made, 1)

                def softplus_1(g, b, i):
                    for q in range(2):
                        wait_for(dve, ln_made, 2 * g + q + 1)
                        if q == 0:
                            wait_for(dve, wij_made, 2 * (g - 1))
                        dve.scalar_tensor_tensor(out=gact[:, b, q, :], in0=bank[1 + q][:, :],
                                                 scalar=bf1_c[:, 0:1], in1=ln[:, q, :], op0=ALU.add,
                                                 op1=ALU.max).then_inc(gact_made, 1)

                def messages_1(g, b, i):
                    for q in range(2):
                        wait_for(dve, hsb_made, 2 * g + q + 1)
                        wait_for(dve, wij_made, 2 * g + q + 1)
                        wait_for(dve, presummed, 2 * g + q - 1)
                        dve.tensor_tensor(xij[:, q, :], bank[4 + q][:, :],
                                          hsb[:, q, :, :].rearrange("p t f -> p (t f)"), ALU.mult
                                          ).then_inc(xij_made, 1)

                def targets_1(g, b, i):
                    wait_for(dve, ranked, g + 1)
                    wait_for(dve, away_made, g + 1)
                    dve.scalar_tensor_tensor(out=shift[:, b, :], in0=bank[0][:, 2 * P:2 * P + T],
                                             scalar=rank_cap[:, 0:1], in1=away[:, b, :], op0=ALU.is_gt,
                                             op1=ALU.mult).then_inc(shift_made, 1)
                    wait_for(dve, shift_made, g + 1)
                    wait_for(dve, earlier_added, g)
                    dve.tensor_tensor(sidx[:, b, :], shift[:, b, :], home[:, b, :], ALU.add).then_inc(sidx_made, 1)

                interleaved(dve, NG, [(1, clamp_1), (0, messages_1), (1, softplus_1), (0, targets_1),
                                      (2, equals_1)])
            with dve.Else():
                def tile1(j):
                    before = STEPS1 * j
                    taken = [0]

                    def w_step(ins):
                        taken[0] += 1
                        ins.then_inc(w_dve, 1)
                        wait_for(dve, w_dve, before + taken[0])

                    wait_for(dve, w_gathered, 16 * (j + 1))
                    w_step(dve.tensor_tensor(h_sum[:, 0, :], h_e[:, 0:D], h_e[:, D:2 * D], ALU.add))
                    w_step(dve.tensor_tensor(h_sum[:, 1, :], h_sum[:, 0, :], h_e[:, 2 * D:3 * D], ALU.add))
                    wait_for(dve, w_cols_in, 32 * (j + 1))
                    wait_for(dve, w_row_in, 16 * (j + 1))
                    w_step(dve.tensor_tensor(eq[:, 0, 0, :], srow[:, 0, 0:P],
                                             scol[:, 0, 0:1].to_broadcast([P, P]), ALU.is_equal))
                    w_step(dve.tensor_tensor(away[:, 0, 0:1], spare_row[:, 0:1], scol[:, 0, 0:1],
                                             ALU.subtract))
                    wait_for(dve, w_pe, 4 * j + 2)
                    w_step(dve.scalar_tensor_tensor(out=shift[:, 0, 0:1], in0=bank[3][:, 0:1],
                                                    scalar=rank_cap[:, 0:1], in1=away[:, 0, 0:1],
                                                    op0=ALU.is_gt, op1=ALU.mult))
                    w_step(dve.tensor_tensor(sidx[:, 0, 0:1], shift[:, 0, 0:1], scol[:, 0, 0:1], ALU.add))
                    w_step(dve.tensor_scalar(exc[:, 0, 0:P], bank[1][:, 0:P], bf1_c[:, 0:1], V_CAP,
                                             ALU.add, ALU.min))
                    wait_for(dve, w_act, 3 * (j + 1))
                    w_step(dve.scalar_tensor_tensor(out=gact[:, 0, 0, 0:P], in0=bank[1][:, 0:P],
                                                    scalar=bf1_c[:, 0:1], in1=ln[:, 0, 0:P],
                                                    op0=ALU.add, op1=ALU.max))
                    wait_for(dve, w_pe, 4 * j + 3)
                    wait_for(dve, w_edge_in, 32 * (j + 1))
                    w_step(dve.tensor_tensor(scaled[:, :], bank[2][:, 0:D], h_sum[:, 1, :], ALU.mult))
                    w_step(dve.tensor_scalar(xij[:, 0, 0:D], scaled[:, :], ccol[:, 0, 0:1], None, ALU.mult))
                    wait_for(dve, w_pe, 4 * (j + 1))
                    w_step(dve.tensor_copy(xo[:, 0, 0, :], bank[4][:, 0:D]))

                each(dve, TILES, tile1)

            def total_c(s, b, i):
                wait_for(dve, c_pairs, s + 1)
                wait_for(dve, c_turned, s - 1)
                dve.tensor_tensor(ag[:, b, :, :], pair[:, b, 0, :, :], pair[:, b, 1, :, :], ALU.add
                                  ).then_inc(c_ag, 1)

            def clamp_c(s, b, i):
                wait_for(dve, c_o, s + 1)
                wait_for(dve, c_ex, s - 1)
                dve.tensor_scalar(exc[:, b, :], bank[2 + b][:, :], bo1_c[:, 0:1], V_CAP, ALU.add,
                                  ALU.min).then_inc(c_exc, 1)

            def softplus_c(s, b, i):
                wait_for(dve, c_ln, s + 1)
                wait_for(dve, c_y, s - 1)
                dve.scalar_tensor_tensor(out=gact[:, b, 0, :], in0=bank[2 + b][:, :],
                                         scalar=bo1_c[:, 0:1], in1=ln[:, b, :], op0=ALU.add,
                                         op1=ALU.max).then_inc(c_g, 1)

            def residual_c(s, b, i):
                wait_for(dve, c_y, s + 1)
                wait_for(dve, c_x_in[b], 16 * (i + 1))
                dve.tensor_tensor(t2[:, b, :, :], bank[4 + b][:, :].rearrange("p (k f) -> p k f", k=K),
                                  xb[:, b, :, :], ALU.add).then_inc(c_t2, 1)
                moments(s, b, NS, t2, c_t2)

            def finish_c(s, b, i):
                wait_for(dve, c_out[b], 16 * i)
                normalize(s, b, NS, t2, c_fin)

            interleaved(dve, NS, [(1, softplus_c), (2, clamp_c), (3, total_c), (1, residual_c), (0, finish_c)])


def kernel(**inputs):
    import numpy as np
    import concourse.bacc as bacc
    from concourse.bass_utils import run_bass_kernel_spmd

    def padded(a, rows, fill=0):
        a = np.asarray(a)
        return np.concatenate([a, np.full((rows - a.shape[0],) + a.shape[1:], fill, a.dtype)])

    arrays = {
        "x": padded(inputs["x"], NT),
        "src": padded(inputs["src"], EP, N),
        "dst": padded(inputs["dst"], EP, N),
        "f_ij": padded(np.asarray(inputs["edge_attr3_1x20"]).reshape(E, RBF), EP),
        "cut": padded(np.asarray(inputs["edge_weight1"]).reshape(E), EP),
        "W": inputs["L0_gnn_W"], "att": inputs["L0_gnn_att"], "bias0": inputs["L0_gnn_bias"],
        "W_in": inputs["L1_gnn_W_in"], "W_f1": inputs["L1_gnn_W_f1"], "b_f1": inputs["L1_gnn_b_f1"],
        "W_f2": inputs["L1_gnn_W_f2"], "b_f2": inputs["L1_gnn_b_f2"],
        "W_o1": inputs["L1_gnn_W_o1"], "b_o1": inputs["L1_gnn_b_o1"],
        "W_o2": inputs["L1_gnn_W_o2"], "b_o2": inputs["L1_gnn_b_o2"],
    }
    arrays = {f"in_{k}": np.ascontiguousarray(v) for k, v in arrays.items()}
    nc = bacc.Bacc("TRN2", target_bir_lowering=False, num_devices=1)
    args = [nc.dram_tensor(k, a.shape, mybir.dt.from_np(a.dtype), kind="ExternalInput").ap()
            for k, a in arrays.items()]
    out = nc.dram_tensor("out", (NT, D), F32, kind="ExternalOutput").ap()
    gnn_kernel(nc, *args, out)
    r = run_bass_kernel_spmd(nc, [arrays], core_ids=[0])
    return r.results[0]["out"][:N]
```
